# Optimizing a Trainium2 kernel written in Bass

```python
import numpy as np
import jax
import jax.numpy as jnp

def _softmax(x, axis=-1):
    return jax.nn.softmax(x, axis=axis)

def _gelu(x):
    return jax.nn.gelu(x, approximate=True)

def _silu(x):
    return jax.nn.silu(x)

def _sigmoid(x):
    return jax.nn.sigmoid(x)

def _layernorm(x, axis=-1, eps=1e-05):
    m = jnp.mean(x, axis=axis, keepdims=True)
    v = jnp.var(x, axis=axis, keepdims=True)
    return (x - m) / jnp.sqrt(v + eps)

def _scatter_add(tgt, idx, src, axis=0):
    return tgt.at[idx].add(src)

def _segment_sum(src, seg, n):
    return jax.ops.segment_sum(src, seg, n)
kernel_name = 'mk_decoder_preln_d4_seqx_r8_82c281'

def setup_inputs(seed: int=0):
    np.random.seed(seed)
    _w = jnp.asarray

    def _rec_inputs():
        import jax
        import jax.numpy as jnp
        _rk = jax.random.key(seed)
        x = 7.22e-05 + 1 * jax.random.normal(jax.random.fold_in(_rk, 1), (16, 128, 128), jnp.float32)
        _lenS = 128 - jax.random.randint(jax.random.fold_in(_rk, 7), (16,), 0, max(1, 128 // 4) + 1, jnp.int32)
        _lenS2 = 77 - jax.random.randint(jax.random.fold_in(_rk, 8), (16,), 0, max(1, 77 // 4) + 1, jnp.int32)
        _ctx_1024P = jax.random.normal(jax.random.fold_in(_rk, 11), (16, 16, 128), jnp.float32)
        _ctx_1024c = jax.random.dirichlet(jax.random.fold_in(_rk, 511), 0.3 * jnp.ones((16,), jnp.float32), (16, 77))
        _ctx_1024t = jnp.einsum('bsk,bkd->bsd', _ctx_1024c, _ctx_1024P)
        _ctx_1024t = _ctx_1024t * jax.lax.rsqrt(jnp.mean(jnp.square(_ctx_1024t)) + 1e-12) * 0.953939
        ctx_1024 = 4.13588e-05 + 0.999923 * (_ctx_1024t + 0.3 * jax.random.normal(jax.random.fold_in(_rk, 611), (16, 77, 128), jnp.float32))
        itok_BxS2_0_2047 = jax.random.randint(jax.random.fold_in(_rk, 14), (16, 77), 0, 256, jnp.int32)
        _validS = jnp.arange(128)[None, :] < _lenS[:, None]
        _validS2 = jnp.arange(77)[None, :] < _lenS2[:, None]
        _causal = jnp.tril(jnp.ones((128, 128), dtype=bool))
        mask_SxS2_ff0 = jnp.where(jnp.ones((128, 77), dtype=bool), 0.0, -1000000000.0).astype(jnp.float32)
        mask_BxS2_bf0 = jnp.logical_not(jnp.ones((16, 77), dtype=bool))
        return (x, ctx_1024, itok_BxS2_0_2047, mask_SxS2_ff0, mask_BxS2_bf0)
    x, ctx_1024, itok_BxS2_0_2047, mask_SxS2_ff0, mask_BxS2_bf0 = _rec_inputs()

    def _L0_attn_setup():
        import jax, jax.numpy as jnp
        import numpy as np
        H = 16
        W = 32
        D_MODEL = 128
        D_FF = 512
        EPS = 1e-05

        def _layernorm(x, g, b):
            mu = jnp.mean(x, axis=-1, keepdims=True)
            var = jnp.mean(jnp.square(x - mu), axis=-1, keepdims=True)
            return (x - mu) * jax.lax.rsqrt(var + EPS) * g + b

        def _sliding_attn(q, k, v, w):
            B, Hh, S, d = q.shape
            nc = S // w
            qc = q.reshape(B, Hh, nc, w, d)
            kp = jnp.pad(k, ((0, 0), (0, 0), (w, w), (0, 0)))
            vp = jnp.pad(v, ((0, 0), (0, 0), (w, w), (0, 0)))
            idx = (jnp.arange(nc) * w)[:, None] + jnp.arange(3 * w)[None, :]
            kc = kp[:, :, idx, :]
            vc = vp[:, :, idx, :]
            scores = jnp.einsum('bhcqd,bhckd->bhcqk', qc, kc)
            q_pos = jnp.arange(nc)[:, None, None] * w + jnp.arange(w)[None, :, None]
            k_pos = jnp.arange(nc)[:, None, None] * w - w + jnp.arange(3 * w)[None, None, :]
            rel = k_pos - q_pos
            valid = (jnp.abs(rel) <= w) & (k_pos >= 0) & (k_pos < S)
            scores = jnp.where(valid[None, None], scores, jnp.float32(-1000000000.0))
            p = jax.nn.softmax(scores, axis=-1)
            out = jnp.einsum('bhcqk,bhckd->bhcqd', p, vc)
            return out.reshape(B, Hh, S, d)
        key = jax.random.key(seed)
        ks = jax.random.split(key, 8)
        B, S = (2, 512)
        src = jax.random.normal(ks[0], (B, S, D_MODEL), dtype=jnp.float32)
        ln1_g = jnp.ones((D_MODEL,), jnp.float32)
        ln1_b = jnp.zeros((D_MODEL,), jnp.float32)
        ln2_g = jnp.ones((D_MODEL,), jnp.float32)
        ln2_b = jnp.zeros((D_MODEL,), jnp.float32)
        W1 = jax.random.normal(ks[1], (D_MODEL, D_FF), jnp.float32) * 0.02
        b1 = jnp.zeros((D_FF,), jnp.float32)
        W2 = jax.random.normal(ks[2], (D_FF, D_MODEL), jnp.float32) * 0.02
        b2 = jnp.zeros((D_MODEL,), jnp.float32)
        return {'src': src, 'ln1_g': ln1_g, 'ln1_b': ln1_b, 'ln2_g': ln2_g, 'ln2_b': ln2_b, 'W1': W1, 'b1': b1, 'W2': W2, 'b2': b2}
    _L0_attn_all = _L0_attn_setup()
    _L0_attn_in = {k: v for k, v in _L0_attn_all.items() if k in ('ln1_g', 'ln1_b', 'ln2_g', 'ln2_b', 'W1', 'b1', 'W2', 'b2')}
    del _L0_attn_all

    def _L0_xattn_setup():
        import jax, jax.numpy as jnp
        import numpy as np
        EMBED_DIM = 128
        NUM_HEADS = 16
        HEAD_DIM = EMBED_DIM // NUM_HEADS
        SCALE = HEAD_DIM ** (-0.5)
        key = jax.random.key(seed)
        ks = jax.random.split(key, 12)
        B, T, S, C = (4, 256, 256, EMBED_DIM)
        inp = {'query': jax.random.normal(ks[0], (B, T, C), dtype=jnp.float32), 'key': jax.random.normal(ks[1], (B, S, C), dtype=jnp.float32), 'value': jax.random.normal(ks[2], (B, S, C), dtype=jnp.float32), 'attn_mask': jnp.zeros((T, S), dtype=jnp.float32), 'key_padding_mask': jnp.zeros((B, S), dtype=bool)}
        std = C ** (-0.5)
        for i, name in enumerate(['q', 'k', 'v', 'out']):
            inp[f'W{name}'] = jax.random.normal(ks[3 + i], (C, C), dtype=jnp.float32) * std
            inp[f'b{name}'] = jnp.zeros((C,), dtype=jnp.float32)
        return inp
    _L0_xattn_all = _L0_xattn_setup()
    _L0_xattn_in = {k: v for k, v in _L0_xattn_all.items() if k in ('Wq', 'bq', 'Wk', 'bk', 'Wv', 'bv', 'Wout', 'bout')}
    del _L0_xattn_all

    def _L0_ffn_setup():
        import jax, jax.numpy as jnp
        import numpy as np
        DIM = 128
        HIDDEN = 512
        E = 8
        B, S = (2, 512)
        key = jax.random.key(seed)
        ks = jax.random.split(key, 8)
        sd = 1.0 / np.sqrt(DIM)
        sh = 1.0 / np.sqrt(HIDDEN)
        return {'x': jax.random.normal(ks[0], (B, S, DIM), dtype=jnp.float32), 'router_w': jax.random.uniform(ks[1], (DIM, E), jnp.float32, -sd, sd), 'router_b': jax.random.uniform(ks[2], (E,), jnp.float32, -sd, sd), 'w1': jax.random.uniform(ks[3], (E, DIM, 2 * HIDDEN), jnp.float32, -sd, sd), 'b1': jax.random.uniform(ks[4], (E, 2 * HIDDEN), jnp.float32, -sd, sd), 'w2': jax.random.uniform(ks[5], (E, HIDDEN, DIM), jnp.float32, -sh, sh), 'b2': jax.random.uniform(ks[6], (E, DIM), jnp.float32, -sh, sh)}
    _L0_ffn_all = _L0_ffn_setup()
    _L0_ffn_in = {k: v for k, v in _L0_ffn_all.items() if k in ('router_w', 'router_b', 'w1', 'b1', 'w2', 'b2')}
    del _L0_ffn_all

    def _L1_attn_setup():
        import jax, jax.numpy as jnp
        import numpy as np
        H = 16
        GRID = 16
        TOK_PER_FRAME = GRID * GRID

        def _rope(x, pos, dim):
            half = dim // 2
            omega = jnp.arange(half, dtype=x.dtype) / (dim / 2.0)
            inv = 1.0 / 10000.0 ** omega
            freq = pos.astype(x.dtype)[:, None] * inv
            sin = jnp.concatenate([jnp.sin(freq), jnp.sin(freq)], axis=-1)
            cos = jnp.concatenate([jnp.cos(freq), jnp.cos(freq)], axis=-1)
            y = x.reshape(*x.shape[:-1], half, 2)
            y1, y2 = (y[..., 0], y[..., 1])
            rot = jnp.stack((-y2, y1), axis=-1).reshape(x.shape)
            return x * cos + rot * sin

        def _apply_3d_rope(qk, f_ids, h_ids, w_ids, d_dim):
            s = 0
            parts = []
            for pos in (f_ids, h_ids, w_ids):
                parts.append(_rope(qk[..., s:s + d_dim], pos, d_dim))
                s += d_dim
            if s < qk.shape[-1]:
                parts.append(qk[..., s:])
            return jnp.concatenate(parts, axis=-1)
        key = jax.random.key(seed)
        ks = jax.random.split(key, 5)
        D = 128
        B, N = (4, 256)
        sc = 0.02
        return {'hidden_states': jax.random.normal(ks[0], (B, N, D), jnp.float32), 'Wq': jax.random.normal(ks[1], (D, D), jnp.float32) * sc, 'bq': jnp.zeros((D,), jnp.float32), 'Wk': jax.random.normal(ks[2], (D, D), jnp.float32) * sc, 'bk': jnp.zeros((D,), jnp.float32), 'Wv': jax.random.normal(ks[3], (D, D), jnp.float32) * sc, 'bv': jnp.zeros((D,), jnp.float32), 'Wo': jax.random.normal(ks[4], (D, D), jnp.float32) * sc, 'bo': jnp.zeros((D,), jnp.float32)}
    _L1_attn_all = _L1_attn_setup()
    _L1_attn_in = {k: v for k, v in _L1_attn_all.items() if k in ('Wq', 'bq', 'Wk', 'bk', 'Wv', 'bv', 'Wo', 'bo')}
    del _L1_attn_all

    def _L1_xattn_setup():
        import jax, jax.numpy as jnp
        import numpy as np
        DIM = 128
        HEADS = 16
        HEAD_DIM = DIM // HEADS
        SCALE = HEAD_DIM ** (-0.5)
        key = jax.random.key(seed)
        ks = jax.random.split(key, 13)
        B, Nq, Nk = (4, 256, 256)
        s = DIM ** (-0.5)
        return {'query': jax.random.normal(ks[0], (B, Nq, DIM), jnp.float32), 'key': jax.random.normal(ks[1], (B, Nk, DIM), jnp.float32), 'value': jax.random.normal(ks[2], (B, Nk, DIM), jnp.float32), 'qpos': jax.random.randint(ks[3], (B, Nq), 0, Nq), 'kpos': jax.random.randint(ks[4], (B, Nk), 0, Nk), 'Wq': jax.random.normal(ks[5], (DIM, DIM), jnp.float32) * s, 'bq': jnp.zeros((DIM,), jnp.float32), 'Wk': jax.random.normal(ks[6], (DIM, DIM), jnp.float32) * s, 'bk': jnp.zeros((DIM,), jnp.float32), 'Wv': jax.random.normal(ks[7], (DIM, DIM), jnp.float32) * s, 'bv': jnp.zeros((DIM,), jnp.float32), 'Wo': jax.random.normal(ks[8], (DIM, DIM), jnp.float32) * s, 'bo': jnp.zeros((DIM,), jnp.float32)}
    _L1_xattn_all = _L1_xattn_setup()
    _L1_xattn_in = {k: v for k, v in _L1_xattn_all.items() if k in ('Wq', 'bq', 'Wk', 'bk', 'Wv', 'bv', 'Wo', 'bo')}
    del _L1_xattn_all

    def _L1_ffn_setup():
        import jax, jax.numpy as jnp
        import numpy as np
        GROUP = 16
        EPS = 1e-05

        def _dequant(q, scale):
            w = q.astype(jnp.float32) / 7.5 - 1.0
            return w * jnp.repeat(scale, GROUP, axis=1)

        def _qlora_linear(x, q, scale, bias, la, lb):
            w = _dequant(q, scale)
            base = jnp.einsum('btd,od->bto', x, w) + bias
            lora = jnp.einsum('btr,or->bto', jnp.einsum('btd,rd->btr', x, la), lb)
            return base + lora

        def _layernorm(x, g, b):
            mu = jnp.mean(x, axis=-1, keepdims=True)
            var = jnp.mean(jnp.square(x - mu), axis=-1, keepdims=True)
            return (x - mu) * jax.lax.rsqrt(var + EPS) * g + b
        key = jax.random.key(seed)
        ks = jax.random.split(key, 6)
        D, R, B, T = (128, 32, 8, 512)
        x = jax.random.normal(ks[0], (B, T, D), dtype=jnp.float32)
        qweights = jax.random.randint(ks[1], (6, D, D), 0, 16, dtype=jnp.int32)
        scales = jax.random.uniform(ks[2], (6, D, D // GROUP), dtype=jnp.float32)
        biases = jax.random.normal(ks[3], (6, D), dtype=jnp.float32) * 0.02
        lora_a = jax.random.normal(ks[4], (6, R, D), dtype=jnp.float32) * 0.02
        lora_b = jax.random.normal(ks[5], (6, D, R), dtype=jnp.float32) * 0.02
        ln_gamma = jnp.ones((3, D), dtype=jnp.float32)
        ln_beta = jnp.zeros((3, D), dtype=jnp.float32)
        return {'x': x, 'qweights': qweights, 'scales': scales, 'biases': biases, 'lora_a': lora_a, 'lora_b': lora_b, 'ln_gamma': ln_gamma, 'ln_beta': ln_beta}
    _L1_ffn_all = _L1_ffn_setup()
    _L1_ffn_in = {k: v for k, v in _L1_ffn_all.items() if k in ('qweights', 'scales', 'biases', 'lora_a', 'lora_b', 'ln_gamma', 'ln_beta')}
    del _L1_ffn_all

    def _L2_attn_setup():
        import jax, jax.numpy as jnp
        import numpy as np
        import math
        D_MODEL = 128
        N_HEADS = 16
        HEAD_DIM = D_MODEL // N_HEADS
        FACTOR = 5
        B, L = (4, 512)
        key = jax.random.key(seed)
        ks = jax.random.split(key, 10)
        s = 1.0 / math.sqrt(D_MODEL)
        U = min(FACTOR * int(math.ceil(math.log(L))), L)
        return {'x': jax.random.normal(ks[0], (B, L, D_MODEL), dtype=jnp.float32), 'Wq': jax.random.normal(ks[1], (D_MODEL, D_MODEL), dtype=jnp.float32) * s, 'bq': jnp.zeros((D_MODEL,), jnp.float32), 'Wk': jax.random.normal(ks[2], (D_MODEL, D_MODEL), dtype=jnp.float32) * s, 'bk': jnp.zeros((D_MODEL,), jnp.float32), 'Wv': jax.random.normal(ks[3], (D_MODEL, D_MODEL), dtype=jnp.float32) * s, 'bv': jnp.zeros((D_MODEL,), jnp.float32), 'Wo': jax.random.normal(ks[4], (D_MODEL, D_MODEL), dtype=jnp.float32) * s, 'bo': jnp.zeros((D_MODEL,), jnp.float32), 'sample_idx': jax.random.permutation(ks[5], L)[:U].astype(jnp.int32)}
    _L2_attn_all = _L2_attn_setup()
    _L2_attn_in = {k: v for k, v in _L2_attn_all.items() if k in ('Wq', 'bq', 'Wk', 'bk', 'Wv', 'bv', 'Wo', 'bo', 'sample_idx')}
    del _L2_attn_all

    def _L2_xattn_setup():
        import jax, jax.numpy as jnp
        import numpy as np
        DIM = 128
        NUM_HEADS = 16
        DIM_HEAD = 64
        INNER = NUM_HEADS * DIM_HEAD
        SCALE = DIM_HEAD ** (-0.5)

        def _layernorm(x, gamma, beta, eps=1e-05):
            mu = jnp.mean(x, axis=-1, keepdims=True)
            var = jnp.mean(jnp.square(x - mu), axis=-1, keepdims=True)
            return (x - mu) * jax.lax.rsqrt(var + eps) * gamma + beta
        key = jax.random.key(seed)
        ks = jax.random.split(key, 8)
        B, SQ, SK = (2, 256, 512)
        x = jax.random.normal(ks[0], (B, SQ, DIM), dtype=jnp.float32)
        context = jax.random.normal(ks[1], (B, SK, DIM), dtype=jnp.float32)
        ln_gamma = jnp.ones((DIM,), jnp.float32)
        ln_beta = jnp.zeros((DIM,), jnp.float32)
        w_q = jax.random.normal(ks[2], (DIM, INNER), dtype=jnp.float32) / np.sqrt(DIM)
        w_kv = jax.random.normal(ks[3], (DIM, 2 * INNER), dtype=jnp.float32) / np.sqrt(DIM)
        w_out = jax.random.normal(ks[4], (INNER, DIM), dtype=jnp.float32) / np.sqrt(INNER)
        b_out = jnp.zeros((DIM,), jnp.float32)
        gate = jnp.array([0.5], jnp.float32)
        return {'x': x, 'context': context, 'ln_gamma': ln_gamma, 'ln_beta': ln_beta, 'w_q': w_q, 'w_kv': w_kv, 'w_out': w_out, 'b_out': b_out, 'gate': gate}
    _L2_xattn_all = _L2_xattn_setup()
    _L2_xattn_in = {k: v for k, v in _L2_xattn_all.items() if k in ('ln_gamma', 'ln_beta', 'w_q', 'w_kv', 'w_out', 'b_out', 'gate')}
    del _L2_xattn_all

    def _L2_ffn_setup():
        import jax, jax.numpy as jnp
        import numpy as np
        D_MODEL, D_FF, RANK = (128, 512, 32)
        B, S = (4, 512)
        key = jax.random.key(seed)
        ks = jax.random.split(key, 7)
        return {'x': jax.random.normal(ks[0], (B, S, D_MODEL), dtype=jnp.float32), 'U1': jax.random.normal(ks[1], (D_MODEL, RANK), dtype=jnp.float32) * 0.02, 'V1': jax.random.normal(ks[2], (RANK, D_FF), dtype=jnp.float32) * 0.02, 'b1': jnp.zeros((D_FF,), dtype=jnp.float32), 'U2': jax.random.normal(ks[3], (D_FF, RANK), dtype=jnp.float32) * 0.02, 'V2': jax.random.normal(ks[4], (RANK, D_MODEL), dtype=jnp.float32) * 0.02, 'b2': jnp.zeros((D_MODEL,), dtype=jnp.float32)}
    _L2_ffn_all = _L2_ffn_setup()
    _L2_ffn_in = {k: v for k, v in _L2_ffn_all.items() if k in ('U1', 'V1', 'b1', 'U2', 'V2', 'b2')}
    del _L2_ffn_all

    def _L3_attn_setup():
        import jax, jax.numpy as jnp
        import numpy as np
        B, S, D, H = (4, 1024, 128, 16)
        HD = D // H

        def elu_feature_map(x):
            return jax.nn.elu(x) + 1.0
        key = jax.random.key(seed)
        k1, k2, k3 = jax.random.split(key, 3)
        x = jax.random.normal(k1, (B, S, D), dtype=jnp.float32)
        w_qkv = jax.random.normal(k2, (3 * D, D), dtype=jnp.float32) * D ** (-0.5)
        w_out = jax.random.normal(k3, (D, D), dtype=jnp.float32) * D ** (-0.5)
        return {'x': x, 'w_qkv': w_qkv, 'w_out': w_out}
    _L3_attn_all = _L3_attn_setup()
    _L3_attn_in = {k: v for k, v in _L3_attn_all.items() if k in ('w_qkv', 'w_out')}
    del _L3_attn_all

    def _L3_xattn_setup():
        import jax, jax.numpy as jnp
        import numpy as np
        D_MODEL = 128
        B, S = (4, 256)
        key = jax.random.key(seed)
        ks = jax.random.split(key, 10)
        s = 1.0 / np.sqrt(D_MODEL)
        return {'k': jax.random.normal(ks[0], (B, S, D_MODEL), jnp.float32), 'v': jax.random.normal(ks[1], (B, S, D_MODEL), jnp.float32), 'q': jax.random.normal(ks[2], (B, S, D_MODEL), jnp.float32), 'Wk': jax.random.normal(ks[3], (D_MODEL, D_MODEL), jnp.float32) * s, 'Wv': jax.random.normal(ks[4], (D_MODEL, D_MODEL), jnp.float32) * s, 'bv': jnp.zeros((D_MODEL,), jnp.float32), 'Wq': jax.random.normal(ks[5], (D_MODEL, D_MODEL), jnp.float32) * s, 'bq': jnp.zeros((D_MODEL,), jnp.float32), 'Wo': jax.random.normal(ks[6], (D_MODEL, D_MODEL), jnp.float32) * s, 'bo': jnp.zeros((D_MODEL,), jnp.float32)}
    _L3_xattn_all = _L3_xattn_setup()
    _L3_xattn_in = {k: v for k, v in _L3_xattn_all.items() if k in ('Wk', 'Wv', 'bv', 'Wq', 'bq', 'Wo', 'bo')}
    del _L3_xattn_all

    def _L3_ffn_setup():
        import jax, jax.numpy as jnp
        import numpy as np
        TOP_K = 2
        key = jax.random.key(seed)
        k0, k1, k2, k3, k4 = jax.random.split(key, 5)
        B, S, H, I, E = (1, 512, 128, 256, 8)
        hidden_states = jax.random.normal(k0, (B, S, H), dtype=jnp.float32)
        wg = jax.random.normal(k1, (E, H), dtype=jnp.float32) * 0.02
        w1 = jax.random.normal(k2, (E, I, H), dtype=jnp.float32) * 0.02
        w3 = jax.random.normal(k3, (E, I, H), dtype=jnp.float32) * 0.02
        w2 = jax.random.normal(k4, (E, H, I), dtype=jnp.float32) * 0.02
        return {'hidden_states': hidden_states, 'wg': wg, 'w1': w1, 'w3': w3, 'w2': w2}
    _L3_ffn_all = _L3_ffn_setup()
    _L3_ffn_in = {k: v for k, v in _L3_ffn_all.items() if k in ('wg', 'w1', 'w3', 'w2')}
    del _L3_ffn_all
    return {'x': x, 'ctx_1024': ctx_1024, 'itok_BxS2_0_2047': itok_BxS2_0_2047, 'mask_SxS2_ff0': mask_SxS2_ff0, 'mask_BxS2_bf0': mask_BxS2_bf0, 'L0_attn_ln1_g': _L0_attn_in['ln1_g'], 'L0_attn_ln1_b': _L0_attn_in['ln1_b'], 'L0_attn_ln2_g': _L0_attn_in['ln2_g'], 'L0_attn_ln2_b': _L0_attn_in['ln2_b'], 'L0_attn_W1': _L0_attn_in['W1'], 'L0_attn_b1': _L0_attn_in['b1'], 'L0_attn_W2': _L0_attn_in['W2'], 'L0_attn_b2': _L0_attn_in['b2'], 'L0_xattn_Wq': _L0_xattn_in['Wq'], 'L0_xattn_bq': _L0_xattn_in['bq'], 'L0_xattn_Wk': _L0_xattn_in['Wk'], 'L0_xattn_bk': _L0_xattn_in['bk'], 'L0_xattn_Wv': _L0_xattn_in['Wv'], 'L0_xattn_bv': _L0_xattn_in['bv'], 'L0_xattn_Wout': _L0_xattn_in['Wout'], 'L0_xattn_bout': _L0_xattn_in['bout'], 'L0_ffn_router_w': _L0_ffn_in['router_w'], 'L0_ffn_router_b': _L0_ffn_in['router_b'], 'L0_ffn_w1': _L0_ffn_in['w1'], 'L0_ffn_b1': _L0_ffn_in['b1'], 'L0_ffn_w2': _L0_ffn_in['w2'], 'L0_ffn_b2': _L0_ffn_in['b2'], 'L1_attn_Wq': _L1_attn_in['Wq'], 'L1_attn_bq': _L1_attn_in['bq'], 'L1_attn_Wk': _L1_attn_in['Wk'], 'L1_attn_bk': _L1_attn_in['bk'], 'L1_attn_Wv': _L1_attn_in['Wv'], 'L1_attn_bv': _L1_attn_in['bv'], 'L1_attn_Wo': _L1_attn_in['Wo'], 'L1_attn_bo': _L1_attn_in['bo'], 'L1_xattn_Wq': _L1_xattn_in['Wq'], 'L1_xattn_bq': _L1_xattn_in['bq'], 'L1_xattn_Wk': _L1_xattn_in['Wk'], 'L1_xattn_bk': _L1_xattn_in['bk'], 'L1_xattn_Wv': _L1_xattn_in['Wv'], 'L1_xattn_bv': _L1_xattn_in['bv'], 'L1_xattn_Wo': _L1_xattn_in['Wo'], 'L1_xattn_bo': _L1_xattn_in['bo'], 'L1_ffn_qweights': _L1_ffn_in['qweights'], 'L1_ffn_scales': _L1_ffn_in['scales'], 'L1_ffn_biases': _L1_ffn_in['biases'], 'L1_ffn_lora_a': _L1_ffn_in['lora_a'], 'L1_ffn_lora_b': _L1_ffn_in['lora_b'], 'L1_ffn_ln_gamma': _L1_ffn_in['ln_gamma'], 'L1_ffn_ln_beta': _L1_ffn_in['ln_beta'], 'L2_attn_Wq': _L2_attn_in['Wq'], 'L2_attn_bq': _L2_attn_in['bq'], 'L2_attn_Wk': _L2_attn_in['Wk'], 'L2_attn_bk': _L2_attn_in['bk'], 'L2_attn_Wv': _L2_attn_in['Wv'], 'L2_attn_bv': _L2_attn_in['bv'], 'L2_attn_Wo': _L2_attn_in['Wo'], 'L2_attn_bo': _L2_attn_in['bo'], 'L2_attn_sample_idx': _L2_attn_in['sample_idx'], 'L2_xattn_ln_gamma': _L2_xattn_in['ln_gamma'], 'L2_xattn_ln_beta': _L2_xattn_in['ln_beta'], 'L2_xattn_w_q': _L2_xattn_in['w_q'], 'L2_xattn_w_kv': _L2_xattn_in['w_kv'], 'L2_xattn_w_out': _L2_xattn_in['w_out'], 'L2_xattn_b_out': _L2_xattn_in['b_out'], 'L2_xattn_gate': _L2_xattn_in['gate'], 'L2_ffn_U1': _L2_ffn_in['U1'], 'L2_ffn_V1': _L2_ffn_in['V1'], 'L2_ffn_b1': _L2_ffn_in['b1'], 'L2_ffn_U2': _L2_ffn_in['U2'], 'L2_ffn_V2': _L2_ffn_in['V2'], 'L2_ffn_b2': _L2_ffn_in['b2'], 'L3_attn_w_qkv': _L3_attn_in['w_qkv'], 'L3_attn_w_out': _L3_attn_in['w_out'], 'L3_xattn_Wk': _L3_xattn_in['Wk'], 'L3_xattn_Wv': _L3_xattn_in['Wv'], 'L3_xattn_bv': _L3_xattn_in['bv'], 'L3_xattn_Wq': _L3_xattn_in['Wq'], 'L3_xattn_bq': _L3_xattn_in['bq'], 'L3_xattn_Wo': _L3_xattn_in['Wo'], 'L3_xattn_bo': _L3_xattn_in['bo'], 'L3_ffn_wg': _L3_ffn_in['wg'], 'L3_ffn_w1': _L3_ffn_in['w1'], 'L3_ffn_w3': _L3_ffn_in['w3'], 'L3_ffn_w2': _L3_ffn_in['w2']}

def reference(x, ctx_1024, itok_BxS2_0_2047, mask_SxS2_ff0, mask_BxS2_bf0, L0_attn_ln1_g, L0_attn_ln1_b, L0_attn_ln2_g, L0_attn_ln2_b, L0_attn_W1, L0_attn_b1, L0_attn_W2, L0_attn_b2, L0_xattn_Wq, L0_xattn_bq, L0_xattn_Wk, L0_xattn_bk, L0_xattn_Wv, L0_xattn_bv, L0_xattn_Wout, L0_xattn_bout, L0_ffn_router_w, L0_ffn_router_b, L0_ffn_w1, L0_ffn_b1, L0_ffn_w2, L0_ffn_b2, L1_attn_Wq, L1_attn_bq, L1_attn_Wk, L1_attn_bk, L1_attn_Wv, L1_attn_bv, L1_attn_Wo, L1_attn_bo, L1_xattn_Wq, L1_xattn_bq, L1_xattn_Wk, L1_xattn_bk, L1_xattn_Wv, L1_xattn_bv, L1_xattn_Wo, L1_xattn_bo, L1_ffn_qweights, L1_ffn_scales, L1_ffn_biases, L1_ffn_lora_a, L1_ffn_lora_b, L1_ffn_ln_gamma, L1_ffn_ln_beta, L2_attn_Wq, L2_attn_bq, L2_attn_Wk, L2_attn_bk, L2_attn_Wv, L2_attn_bv, L2_attn_Wo, L2_attn_bo, L2_attn_sample_idx, L2_xattn_ln_gamma, L2_xattn_ln_beta, L2_xattn_w_q, L2_xattn_w_kv, L2_xattn_w_out, L2_xattn_b_out, L2_xattn_gate, L2_ffn_U1, L2_ffn_V1, L2_ffn_b1, L2_ffn_U2, L2_ffn_V2, L2_ffn_b2, L3_attn_w_qkv, L3_attn_w_out, L3_xattn_Wk, L3_xattn_Wv, L3_xattn_bv, L3_xattn_Wq, L3_xattn_bq, L3_xattn_Wo, L3_xattn_bo, L3_ffn_wg, L3_ffn_w1, L3_ffn_w3, L3_ffn_w2):
    import jax
    import jax.numpy as jnp

    def _L0_attn_ref(src, ln1_g, ln1_b, ln2_g, ln2_b, W1, b1, W2, b2):
        import jax, jax.numpy as jnp
        import numpy as np
        H = 16
        W = 32
        D_MODEL = 128
        D_FF = 512
        EPS = 1e-05

        def _layernorm(x, g, b):
            mu = jnp.mean(x, axis=-1, keepdims=True)
            var = jnp.mean(jnp.square(x - mu), axis=-1, keepdims=True)
            return (x - mu) * jax.lax.rsqrt(var + EPS) * g + b

        def _sliding_attn(q, k, v, w):
            B, Hh, S, d = q.shape
            nc = S // w
            qc = q.reshape(B, Hh, nc, w, d)
            kp = jnp.pad(k, ((0, 0), (0, 0), (w, w), (0, 0)))
            vp = jnp.pad(v, ((0, 0), (0, 0), (w, w), (0, 0)))
            idx = (jnp.arange(nc) * w)[:, None] + jnp.arange(3 * w)[None, :]
            kc = kp[:, :, idx, :]
            vc = vp[:, :, idx, :]
            scores = jnp.einsum('bhcqd,bhckd->bhcqk', qc, kc)
            q_pos = jnp.arange(nc)[:, None, None] * w + jnp.arange(w)[None, :, None]
            k_pos = jnp.arange(nc)[:, None, None] * w - w + jnp.arange(3 * w)[None, None, :]
            rel = k_pos - q_pos
            valid = (jnp.abs(rel) <= w) & (k_pos >= 0) & (k_pos < S)
            scores = jnp.where(valid[None, None], scores, jnp.float32(-1000000000.0))
            p = jax.nn.softmax(scores, axis=-1)
            out = jnp.einsum('bhcqk,bhckd->bhcqd', p, vc)
            return out.reshape(B, Hh, S, d)
        B, S, _ = src.shape
        d_head = D_MODEL // H
        qkv = src.reshape(B, S, H, d_head).transpose(0, 2, 1, 3)
        attn = _sliding_attn(qkv, qkv, qkv, W)
        attn = attn.transpose(0, 2, 1, 3).reshape(B, S, D_MODEL)
        x = _layernorm(src + attn, ln1_g, ln1_b)
        ff = jnp.maximum(x @ W1 + b1, 0.0) @ W2 + b2
        return _layernorm(x + ff, ln2_g, ln2_b)

    def _L0_xattn_ref(query, key, value, attn_mask, key_padding_mask, Wq, bq, Wk, bk, Wv, bv, Wout, bout):
        import jax, jax.numpy as jnp
        import numpy as np
        EMBED_DIM = 128
        NUM_HEADS = 16
        HEAD_DIM = EMBED_DIM // NUM_HEADS
        SCALE = HEAD_DIM ** (-0.5)
        B, T, C = query.shape
        S = key.shape[1]
        H, D = (NUM_HEADS, HEAD_DIM)
        q = (query @ Wq.T + bq).reshape(B, T, H, D).transpose(0, 2, 1, 3)
        k = (key @ Wk.T + bk).reshape(B, S, H, D).transpose(0, 2, 1, 3)
        v = (value @ Wv.T + bv).reshape(B, S, H, D).transpose(0, 2, 1, 3)
        scores = jnp.einsum('bhtd,bhsd->bhts', q, k) * SCALE
        scores = scores + attn_mask[None, None, :, :]
        scores = jnp.where(key_padding_mask[:, None, None, :], -jnp.inf, scores)
        weights = jax.nn.softmax(scores, axis=-1)
        attn_out = jnp.einsum('bhts,bhsd->bhtd', weights, v)
        attn_out = attn_out.transpose(0, 2, 1, 3).reshape(B, T, C)
        return attn_out @ Wout.T + bout

    def _L0_ffn_ref(x, router_w, router_b, w1, b1, w2, b2):
        import jax, jax.numpy as jnp
        import numpy as np
        DIM = 128
        HIDDEN = 512
        E = 8
        B, S = (2, 512)
        logits = jnp.einsum('bsd,de->bse', x, router_w) + router_b
        probs = jax.nn.softmax(logits, axis=-1)
        top1 = jnp.argmax(probs, axis=-1)
        out = jnp.zeros_like(x)
        for i in range(E):
            h = jnp.einsum('bsd,df->bsf', x, w1[i]) + b1[i]
            a, g = jnp.split(h, 2, axis=-1)
            y = jnp.einsum('bsh,hd->bsd', a * jax.nn.sigmoid(g), w2[i]) + b2[i]
            out = out + jnp.where((top1 == i)[..., None], y, 0.0)
        return out

    def _L1_attn_ref(hidden_states, Wq, bq, Wk, bk, Wv, bv, Wo, bo):
        import jax, jax.numpy as jnp
        import numpy as np
        H = 16
        GRID = 16
        TOK_PER_FRAME = GRID * GRID

        def _rope(x, pos, dim):
            half = dim // 2
            omega = jnp.arange(half, dtype=x.dtype) / (dim / 2.0)
            inv = 1.0 / 10000.0 ** omega
            freq = pos.astype(x.dtype)[:, None] * inv
            sin = jnp.concatenate([jnp.sin(freq), jnp.sin(freq)], axis=-1)
            cos = jnp.concatenate([jnp.cos(freq), jnp.cos(freq)], axis=-1)
            y = x.reshape(*x.shape[:-1], half, 2)
            y1, y2 = (y[..., 0], y[..., 1])
            rot = jnp.stack((-y2, y1), axis=-1).reshape(x.shape)
            return x * cos + rot * sin

        def _apply_3d_rope(qk, f_ids, h_ids, w_ids, d_dim):
            s = 0
            parts = []
            for pos in (f_ids, h_ids, w_ids):
                parts.append(_rope(qk[..., s:s + d_dim], pos, d_dim))
                s += d_dim
            if s < qk.shape[-1]:
                parts.append(qk[..., s:])
            return jnp.concatenate(parts, axis=-1)
        B, N, D = hidden_states.shape
        hd = D // H
        d_dim = 2 * (hd // 3 // 2)

        def heads(x):
            return x.reshape(B, N, H, hd).transpose(0, 2, 1, 3)
        q = heads(hidden_states @ Wq + bq)
        k = heads(hidden_states @ Wk + bk)
        v = heads(hidden_states @ Wv + bv)
        ids = jnp.arange(N)
        f_ids = ids // TOK_PER_FRAME
        rem = ids - TOK_PER_FRAME * f_ids
        h_ids = rem // GRID
        w_ids = rem - GRID * h_ids
        q = _apply_3d_rope(q, f_ids, h_ids, w_ids, d_dim)
        k = _apply_3d_rope(k, f_ids, h_ids, w_ids, d_dim)
        scale = hd ** (-0.5)
        attn = jnp.einsum('bhqd,bhkd->bhqk', q, k) * scale
        attn = jax.nn.softmax(attn.astype(jnp.float32), axis=-1).astype(q.dtype)
        ctx = jnp.einsum('bhqk,bhkd->bhqd', attn, v)
        ctx = ctx.transpose(0, 2, 1, 3).reshape(B, N, D)
        return ctx @ Wo + bo

    def _L1_xattn_ref(query, key, value, qpos, kpos, Wq, bq, Wk, bk, Wv, bv, Wo, bo):
        import jax, jax.numpy as jnp
        import numpy as np
        DIM = 128
        HEADS = 16
        HEAD_DIM = DIM // HEADS
        SCALE = HEAD_DIM ** (-0.5)
        B, Nq, C = query.shape

        def split_heads(x):
            return x.reshape(x.shape[0], x.shape[1], HEADS, HEAD_DIM).transpose(0, 2, 1, 3)
        q = split_heads(query @ Wq + bq)
        k = split_heads(key @ Wk + bk)
        v = split_heads(value @ Wv + bv)
        attn = jnp.einsum('bhqd,bhkd->bhqk', q, k) * SCALE
        attn = jax.nn.softmax(attn, axis=-1)
        x = jnp.einsum('bhqk,bhkd->bhqd', attn, v)
        x = x.transpose(0, 2, 1, 3).reshape(B, Nq, C)
        return x @ Wo + bo

    def _L1_ffn_ref(x, qweights, scales, biases, lora_a, lora_b, ln_gamma, ln_beta):
        import jax, jax.numpy as jnp
        import numpy as np
        GROUP = 16
        EPS = 1e-05

        def _dequant(q, scale):
            w = q.astype(jnp.float32) / 7.5 - 1.0
            return w * jnp.repeat(scale, GROUP, axis=1)

        def _qlora_linear(x, q, scale, bias, la, lb):
            w = _dequant(q, scale)
            base = jnp.einsum('btd,od->bto', x, w) + bias
            lora = jnp.einsum('btr,or->bto', jnp.einsum('btd,rd->btr', x, la), lb)
            return base + lora

        def _layernorm(x, g, b):
            mu = jnp.mean(x, axis=-1, keepdims=True)
            var = jnp.mean(jnp.square(x - mu), axis=-1, keepdims=True)
            return (x - mu) * jax.lax.rsqrt(var + EPS) * g + b
        h = x
        for blk in range(3):
            i0, i1 = (2 * blk, 2 * blk + 1)
            y = _qlora_linear(h, qweights[i0], scales[i0], biases[i0], lora_a[i0], lora_b[i0])
            y = _layernorm(y, ln_gamma[blk], ln_beta[blk])
            y = jax.nn.gelu(y, approximate=False)
            y = _qlora_linear(y, qweights[i1], scales[i1], biases[i1], lora_a[i1], lora_b[i1])
            h = y + h
        return h

    def _L2_attn_ref(x, Wq, bq, Wk, bk, Wv, bv, Wo, bo, sample_idx):
        import jax, jax.numpy as jnp
        import numpy as np
        import math
        D_MODEL = 128
        N_HEADS = 16
        HEAD_DIM = D_MODEL // N_HEADS
        FACTOR = 5
        B, L = (4, 512)
        Bv, Lv, _ = x.shape
        scale = HEAD_DIM ** (-0.5)
        U = min(FACTOR * int(math.ceil(math.log(Lv))), Lv)

        def proj(W, b):
            y = jnp.einsum('bld,de->ble', x, W) + b
            return y.reshape(Bv, Lv, N_HEADS, HEAD_DIM).transpose(0, 2, 1, 3)
        Q = proj(Wq, bq)
        K = proj(Wk, bk)
        V = proj(Wv, bv)
        K_sample = K[:, :, sample_idx, :]
        QK_s = jnp.einsum('bhld,bhsd->bhls', Q, K_sample) * scale
        M = QK_s.max(axis=-1) - QK_s.mean(axis=-1)
        _, top_idx = jax.lax.top_k(M, U)
        Q_red = jnp.take_along_axis(Q, top_idx[..., None], axis=2)
        scores = jnp.einsum('bhud,bhld->bhul', Q_red, K) * scale
        attn = jax.nn.softmax(scores, axis=-1)
        out_red = jnp.einsum('bhul,bhld->bhud', attn, V)
        out = jnp.broadcast_to(V.mean(axis=2, keepdims=True), (Bv, N_HEADS, Lv, HEAD_DIM))
        bi = jnp.arange(Bv)[:, None, None]
        hi = jnp.arange(N_HEADS)[None, :, None]
        out = out.at[bi, hi, top_idx].set(out_red)
        out = out.transpose(0, 2, 1, 3).reshape(Bv, Lv, D_MODEL)
        return jnp.einsum('bld,de->ble', out, Wo) + bo

    def _L2_xattn_ref(x, context, ln_gamma, ln_beta, w_q, w_kv, w_out, b_out, gate):
        import jax, jax.numpy as jnp
        import numpy as np
        DIM = 128
        NUM_HEADS = 16
        DIM_HEAD = 64
        INNER = NUM_HEADS * DIM_HEAD
        SCALE = DIM_HEAD ** (-0.5)

        def _layernorm(x, gamma, beta, eps=1e-05):
            mu = jnp.mean(x, axis=-1, keepdims=True)
            var = jnp.mean(jnp.square(x - mu), axis=-1, keepdims=True)
            return (x - mu) * jax.lax.rsqrt(var + eps) * gamma + beta
        B, SQ, _ = x.shape
        SK = context.shape[1]
        xn = _layernorm(x, ln_gamma, ln_beta)
        q = (xn @ w_q).reshape(B, SQ, NUM_HEADS, DIM_HEAD)
        kv = context @ w_kv
        k, v = jnp.split(kv, 2, axis=-1)
        k = k.reshape(B, SK, NUM_HEADS, DIM_HEAD)
        v = v.reshape(B, SK, NUM_HEADS, DIM_HEAD)
        scores = jnp.einsum('bqhd,bkhd->bhqk', q * SCALE, k)
        attn = jax.nn.softmax(scores, axis=-1)
        out = jnp.einsum('bhqk,bkhd->bqhd', attn, v).reshape(B, SQ, INNER)
        out = out @ w_out + b_out
        return out * jnp.tanh(gate[0])

    def _L2_ffn_ref(x, U1, V1, b1, U2, V2, b2):
        import jax, jax.numpy as jnp
        import numpy as np
        D_MODEL, D_FF, RANK = (128, 512, 32)
        B, S = (4, 512)
        P = jnp.einsum('bsd,dr->bsr', x, U1)
        H = jax.nn.gelu(jnp.einsum('bsr,rf->bsf', P, V1) + b1)
        Q = jnp.einsum('bsf,fr->bsr', H, U2)
        return jnp.einsum('bsr,rd->bsd', Q, V2) + b2

    def _L3_attn_ref(x, w_qkv, w_out):
        import jax, jax.numpy as jnp
        import numpy as np
        B, S, D, H = (4, 1024, 128, 16)
        HD = D // H

        def elu_feature_map(x):
            return jax.nn.elu(x) + 1.0
        Bv, Sv, Dv = x.shape
        qkv = (x @ w_qkv.T).reshape(Bv, Sv, 3, H, HD)
        qkv = jnp.transpose(qkv, (2, 0, 3, 1, 4))
        q, k, v = (qkv[0], qkv[1], qkv[2])
        q = elu_feature_map(q)
        k = elu_feature_map(k)
        kv = jnp.einsum('bhsd,bhse->bhde', k, v)
        out = jnp.einsum('bhsd,bhde->bhse', q, kv)
        k_sum = k.sum(axis=2)
        normalizer = jnp.einsum('bhsd,bhd->bhs', q, k_sum)[..., None]
        normalizer = jnp.maximum(normalizer, 1e-06)
        out = (out / normalizer).transpose(0, 2, 1, 3).reshape(Bv, Sv, Dv)
        return out @ w_out.T

    def _L3_xattn_ref(k, v, q, Wk, Wv, bv, Wq, bq, Wo, bo):
        import jax, jax.numpy as jnp
        import numpy as np
        D_MODEL = 128
        B, S = (4, 256)
        kp = jnp.einsum('bsd,ed->bse', k, Wk)
        vp = jnp.einsum('bsd,ed->bse', v, Wv) + bv
        qp = jnp.einsum('bsd,ed->bse', q, Wq) + bq
        scale = 1.0 / jnp.sqrt(jnp.float32(kp.shape[-1]))
        scores = jnp.einsum('bqd,bkd->bqk', qp, kp) * scale
        probs = jax.nn.softmax(scores, axis=-1)
        ctx = jnp.einsum('bqk,bkd->bqd', probs, vp)
        return jnp.einsum('bqd,ed->bqe', ctx, Wo) + bo

    def _L3_ffn_ref(hidden_states, wg, w1, w3, w2):
        import jax, jax.numpy as jnp
        import numpy as np
        TOP_K = 2
        orig_shape = hidden_states.shape
        H = orig_shape[-1]
        E = wg.shape[0]
        x = hidden_states.reshape(-1, H)
        router_logits = x @ wg.T
        probs = jax.nn.softmax(router_logits, axis=-1)
        topk_w, topk_idx = jax.lax.top_k(probs, TOP_K)
        topk_w = topk_w / jnp.sum(topk_w, axis=-1, keepdims=True)
        expert_w = jnp.sum(jax.nn.one_hot(topk_idx, E, dtype=x.dtype) * topk_w[..., None], axis=1)
        h1 = jnp.einsum('th,eih->tei', x, w1)
        h3 = jnp.einsum('th,eih->tei', x, w3)
        y = jnp.einsum('tei,ehi->teh', jax.nn.silu(h1) * h3, w2)
        out = jnp.einsum('te,teh->th', expert_w, y)
        return out.reshape(orig_shape)
    x = x + _L0_attn_ref(_layernorm(x, axis=-1), L0_attn_ln1_g, L0_attn_ln1_b, L0_attn_ln2_g, L0_attn_ln2_b, L0_attn_W1, L0_attn_b1, L0_attn_W2, L0_attn_b2)
    x = x + _L0_xattn_ref(_layernorm(x, axis=-1), ctx_1024, ctx_1024, mask_SxS2_ff0, mask_BxS2_bf0, L0_xattn_Wq, L0_xattn_bq, L0_xattn_Wk, L0_xattn_bk, L0_xattn_Wv, L0_xattn_bv, L0_xattn_Wout, L0_xattn_bout)
    x = x + _L0_ffn_ref(_layernorm(x, axis=-1), L0_ffn_router_w, L0_ffn_router_b, L0_ffn_w1, L0_ffn_b1, L0_ffn_w2, L0_ffn_b2)
    x = x + _L1_attn_ref(_layernorm(x, axis=-1), L1_attn_Wq, L1_attn_bq, L1_attn_Wk, L1_attn_bk, L1_attn_Wv, L1_attn_bv, L1_attn_Wo, L1_attn_bo)
    x = x + _L1_xattn_ref(_layernorm(x, axis=-1), ctx_1024, ctx_1024, itok_BxS2_0_2047, itok_BxS2_0_2047, L1_xattn_Wq, L1_xattn_bq, L1_xattn_Wk, L1_xattn_bk, L1_xattn_Wv, L1_xattn_bv, L1_xattn_Wo, L1_xattn_bo)
    x = x + _L1_ffn_ref(_layernorm(x, axis=-1), L1_ffn_qweights, L1_ffn_scales, L1_ffn_biases, L1_ffn_lora_a, L1_ffn_lora_b, L1_ffn_ln_gamma, L1_ffn_ln_beta)
    x = x + _L2_attn_ref(_layernorm(x, axis=-1), L2_attn_Wq, L2_attn_bq, L2_attn_Wk, L2_attn_bk, L2_attn_Wv, L2_attn_bv, L2_attn_Wo, L2_attn_bo, L2_attn_sample_idx)
    x = x + _L2_xattn_ref(_layernorm(x, axis=-1), ctx_1024, L2_xattn_ln_gamma, L2_xattn_ln_beta, L2_xattn_w_q, L2_xattn_w_kv, L2_xattn_w_out, L2_xattn_b_out, L2_xattn_gate)
    x = x + _L2_ffn_ref(_layernorm(x, axis=-1), L2_ffn_U1, L2_ffn_V1, L2_ffn_b1, L2_ffn_U2, L2_ffn_V2, L2_ffn_b2)
    x = x + _L3_attn_ref(_layernorm(x, axis=-1), L3_attn_w_qkv, L3_attn_w_out)
    x = x + _L3_xattn_ref(ctx_1024, ctx_1024, _layernorm(x, axis=-1), L3_xattn_Wk, L3_xattn_Wv, L3_xattn_bv, L3_xattn_Wq, L3_xattn_bq, L3_xattn_Wo, L3_xattn_bo)
    x = x + _L3_ffn_ref(_layernorm(x, axis=-1), L3_ffn_wg, L3_ffn_w1, L3_ffn_w3, L3_ffn_w2)
    return x

_drawn_inputs = setup_inputs


def setup_inputs(seed=0):
    import zlib

    import numpy as np

    out = dict(_drawn_inputs(seed))
    spreads = {'mask_SxS2_ff0': (0.0, 0.784),
     'L0_attn_ln1_g': (1.0, 0.2),
     'L0_attn_ln1_b': (0.0, 0.1),
     'L0_attn_ln2_g': (1.0, 0.2),
     'L0_attn_ln2_b': (0.0, 0.1),
     'L0_attn_b1': (0.0, 0.364),
     'L0_attn_b2': (0.0, 0.1),
     'L0_xattn_bq': (0.0, 0.5),
     'L0_xattn_bk': (0.0, 0.8),
     'L0_xattn_bv': (0.0, 0.1),
     'L0_xattn_bout': (0.0, 0.1),
     'L1_attn_bq': (0.0, 0.8),
     'L1_attn_bk': (0.0, 0.8),
     'L1_attn_bv': (0.0, 0.626),
     'L1_attn_bo': (0.0, 0.1),
     'L1_xattn_bq': (0.0, 0.749),
     'L1_xattn_bk': (0.0, 0.8),
     'L1_xattn_bv': (0.0, 0.1),
     'L1_xattn_bo': (0.0, 0.1),
     'L1_ffn_ln_gamma': (1.0, 0.2),
     'L1_ffn_ln_beta': (0.0, 0.1),
     'L2_attn_bq': (0.0, 0.8),
     'L2_attn_bk': (0.0, 0.8),
     'L2_attn_bv': (0.0, 0.558),
     'L2_attn_bo': (0.0, 0.458),
     'L2_xattn_ln_gamma': (1.0, 0.6),
     'L2_xattn_ln_beta': (0.0, 0.8),
     'L2_xattn_b_out': (0.0, 0.8),
     'L2_ffn_b1': (0.0, 0.8),
     'L2_ffn_b2': (0.0, 0.462),
     'L3_xattn_bv': (0.0, 0.551),
     'L3_xattn_bq': (0.0, 0.8),
     'L3_xattn_bo': (0.0, 0.469)}
    factors = {'L0_ffn_b1': 7.885,
     'L0_ffn_b2': 4.621,
     'L1_attn_Wq': 8.0,
     'L1_attn_Wk': 8.0,
     'L1_attn_Wv': 7.669,
     'L1_attn_Wo': 3.956,
     'L1_ffn_biases': 5.762,
     'L1_ffn_lora_a': 5.771,
     'L1_ffn_lora_b': 5.842,
     'L2_attn_Wq': 5.412,
     'L2_attn_Wk': 5.426,
     'L2_xattn_w_q': 3.101,
     'L2_ffn_U1': 8.0,
     'L2_ffn_V1': 8.0,
     'L2_ffn_U2': 8.0,
     'L2_ffn_V2': 8.0,
     'L3_ffn_wg': 8.0,
     'L3_ffn_w1': 8.0,
     'L3_ffn_w3': 8.0,
     'L3_ffn_w2': 8.0}
    for name, (base, spread) in spreads.items():
        noise = np.random.default_rng([zlib.crc32(name.encode()), seed]).standard_normal(out[name].shape)
        drawn = base * np.exp(spread * noise) if base else spread * noise
        out[name] = jnp.asarray(drawn.astype(out[name].dtype))
    for name, factor in factors.items():
        out[name] = (out[name] * factor).astype(out[name].dtype)
    return out
```

```python
from contextlib import ExitStack

import numpy as np
import concourse.bass as bass
from concourse import mybir

F32 = mybir.dt.float32
BF16 = mybir.dt.bfloat16
I32 = mybir.dt.int32
U8 = mybir.dt.uint8
ALU = mybir.AluOpType
ACT = mybir.ActivationFunctionType
AX = mybir.AxisListType

NB, S, D = 16, 128, 128
SC = 77
H, DH = 16, 8
U = 4
NG = NB // U
GT = U * S
WINDOW = 32
HX, DX = 16, 64
E0, F0 = 8, 512
E3, F3 = 8, 256
NSAMP = 35
NTOP = 25
EPS = 1e-5
SCALE8 = float(DH) ** -0.5
GONE = -3.0e38

WIDTHS = [
    ("L0_attn", [("L0a_w1", 512), ("L0a_w2", 512)]),
    ("L0_xattn", [("L0x_wq", 128), ("L0x_wk", 128), ("L0x_wv", 128), ("L0x_wo", 128)]),
    ("L0_ffn", [("L0f_rw", E0), ("L0f_w1", E0 * 2 * F0), ("L0f_w2", E0 * F0)]),
    ("L1_attn", [("L1a_wq", 128), ("L1a_wk", 128), ("L1a_wv", 128), ("L1a_wo", 128)]),
    ("L1_xattn", [("L1x_wq", 128), ("L1x_wk", 128), ("L1x_wv", 128), ("L1x_wo", 128)]),
    ("L1_ffn", [("L1f_la", 768), ("L1f_lb", 768)]),
    ("L2_attn", [("L2a_wq", 128), ("L2a_wk", 128), ("L2a_wv", 128), ("L2a_wo", 128)]),
    ("L2_xattn", [("L2x_wq", 1024), ("L2x_wkv", 2048), ("L2x_wo", 1024)]),
    ("L2_ffn", [("L2f_u1", 32), ("L2f_v1", 512), ("L2f_u2", 128), ("L2f_v2", 128)]),
    ("L3_attn", [("L3a_wqkv", 384), ("L3a_wo", 128)]),
    ("L3_xattn", [("L3x_wq", 128), ("L3x_wk", 128), ("L3x_wv", 128), ("L3x_wo", 128)]),
    ("L3_ffn", [("L3f_wg", E3), ("L3f_w1", E3 * F3), ("L3f_w3", E3 * F3), ("L3f_w2", E3 * F3)]),
]
WAT, WSPAN, _at = {}, {}, 0
for _block, _parts in WIDTHS:
    if _block == "L3_ffn":
        WHBM, WCOLS = _at + sum(n for _, n in _parts), _at
        _at = WSPAN["L0_ffn"][0]
    _first = _at
    for _name, _n in _parts:
        WAT[_name] = (_at, _n)
        _at += _n
    WSPAN[_block] = (_first, _at)
assert WSPAN["L3_ffn"][1] <= WSPAN["L0_ffn"][1]

COLS = [("L0a_g1", 1), ("L0a_b1", 1), ("L0a_fb", 4), ("L0x_bq", 1), ("L0x_bk", 1), ("L0x_bv", 1),
        ("L0f_b1", 64), ("L1a_bq", 1), ("L1a_bk", 1), ("L1a_bv", 1), ("L1x_bq", 1), ("L1x_bk", 1),
        ("L1x_bv", 1), ("L1f_g", 3), ("L1f_b", 3), ("L2a_bq", 1), ("L2a_bk", 1), ("L2a_bv", 1),
        ("L2x_g", 1), ("L2x_b", 1), ("L2f_b1", 4), ("L3x_bq", 1), ("L3x_bv", 1)]
ROWS = [("L0a_b2", 128), ("L0x_bo", 128), ("L0f_rb", E0), ("L0f_b2", E0 * 128), ("L1a_bo", 128),
        ("L1x_bo", 128), ("L1f_bias", 768), ("L2a_bo", 128), ("L2x_bo", 128), ("L2f_b2", 128),
        ("L3x_bo", 128)]
CONSTS = [("ident", 128), ("bdiag", 128), ("bdiag16", 16), ("heads4", 4), ("rot", 128), ("cos", 128),
          ("sin", 128), ("window", 128), ("rank", 8), ("part", 1)]


def offsets(table):
    at, out = 0, {}
    for name, n in table:
        out[name] = (at, n)
        at += n
    return out, at


CAT, NCOLS = offsets(COLS)
RAT, NROWS = offsets(ROWS)
KAT, NCONST = offsets(CONSTS)

NORM = dict(xg_ready=1, stats=U, moments=U, vareps=1, rstd=1, xn_ready=U, xnT_psum=1, xnT_ready=1)
HEADS = dict(q_psum=1, q_ready=1, k_psum=1, k_ready=4, v_psum=1, v_ready=1,
             s_psum=8, s_max=8, s_sub=8, p_ready=8, pt_psum=8, pt_ready=8, o_psum=8,
             o_recip=U, o_ready=U)
PROJ = dict(oT_psum=1, oT_ready=1, y_psum=1, x_done=1)


def times(d, n):
    return {k: v * n for k, v in d.items()}


def merged(*parts):
    out = {}
    for p in parts:
        for k, v in p.items():
            out[k] = out.get(k, 0) + v
    return out


LN = dict(stats=U, moments=U, vareps=1, rstd=1, xn_ready=U)
LNT = dict(xnT_psum=1, xnT_ready=1)
EXPERTS0 = dict(gv_psum=E0 * 4, sg_ready=E0 * 4, h_ready=E0 * 4, ye_psum=E0, acc=E0 * U)
EXPERTS3 = dict(gv_psum=E3 * 2, sg_ready=E3 * 2, h_ready=E3 * 2, ye_psum=E3, acc=E3 * U)
PER = {
    "L0_attn": merged(NORM, HEADS, LN, LNT, LN, dict(res1=1, f_psum=4, f_ready=4, y_psum=1, x_done=3,
                                                     q_psum=-1, q_ready=-1, k_psum=-1, v_psum=-1)),
    "L0_xattn": merged(NORM, HEADS, PROJ, dict(ctx_ready=1, s_mask=8)),
    "L0_ffn": merged(NORM, EXPERTS0, dict(r_psum=1, r_step=5, x_done=1)),
    "L1_attn": merged(NORM, HEADS, PROJ, dict(rot_psum=2, rope=6, kT_ready=1)),
    "L1_xattn": merged(NORM, HEADS, PROJ, dict(ctx_ready=1)),
    "L1_ffn": merged(NORM, times(LN, 3), times(LNT, 5), dict(y_psum=6, h_res=3, x_done=1)),
    "L2_attn": merged(NORM, HEADS, PROJ, dict(smp_psum=2, smp_ready=5, smps_psum=4, smp_red=16, m_step=3,
                                              mT_psum=1, top=9, sel_psum=1, sel_ready=2, vm_psum=1,
                                              vm_ready=1, o_mix=8)),
    "L2_xattn": merged(NORM, LN, dict(ctx_ready=1, q_psum=8, q_ready=8, k_psum=8, k_ready=8, v_psum=8,
                                           v_ready=8, s_psum=16, s_max=16, s_sub=16, p_ready=16, s_sum=16,
                                           s_rec=16, s_nrm=16, pt_psum=16, pt_ready=16, o_psum=16,
                                           oT_ready=16, y_psum=1, x_done=1)),
    "L2_ffn": merged(NORM, dict(q_psum=1, q_ready=1, f_psum=4, f_ready=4, o_psum=1, oT_ready=1, y_psum=1,
                                x_done=1)),
    "L3_attn": merged(NORM, PROJ, dict(q_psum=1, q_ready=1, k_psum=2, v_ready=2, elu_min=3, elu_exp=3, k_ready=2,
                                       s_psum=U, kv_ready=2 * U, o_psum=U, o_recip=2 * U, o_ready=U)),
    "L3_xattn": merged(NORM, PROJ, dict(ctx_ready=1, q_psum=1, q_ready=1, k_psum=1, k_ready=1, v_psum=1,
                                        v_ready=1, s_psum=1, s_max=1, s_sub=1, p_ready=1, s_sum=1, s_rec=1,
                                        s_nrm=1, pt_psum=1, pt_ready=1), ),
    "L3_ffn": merged(NORM, EXPERTS3, dict(r_psum=1, r_step=16, g_step=3, r_exp=1, x_done=1)),
}
BLOCKS = [b for b, _ in WIDTHS]
NAMES = sorted({k for d in PER.values() for k in d})
BASE, _sum = {}, {n: 0 for n in NAMES}
_sum["x_done"] = 1
for _b in BLOCKS:
    BASE[_b] = dict(_sum)
    for _k, _v in PER[_b].items():
        _sum[_k] += NG * _v


def build(nc, io):
    with ExitStack() as ctx:
        def sb(name, shape, dt=F32):
            return ctx.enter_context(nc.sbuf_tensor(name, shape, dt))

        def psum(name, shape, dt=F32):
            return ctx.enter_context(nc.psum_tensor(name, shape, dt))

        sem = {n: ctx.enter_context(nc.semaphore(n)) for n in NAMES}
        loaded = {b: ctx.enter_context(nc.semaphore("loaded_" + b)) for b in BLOCKS}
        small_in = ctx.enter_context(nc.semaphore("small_in"))
        x_in = ctx.enter_context(nc.semaphore("x_in"))
        setup_v = ctx.enter_context(nc.semaphore("setup_v"))
        setup_g = ctx.enter_context(nc.semaphore("setup_g"))
        setup_a = ctx.enter_context(nc.semaphore("setup_a"))
        lora_psum = ctx.enter_context(nc.semaphore("lora_psum"))
        passed_v = ctx.enter_context(nc.semaphore("passed_v"))
        passed_t = ctx.enter_context(nc.semaphore("passed_t"))
        stored = ctx.enter_context(nc.semaphore("stored"))

        class Counts:

            def __init__(self, block, g):
                self.block, self.g = block, g

            def __call__(self, name, k):
                per, base = PER[self.block][name], BASE[self.block][name]
                return sem[name], self.g * per + (base + k)

        w_all = sb("w_all", [128, WCOLS])
        consts = sb("consts", [128, NCONST])
        cols = sb("cols", [128, NCOLS])
        rows = sb("rows", [1, NROWS])
        x = sb("x", [128, NB * D])
        ctxT = sb("ctxT", [128, NB * SC])
        ones = sb("ones", [128, 128])
        mean_w = sb("mean_w", [128, 128])
        neghalf = sb("neghalf", [128, U])
        window_bf = sb("window_bf", [128, S], BF16)
        ident_bf = sb("ident_bf", [128, 128], BF16)
        g2b = sb("g2b", [128, 2, D])
        gate = sb("gate", [128, 2])
        amask = sb("amask", [128, SC])
        pad_words = sb("pad_words", [128, NB * SC // 4], I32)
        pad_u8 = pad_words[:, :].bitcast(U8)
        cmask = sb("cmask", [128, NB * SC])
        idx_i = sb("idx_i", [128, NSAMP], I32)
        idx_f = sb("idx_f", [128, 2, NSAMP])
        onehot = sb("onehot", [128, NSAMP])
        wt = sb("wt", [128, 768])

        xg = sb("xg", [128, GT])
        st = sb("st", [128, U, 6])
        mv = sb("mv", [128, U, 2])
        ve = sb("ve", [128, U])
        rstd = sb("rstd", [128, U])
        xn = sb("xn", [128, GT])
        xm = sb("xm", [128, GT])
        xnT = sb("xnT", [128, GT])
        xmT = sb("xmT", [128, GT])
        qT = sb("qT", [128, GT])
        kTr = sb("kTr", [128, GT])
        kTx = sb("kTx", [128, U, 4, S])
        vx = sb("vx", [128, U, H, DH + 1])
        smx = sb("smx", [128, 2, 8])
        p = sb("p", [128, 2, 8 * S])
        pT = sb("pT", [128, 2, 8, S])
        qw = pT[:, 0, 0:6, :].rearrange("p j s -> p (j s)").bitcast(I32)
        scl = pT[:, 1, 0:6, :].rearrange("p j s -> p (j s)")
        rec = sb("rec", [128, 2, H])
        on = sb("on", [128, GT])
        oT = sb("oT", [128, GT])
        ctxg = sb("ctxg", [128, U * SC])
        fT = sb("fT", [128, 2, 4, GT])
        rope1, rope2 = fT[:, 1, 0:2, :], fT[:, 1, 2:4, :]
        sg = sb("sg", [128, 2, GT])
        acc = sb("acc", [128, GT])
        gates = sb("gates", [128, U, 8])
        rt = sb("rt", [128, 6, U, 8])
        rm = sb("rm", [128, 6, U])
        xsT = sb("xsT", [128, U * NSAMP])
        ksx = sb("ksx", [128, U, 4, NSAMP])
        red = sb("red", [128, 3, U * H])
        cand = sb("cand", [U * H, 5, S])
        top8 = sb("top8", [U * H, 4, 8])
        sel = sb("sel", [128, 2, U * H])
        vmean = sb("vmean", [128, GT])
        kvm = sb("kvm", [128, 2, D + H])

        a0 = WAT["L0f_w1"][0]
        qT8 = w_all[:, a0:a0 + 8 * GT].rearrange("p (b t) -> p b t", b=8)
        kT8 = w_all[:, a0 + 8 * GT:a0 + 8 * GT + 8 * U * SC].rearrange("p (b t) -> p b t", b=8)
        v8 = w_all[:, a0 + 7168:a0 + 7168 + U * 1024].rearrange("p (u n) -> p u n", u=U)
        assert 8 * GT + 8 * U * SC <= 7168 and a0 + 7168 + U * 1024 <= WSPAN["L0_ffn"][1]

        psS = [psum("psS0", [128, 2, 512]), psum("psS1", [128, 2, 512])]
        psT = psum("psT", [128, 2, 512])
        psA = psum("psA", [128, 512])
        psB = psum("psB", [128, 512])
        psO = [psA, psB]

        def w(name, a=0, b=None):
            at, n = WAT[name]
            return w_all[:, at + a:at + (n if b is None else b)]

        def col(name, i=0):
            return cols[:, CAT[name][0] + i:CAT[name][0] + i + 1]

        def row(name, a=0, b=None):
            at, n = RAT[name]
            return rows[0:1, at + a:at + (n if b is None else b)]

        def const(name):
            at, n = KAT[name]
            return consts[:, at:at + n]

        ident, bdiag, bdiag16 = const("ident"), const("bdiag"), const("bdiag16")
        heads4, rank, part = const("heads4"), const("rank"), const("part")
        ones_row = ones[0:1, 0:128]

        def un(t, u):
            return t[:, u * 128:(u + 1) * 128]

        block = ctx.enter_context(nc.Block())
        NSMALL = 13

        @block.sync
        def _(sp):
            sp.dma_start(x[:, :], io["x"]).then_inc(x_in, 16)
            sp.dma_start(consts[:, :], io["consts"]).then_inc(small_in, 16)
            sp.dma_start(cols[:, :], io["cols"]).then_inc(small_in, 16)
            sp.dma_start(rows[:, :], io["rows"]).then_inc(small_in, 16)
            sp.dma_start(ctxT[:, :], io["ctxT"]).then_inc(small_in, 16)
            sp.dma_start(amask[:, :], io["amask"]).then_inc(small_in, 16)
            sp.dma_start(pad_words[:, :], io["pad"].partition_broadcast(128)).then_inc(small_in, 16)
            sp.dma_start(g2b[:, 0, :], io["ln2_g"].partition_broadcast(128)).then_inc(small_in, 16)
            sp.dma_start(g2b[:, 1, :], io["ln2_b"].partition_broadcast(128)).then_inc(small_in, 16)
            sp.dma_start(gate[:, 0:1], io["gate"].partition_broadcast(128)).then_inc(small_in, 16)
            sp.dma_start(idx_i[:, :], io["idx"].partition_broadcast(128)).then_inc(small_in, 16)
            sp.dma_start(qw, io["qw"]).then_inc(small_in, 16)
            sp.dma_start(scl, io["scl"]).then_inc(small_in, 16)
            for b in BLOCKS[:6]:
                a, z = WSPAN[b]
                sp.dma_start(w_all[:, a:z], io["w"][:, a:z]).then_inc(loaded[b], 16)
            for b in BLOCKS[6:11]:
                a, z = WSPAN[b]
                sp.dma_start(w_all[:, a:z], io["w"][:, a:z]).then_inc(loaded[b], 16)
            sp.wait_ge(sem["x_done"], BASE["L2_ffn"]["x_done"])
            a, z = WSPAN["L3_ffn"]
            sp.dma_start(w_all[:, a:z], io["w"][:, WCOLS:WHBM]).then_inc(loaded["L3_ffn"], 16)
            sp.wait_ge(sem["x_done"], _sum["x_done"])
            sp.dma_start(io["out"], x[:, :]).then_inc(stored, 16)
            sp.wait_ge(stored, 16)

        def norm_dve(dve, at, r, src, dst, after=None):
            for u in range(U):
                if after:
                    dve.wait_ge(*after(u))
                nc.vector.bn_stats(st[:, u, :], src(u)).then_inc(sem["stats"], 1)
            dve.wait_ge(*at("stats", r * U + U))
            met_dve(dve)
            for u in range(U):
                nc.vector.bn_aggr(mv[:, u, :], st[:, u, :]).then_inc(sem["moments"], 1)
            dve.wait_ge(*at("moments", (r + 1) * U))
            nc.vector.tensor_scalar(ve[:, :], mv[:, :, 1], EPS, None, ALU.add).then_inc(sem["vareps"], 1)
            dve.wait_ge(*at("rstd", r + 1))
            for u in range(U):
                nc.vector.tensor_scalar(dst(u), src(u), mv[:, u, 0:1], rstd[:, u:u + 1],
                                        ALU.subtract, ALU.mult).then_inc(sem["xn_ready"], 1)

        def norm_pool(pool, at, r):
            pool.wait_ge(*at("vareps", r + 1))
            nc.gpsimd.tensor_tensor(rstd[:, :], ve[:, :], neghalf[:, :], ALU.pow).then_inc(sem["rstd"], 1)

        def met_dve(dve):
            dve.sem_inc(passed_v, 1)

        def met_pe(pe):
            pe.sem_inc(passed_t, 1)

        def load_group_dve(dve, at, g):
            dve.wait_ge(*at("x_done", 0))
            met_dve(dve)
            nc.vector.tensor_copy(xg[:, :], x[:, bass.ts(g, GT)]).then_inc(sem["xg_ready"], 1)

        def norm_in_dve(dve, at, g):
            load_group_dve(dve, at, g)
            dve.wait_ge(*at("xg_ready", 1))
            norm_dve(dve, at, 0, lambda u: un(xg, u), lambda u: un(xn, u))

        def flip_pe(pe, at, r, src, ready, k0):
            for u in range(U):
                pe.wait_ge(*at(ready, k0 + u + 1))
                ins = nc.tensor.transpose(un(psA, u), un(src, u), ident)
            ins.then_inc(sem["xnT_psum"], 1)

        def flip_act(act, at, r, dst):
            act.wait_ge(*at("xnT_psum", r + 1))
            nc.scalar.copy(dst[:, :], psA[:, :]).then_inc(sem["xnT_ready"], 1)

        def ctx_pool(pool, at, g):
            pool.wait_ge(*at("x_done", 0))
            nc.gpsimd.tensor_copy(ctxg[:, :], ctxT[:, bass.ts(g, U * SC)]).then_inc(sem["ctx_ready"], 1)

        def score_step_pe(pe, at, i, nk, window=False, qsrc=qT):
            u, half = divmod(i, 2)
            if i == 0:
                if not window:
                    pe.wait_ge(*at("q_ready", 1))
                    pe.wait_ge(*at("v_ready", 1))
                pe.wait_ge(*at("k_ready", 4))
            if i >= 2:
                pe.wait_ge(*at("s_sub", i - 1))
            for b in range(2):
                g = 2 * half + b
                rs = slice(32 * g, 32 * g + 32)
                ins = nc.tensor.matmul(psS[half][:, b, 0:4 * nk], qsrc[rs, u * S:(u + 1) * S],
                                       kTx[rs, u, :, 0:nk], start=True, stop=not window)
            if window:
                for b in range(2):
                    ins = nc.tensor.matmul(psS[half][:, b, 0:4 * nk], ident_bf[:, :],
                                           window_bf[:, :].unsqueeze(1).broadcast_to([128, 4, S]),
                                           start=False, stop=True)
            ins.then_inc(sem["s_psum"], 1)

        def turn_step_pe(pe, at, i, nk):
            pe.wait_ge(*at("p_ready", i + 1))
            if i >= 1:
                pe.wait_ge(*at("pt_ready", i))
            for j in range(8):
                ins = nc.tensor.transpose(psT[0:nk, j // 4, (j % 4) * S:(j % 4 + 1) * S],
                                          p[:, i % 2, j * nk:(j + 1) * nk], ident)
            ins.then_inc(sem["pt_psum"], 1)

        def value_step_pe(pe, at, i, nk):
            u, half = divmod(i, 2)
            pe.wait_ge(*at("pt_ready", i + 1))
            if u >= 2:
                pe.wait_ge(*at("o_ready", u - 1))
            for j in range(8):
                h = 8 * half + j
                ins = nc.tensor.matmul(psO[u % 2][:, h * (DH + 1):(h + 1) * (DH + 1)], pT[0:nk, i % 2, j, :],
                                       vx[0:nk, u, h, :], start=True, stop=True)
            ins.then_inc(sem["o_psum"], 1)

        def heads_pe(pe, at, nk, window=False, qsrc=qT):
            for t in range(2 * U + 2):
                if t < 2 * U:
                    score_step_pe(pe, at, t, nk, window, qsrc)
                if 1 <= t <= 2 * U:
                    turn_step_pe(pe, at, t - 1, nk)
                if t >= 2:
                    value_step_pe(pe, at, t - 2, nk)

        def s_view(half, nk):
            return psS[half][:, :, 0:4 * nk].rearrange("p b (j k) -> p b j k", j=4)

        def softmax_step_dve(dve, at, i, nk, mask=None):
            half = i % 2
            dve.wait_ge(*at("s_psum", i + 1))
            if mask is not None:
                for b in range(2):
                    m = mask(i // 2).unsqueeze(1).broadcast_to([128, 4, nk])
                    sv = psS[half][:, b, 0:4 * nk].rearrange("p (j k) -> p j k", j=4)
                    ins = nc.vector.tensor_tensor(sv, sv, m, ALU.add)
                ins.then_inc(sem["s_mask"], 1)
                dve.wait_ge(*at("s_mask", i + 1))
            mx = smx[:, half, :].rearrange("p (b j) -> p b j", b=2)
            nc.vector.tensor_reduce(mx, s_view(half, nk), AX.X, ALU.max).then_inc(sem["s_max"], 1)
            dve.wait_ge(*at("s_max", i + 1))
            if i >= 2:
                dve.wait_ge(*at("pt_psum", i - 1))
            pv = p[:, half, 0:8 * nk].rearrange("p (b j k) -> p b j k", b=2, j=4)
            nc.vector.tensor_tensor(pv, s_view(half, nk), mx.unsqueeze(3).broadcast_to([128, 2, 4, nk]),
                                    ALU.subtract).then_inc(sem["s_sub"], 1)

        def finish_heads_dve(dve, at, u, dst=None):
            dve.wait_ge(*at("o_psum", 2 * u + 2))
            o = psO[u % 2][:, 0:H * (DH + 1)].rearrange("p (h e) -> p h e", h=H)
            nc.vector.reciprocal(rec[:, u % 2, :], o[:, :, DH]).then_inc(sem["o_recip"], 1)
            dve.wait_ge(*at("o_recip", u + 1))
            dv = un(on, u).rearrange("p (h e) -> p h e", h=H)
            rb = rec[:, u % 2, :].unsqueeze(2).broadcast_to([128, H, DH])
            if dst is None:
                nc.vector.tensor_tensor(dv, o[:, :, 0:DH], rb, ALU.mult).then_inc(sem["o_ready"], 1)
            else:
                dst(u, dv, o[:, :, 0:DH], rb)

        def heads_dve(dve, at, nk, mask=None, dst=None):
            for t in range(2 * U + 2):
                if t < 2 * U:
                    softmax_step_dve(dve, at, t, nk, mask)
                if t >= 3 and t % 2 == 1:
                    finish_heads_dve(dve, at, (t - 3) // 2, dst)

        def heads_act(act, at, nk, scale):
            for t in range(2 * U + 1):
                if t < 2 * U:
                    act.wait_ge(*at("s_sub", t + 1))
                    pv = p[:, t % 2, 0:8 * nk]
                    nc.scalar.activation(pv, pv, ACT.Exp, scale=scale).then_inc(sem["p_ready"], 1)
                if t >= 1:
                    i = t - 1
                    act.wait_ge(*at("pt_psum", i + 1))
                    if i >= 2:
                        act.wait_ge(*at("o_psum", i - 1))
                    nc.scalar.copy(pT[0:nk, i % 2, :, :].rearrange("p (b j) s -> p b (j s)", b=2),
                                   psT[0:nk, :, :]).then_inc(sem["pt_ready"], 1)

        def expand_keys_dve(dve, at, nk, src, bias, ready):
            dve.wait_ge(*ready)
            for j in range(4):
                nc.vector.tensor_scalar(kTx[:, :, j, 0:nk], src.rearrange("p (u k) -> p u k", u=U), bias,
                                        heads4[:, j:j + 1], ALU.add, ALU.mult).then_inc(sem["k_ready"], 1)

        def values_act(act, at, nk, src):
            act.wait_ge(*at("v_psum", 1))
            nc.scalar.copy(vx[0:nk, :, :, 0:DH].rearrange("p u h e -> p (u h) e"),
                           src.rearrange("p (n e) -> p n e", e=DH)).then_inc(sem["v_ready"], 1)

        def project_pe(pe, at, wo, bo):
            pe.wait_ge(*at("o_ready", U))
            for u in range(U):
                ins = nc.tensor.transpose(un(psB, u), un(on, u), ident)
            ins.then_inc(sem["oT_psum"], 1)
            rows_pe(pe, at, oT, wo, bo, at("oT_ready", 1))

        def rows_pe(pe, at, lhs, wo, bo, ready, dst=psA):
            pe.wait_ge(*ready)
            for u in range(U):
                ins = nc.tensor.matmul(un(dst, u), un(lhs, u), wo, start=True, stop=bo is None)
                if bo is not None:
                    ins = nc.tensor.matmul(un(dst, u), ones_row, bo, start=False, stop=True)
            ins.then_inc(sem["y_psum"], 1)

        def project_act(act, at, bv):
            act.wait_ge(*at("oT_psum", 1))
            if bv is None:
                nc.scalar.copy(oT[:, :], psB[:, :]).then_inc(sem["oT_ready"], 1)
            else:
                nc.scalar.activation(oT[:, :], psB[:, :], ACT.Identity, bias=bv).then_inc(sem["oT_ready"], 1)

        def residual_dve(dve, at, g, k=1, bank=psA):
            dve.wait_ge(*at("y_psum", k))
            nc.vector.tensor_tensor(x[:, bass.ts(g, GT)], xg[:, :], bank[:, :], ALU.add).then_inc(sem["x_done"], 1)

        def l0_attn_pe(pe, at, g):
            flip_pe(pe, at, 0, xn, "xn_ready", 0)
            pe.wait_ge(*at("xnT_ready", 1))
            pe.wait_ge(*at("v_ready", 1))
            heads_pe(pe, at, S, window=True, qsrc=xnT)
            flip_pe(pe, at, 1, xm, "xn_ready", U)
            pe.wait_ge(*at("xnT_ready", 2))
            for b in range(4):
                nc.tensor.matmul(psS[b // 2][:, b % 2, :], w("L0a_w1", b * 128, b * 128 + 128), xmT[:, :],
                                 start=True, stop=True).then_inc(sem["f_psum"], 1)
            pe.wait_ge(*at("f_ready", 4))
            for u in range(U):
                for b in range(4):
                    nc.tensor.matmul(un(psB, u), un(fT[:, 0, b, :], u), w("L0a_w2", b * 128, b * 128 + 128),
                                     start=(b == 0), stop=False)
                nc.tensor.matmul(un(psB, u), un(xmT, u), ident, start=False, stop=False)
                ins = nc.tensor.matmul(un(psB, u), ones_row, row("L0a_b2"), start=False, stop=True)
            ins.then_inc(sem["y_psum"], 1)

        def l0_attn_act(act, at, g):
            flip_act(act, at, 0, xnT)
            act.wait_ge(*at("xn_ready", U))
            nc.scalar.copy(vx[:, :, :, 0:DH].rearrange("p u h e -> p (u h) e"),
                           xn[:, :].rearrange("p (n e) -> p n e", e=DH)).then_inc(sem["v_ready"], 1)
            heads_act(act, at, S, 1.0)
            act.wait_ge(*at("xnT_psum", 2))
            nc.scalar.activation(xmT[:, :], psA[:, :], ACT.Identity, bias=col("L0a_b1"),
                                 scale=col("L0a_g1")).then_inc(sem["xnT_ready"], 1)
            for b in range(4):
                act.wait_ge(*at("f_psum", b + 1))
                nc.scalar.activation(fT[:, 0, b, :], psS[b // 2][:, b % 2, :], ACT.Relu,
                                     bias=col("L0a_fb", b)).then_inc(sem["f_ready"], 1)

        def l0_attn_dve(dve, at, g):
            norm_in_dve(dve, at, g)
            dve.wait_ge(*at("xnT_ready", 1))
            for j in range(4):
                nc.vector.tensor_scalar(kTx[:, :, j, :], xnT[:, :].rearrange("p (u k) -> p u k", u=U),
                                        heads4[:, j:j + 1], None, ALU.mult).then_inc(sem["k_ready"], 1)
            heads_dve(dve, at, S)
            dve.wait_ge(*at("o_ready", U))
            nc.vector.tensor_tensor(on[:, :], on[:, :], xn[:, :], ALU.add).then_inc(sem["res1"], 1)
            dve.wait_ge(*at("res1", 1))
            norm_dve(dve, at, 1, lambda u: un(on, u), lambda u: un(xm, u))
            norm_dve(dve, at, 2, lambda u: un(psB, u), lambda u: un(xn, u), after=lambda u: at("y_psum", 1))
            dve.wait_ge(*at("xn_ready", 3 * U))
            v3 = xn[:, :].rearrange("p (u d) -> p u d", u=U)
            gain = g2b[:, 0, :].unsqueeze(1).broadcast_to([128, U, D])
            shift = g2b[:, 1, :].unsqueeze(1).broadcast_to([128, U, D])
            nc.vector.tensor_tensor(v3, v3, gain, ALU.mult).then_inc(sem["x_done"], 1)
            dve.wait_ge(*at("x_done", 1))
            nc.vector.tensor_tensor(v3, v3, shift, ALU.add).then_inc(sem["x_done"], 1)
            dve.wait_ge(*at("x_done", 2))
            nc.vector.tensor_tensor(x[:, bass.ts(g, GT)], xg[:, :], xn[:, :], ALU.add).then_inc(sem["x_done"], 1)

        def l0_attn_pool(pool, at, g):
            for r in range(3):
                norm_pool(pool, at, r)

        def cross_pe(pe, at, g, pre, wo, bo):
            pe.wait_ge(*at("ctx_ready", 1))
            nc.tensor.matmul(psS[0][:, 0, 0:U * SC], w(pre + "_wk"), ctxg[:, :], start=True,
                             stop=True).then_inc(sem["k_psum"], 1)
            for u in range(U):
                ins = nc.tensor.matmul(psS[1][0:SC, 0, u * 128:(u + 1) * 128], ctxg[:, u * SC:(u + 1) * SC],
                                       w(pre + "_wv"), start=True, stop=True)
            ins.then_inc(sem["v_psum"], 1)
            flip_pe(pe, at, 0, xn, "xn_ready", 0)
            pe.wait_ge(*at("xnT_ready", 1))
            nc.tensor.matmul(psB[:, :], w(pre + "_wq"), xnT[:, :], start=True, stop=True).then_inc(sem["q_psum"], 1)
            heads_pe(pe, at, SC)
            project_pe(pe, at, wo, bo)

        def cross_act(act, at, g, pre, scale, q_on_act=True):
            values_act(act, at, SC, psS[1][0:SC, 0, :])
            flip_act(act, at, 0, xnT)
            if q_on_act:
                act.wait_ge(*at("q_psum", 1))
                nc.scalar.activation(qT[:, :], psB[:, :], ACT.Identity, bias=col(pre + "_bq")).then_inc(sem["q_ready"], 1)
            heads_act(act, at, SC, scale)
            project_act(act, at, col(pre + "_bv"))

        def cross_pool(pool, at, g):
            ctx_pool(pool, at, g)
            norm_pool(pool, at, 0)

        def l0_xattn_dve(dve, at, g):
            norm_in_dve(dve, at, g)
            expand_keys_dve(dve, at, SC, psS[0][:, 0, 0:U * SC], col("L0x_bk"), at("k_psum", 1))
            dve.wait_ge(*at("q_psum", 1))
            nc.vector.tensor_scalar(qT[:, :], psB[:, :], col("L0x_bq"), SCALE8, ALU.add,
                                    ALU.mult).then_inc(sem["q_ready"], 1)
            heads_dve(dve, at, SC, mask=lambda u: cmask[:, bass.ts(g * U + u, SC)])
            residual_dve(dve, at, g)

        def l1_xattn_dve(dve, at, g):
            norm_in_dve(dve, at, g)
            expand_keys_dve(dve, at, SC, psS[0][:, 0, 0:U * SC], col("L1x_bk"), at("k_psum", 1))
            heads_dve(dve, at, SC)
            residual_dve(dve, at, g)

        def experts_pe(pe, at, g, ne, nb, wgate, wval, wout, bout):
            for e in range(ne):
                for b in range(nb):
                    j = e * nb + b
                    if j >= 2:
                        pe.wait_ge(*at("h_ready", j - 1))
                    nc.tensor.matmul(psS[0][:, j % 2, :], wgate(e, b), xnT[:, :], start=True, stop=True)
                    nc.tensor.matmul(psS[1][:, j % 2, :], wval(e, b), xnT[:, :], start=True,
                                     stop=True).then_inc(sem["gv_psum"], 1)
                if e >= 1:
                    expert_out_pe(pe, at, e - 1, nb, wout, bout)
            expert_out_pe(pe, at, ne - 1, nb, wout, bout)

        def expert_out_pe(pe, at, e, nb, wout, bout):
            pe.wait_ge(*at("h_ready", (e + 1) * nb))
            if e >= 2:
                pe.wait_ge(*at("acc", (e - 1) * U))
            for u in range(U):
                for b in range(nb):
                    ins = nc.tensor.matmul(un(psT[:, e % 2, :], u), un(fT[:, e % 2, b, :], u), wout(e, b),
                                           start=(b == 0), stop=(b == nb - 1 and bout is None))
                if bout is not None:
                    ins = nc.tensor.matmul(un(psT[:, e % 2, :], u), ones_row, bout(e), start=False, stop=True)
            ins.then_inc(sem["ye_psum"], 1)

        def experts_act(act, at, ne, nb, func, bgate):
            for j in range(ne * nb):
                act.wait_ge(*at("gv_psum", j + 1))
                if j >= 2:
                    act.wait_ge(*at("h_ready", j - 1))
                bias = bgate(j // nb, j % nb) if bgate else 0.0
                nc.scalar.activation(sg[:, j % 2, :], psS[0][:, j % 2, :], func, bias=bias).then_inc(sem["sg_ready"], 1)

        def experts_dve(dve, at, g, ne, nb, bval):
            for e in range(ne):
                for b in range(nb):
                    j = e * nb + b
                    dve.wait_ge(*at("sg_ready", j + 1))
                    if e >= 2 and b == 0:
                        dve.wait_ge(*at("ye_psum", e - 1))
                    hv = psS[1][:, j % 2, :]
                    if bval:
                        ins = nc.vector.scalar_tensor_tensor(out=fT[:, e % 2, b, :], in0=hv, scalar=bval(e, b),
                                                             in1=sg[:, j % 2, :], op0=ALU.add, op1=ALU.mult)
                    else:
                        ins = nc.vector.tensor_tensor(fT[:, e % 2, b, :], hv, sg[:, j % 2, :], ALU.mult)
                    ins.then_inc(sem["h_ready"], 1)
                if e >= 1:
                    gather_dve(dve, at, g, e - 1, ne)
            gather_dve(dve, at, g, ne - 1, ne)

        def gather_dve(dve, at, g, e, ne):
            dve.wait_ge(*at("ye_psum", e + 1))
            for u in range(U):
                if e >= 1:
                    dve.wait_ge(*at("acc", (e - 1) * U + u + 1))
                base = xg if e == 0 else acc
                nc.vector.scalar_tensor_tensor(out=un(acc, u), in0=un(psT[:, e % 2, :], u),
                                               scalar=gates[:, u, e:e + 1], in1=un(base, u), op0=ALU.mult,
                                               op1=ALU.add).then_inc(sem["acc"], 1)
            if e == ne - 1:
                dve.wait_ge(*at("acc", ne * U))
                met_dve(dve)
                nc.vector.tensor_copy(x[:, bass.ts(g, GT)], acc[:, :]).then_inc(sem["x_done"], 1)

        def router_pe(pe, at, wr, br):
            for u in range(U):
                ins = nc.tensor.matmul(psB[:, u * 8:(u + 1) * 8], un(xnT, u), wr, start=True, stop=br is None)
                if br is not None:
                    ins = nc.tensor.matmul(psB[:, u * 8:(u + 1) * 8], ones_row, br, start=False, stop=True)
            ins.then_inc(sem["r_psum"], 1)

        logits = psB[:, 0:U * 8].rearrange("p (u e) -> p u e", u=U)

        def b8(t):
            return t.unsqueeze(2).broadcast_to([128, U, 8])

        rank4 = rank.unsqueeze(1).broadcast_to([128, U, 8])

        def first_max_dve(dve, at, k, src, m, t, dst):
            nc.vector.tensor_reduce(rm[:, m, :], src, AX.X, ALU.max).then_inc(sem["r_step"], 1)
            dve.wait_ge(*at("r_step", k + 1))
            nc.vector.tensor_tensor(rt[:, t, :, :], src, b8(rm[:, m, :]), ALU.is_equal).then_inc(sem["r_step"], 1)
            dve.wait_ge(*at("r_step", k + 2))
            nc.vector.tensor_tensor(rt[:, t, :, :], rt[:, t, :, :], rank4, ALU.mult).then_inc(sem["r_step"], 1)
            dve.wait_ge(*at("r_step", k + 3))
            nc.vector.tensor_reduce(rm[:, 5, :], rt[:, t, :, :], AX.X, ALU.max).then_inc(sem["r_step"], 1)
            dve.wait_ge(*at("r_step", k + 4))
            nc.vector.tensor_tensor(dst, rt[:, t, :, :], b8(rm[:, 5, :]), ALU.is_equal).then_inc(sem["r_step"], 1)
            dve.wait_ge(*at("r_step", k + 5))

        def l0_ffn_pe(pe, at, g):
            flip_pe(pe, at, 0, xn, "xn_ready", 0)
            pe.wait_ge(*at("xnT_ready", 1))
            router_pe(pe, at, w("L0f_rw"), row("L0f_rb"))
            experts_pe(pe, at, g, E0, 4,
                       lambda e, b: w("L0f_w1", e * 1024 + 512 + b * 128, e * 1024 + 512 + b * 128 + 128),
                       lambda e, b: w("L0f_w1", e * 1024 + b * 128, e * 1024 + b * 128 + 128),
                       lambda e, b: w("L0f_w2", (e * 4 + b) * 128, (e * 4 + b) * 128 + 128),
                       lambda e: row("L0f_b2", e * 128, e * 128 + 128))

        def l0_ffn_act(act, at, g):
            flip_act(act, at, 0, xnT)
            experts_act(act, at, E0, 4, ACT.Sigmoid, lambda e, b: col("L0f_b1", e * 8 + 4 + b))

        def l0_ffn_dve(dve, at, g):
            norm_in_dve(dve, at, g)
            dve.wait_ge(*at("r_psum", 1))
            first_max_dve(dve, at, 0, logits, 0, 0, gates[:, :, :])
            experts_dve(dve, at, g, E0, 4, lambda e, b: col("L0f_b1", e * 8 + b))

        def norm_only_pool(pool, at, g):
            norm_pool(pool, at, 0)

        def l3_ffn_pe(pe, at, g):
            flip_pe(pe, at, 0, xn, "xn_ready", 0)
            pe.wait_ge(*at("xnT_ready", 1))
            router_pe(pe, at, w("L3f_wg"), None)
            experts_pe(pe, at, g, E3, 2,
                       lambda e, b: w("L3f_w1", (e * 2 + b) * 128, (e * 2 + b) * 128 + 128),
                       lambda e, b: w("L3f_w3", (e * 2 + b) * 128, (e * 2 + b) * 128 + 128),
                       lambda e, b: w("L3f_w2", (e * 2 + b) * 128, (e * 2 + b) * 128 + 128), None)

        def l3_ffn_act(act, at, g):
            flip_act(act, at, 0, xnT)
            act.wait_ge(*at("r_step", 2))
            nc.scalar.activation(rt[:, 1, :, :], rt[:, 0, :, :], ACT.Exp).then_inc(sem["r_exp"], 1)
            experts_act(act, at, E3, 2, ACT.Silu, None)

        def l3_ffn_dve(dve, at, g):
            norm_in_dve(dve, at, g)
            dve.wait_ge(*at("r_psum", 1))
            step = [0]

            def inc(ins):
                step[0] += 1
                ins.then_inc(sem["r_step"], 1)
                dve.wait_ge(*at("r_step", step[0]))

            inc(nc.vector.tensor_reduce(rm[:, 0, :], logits, AX.X, ALU.max))
            inc(nc.vector.tensor_tensor(rt[:, 0, :, :], logits, b8(rm[:, 0, :]), ALU.subtract))
            dve.wait_ge(*at("r_exp", 1))
            first_max_dve(dve, at, 2, rt[:, 1, :, :], 1, 2, rt[:, 3, :, :])
            step[0] = 7
            inc(nc.vector.tensor_scalar(rt[:, 4, :, :], rt[:, 3, :, :], -2.0, None, ALU.mult))
            inc(nc.vector.tensor_tensor(rt[:, 4, :, :], rt[:, 4, :, :], rt[:, 1, :, :], ALU.add))
            first_max_dve(dve, at, 9, rt[:, 4, :, :], 2, 2, rt[:, 5, :, :])
            step[0] = 14
            inc(nc.vector.tensor_tensor(rm[:, 3, :], rm[:, 1, :], rm[:, 2, :], ALU.add))
            nc.vector.reciprocal(rm[:, 4, :], rm[:, 3, :]).then_inc(sem["r_step"], 1)
            dve.wait_ge(*at("r_step", 16))
            inc2 = sem["g_step"]
            nc.vector.tensor_tensor(rt[:, 3, :, :], rt[:, 3, :, :], rt[:, 5, :, :], ALU.add).then_inc(inc2, 1)
            dve.wait_ge(*at("g_step", 1))
            nc.vector.tensor_tensor(rt[:, 3, :, :], rt[:, 3, :, :], rt[:, 1, :, :], ALU.mult).then_inc(inc2, 1)
            dve.wait_ge(*at("g_step", 2))
            nc.vector.tensor_tensor(gates[:, :, :], rt[:, 3, :, :], b8(rm[:, 4, :]), ALU.mult).then_inc(inc2, 1)
            dve.wait_ge(*at("g_step", 3))
            experts_dve(dve, at, g, E3, 2, None)

        def self_qkv_pe(pe, at, pre):
            flip_pe(pe, at, 0, xn, "xn_ready", 0)
            pe.wait_ge(*at("xnT_ready", 1))
            nc.tensor.matmul(psB[:, :], w(pre + "_wq"), xnT[:, :], start=True, stop=True).then_inc(sem["q_psum"], 1)
            nc.tensor.matmul(psS[0][:, 0, :], w(pre + "_wk"), xnT[:, :], start=True,
                             stop=True).then_inc(sem["k_psum"], 1)
            for u in range(U):
                ins = nc.tensor.matmul(psS[1][:, 0, u * 128:(u + 1) * 128], un(xnT, u), w(pre + "_wv"),
                                       start=True, stop=True)
            ins.then_inc(sem["v_psum"], 1)

        def l1_attn_pe(pe, at, g):
            self_qkv_pe(pe, at, "L1a")
            pe.wait_ge(*at("q_ready", 1))
            nc.tensor.matmul(psS[0][:, 1, :], const("rot"), qT[:, :], start=True, stop=True).then_inc(sem["rot_psum"], 1)
            pe.wait_ge(*at("kT_ready", 1))
            nc.tensor.matmul(psS[1][:, 1, :], const("rot"), kTr[:, :], start=True, stop=True).then_inc(sem["rot_psum"], 1)
            pe.wait_ge(*at("rope", 6))
            heads_pe(pe, at, S, qsrc=xmT)
            project_pe(pe, at, w("L1a_wo"), row("L1a_bo"))

        def l1_attn_act(act, at, g):
            flip_act(act, at, 0, xnT)
            act.wait_ge(*at("q_psum", 1))
            nc.scalar.activation(qT[:, :], psB[:, :], ACT.Identity, bias=col("L1a_bq")).then_inc(sem["q_ready"], 1)
            act.wait_ge(*at("k_psum", 1))
            nc.scalar.activation(kTr[:, :], psS[0][:, 0, :], ACT.Identity, bias=col("L1a_bk")).then_inc(sem["kT_ready"], 1)
            values_act(act, at, S, psS[1][:, 0, :])
            heads_act(act, at, S, SCALE8)
            project_act(act, at, col("L1a_bv"))

        def l1_attn_dve(dve, at, g):
            norm_in_dve(dve, at, g)
            cosb = const("cos").unsqueeze(1).broadcast_to([128, U, S])
            sinb = const("sin").unsqueeze(1).broadcast_to([128, U, S])

            def v3(t):
                return t.rearrange("p (u k) -> p u k", u=U)

            def rope(n, src, ready, rot):
                dve.wait_ge(*ready)
                nc.vector.tensor_tensor(v3(rope1[:, n, :]), v3(src), cosb, ALU.mult).then_inc(sem["rope"], 1)
                dve.wait_ge(*at("rot_psum", n + 1))
                nc.vector.tensor_tensor(v3(rope2[:, n, :]), v3(rot), sinb, ALU.mult).then_inc(sem["rope"], 1)
                dve.wait_ge(*at("rope", 3 * n + 2))
                dst = xmT if n == 0 else rope1[:, 1, :]
                nc.vector.tensor_tensor(dst[:, :] if n == 0 else dst, rope1[:, n, :], rope2[:, n, :],
                                        ALU.add).then_inc(sem["rope"], 1)

            rope(0, qT[:, :], at("q_ready", 1), psS[0][:, 1, :])
            rope(1, kTr[:, :], at("kT_ready", 1), psS[1][:, 1, :])
            dve.wait_ge(*at("rope", 6))
            for j in range(4):
                nc.vector.tensor_scalar(kTx[:, :, j, :], v3(rope1[:, 1, :]), heads4[:, j:j + 1], None,
                                        ALU.mult).then_inc(sem["k_ready"], 1)
            heads_dve(dve, at, S)
            residual_dve(dve, at, g)

        def l1_ffn_pe(pe, at, g):
            flip_pe(pe, at, 0, xn, "xn_ready", 0)
            for blk in range(3):
                def wl(i):
                    return wt[:, i * 128:(i + 1) * 128]

                def bl(i):
                    return row("L1f_bias", i * 128, i * 128 + 128)
                rows_pe(pe, at, xnT, wl(2 * blk), bl(2 * blk), at("xnT_ready", 2 * blk + 1), dst=psB)
                flip_pe(pe, at, 0, xm, "xn_ready", U * (blk + 1))
                rows_pe(pe, at, xmT, wl(2 * blk + 1), bl(2 * blk + 1), at("xnT_ready", 2 * blk + 2), dst=psB)
                if blk < 2:
                    pe.wait_ge(*at("h_res", blk + 1))
                    for u in range(U):
                        ins = nc.tensor.transpose(un(psA, u), un(xn, u), ident)
                    ins.then_inc(sem["xnT_psum"], 1)

        def l1_ffn_act(act, at, g):
            flip_act(act, at, 0, xnT)
            for blk in range(3):
                act.wait_ge(*at("xnT_psum", 2 * blk + 2))
                nc.scalar.activation(xmT[:, :], psA[:, :], ACT.Gelu, bias=col("L1f_b", blk),
                                     scale=col("L1f_g", blk)).then_inc(sem["xnT_ready"], 1)
                if blk < 2:
                    flip_act(act, at, 2 * blk + 2, xnT)

        def l1_ffn_dve(dve, at, g):
            norm_in_dve(dve, at, g)
            for blk in range(3):
                norm_dve(dve, at, blk + 1, lambda u: un(psB, u), lambda u: un(xm, u),
                         after=lambda u: at("y_psum", 2 * blk + 1))
                dve.wait_ge(*at("y_psum", 2 * blk + 2))
                nc.vector.tensor_tensor(xn[:, :], xn[:, :], psB[:, :], ALU.add).then_inc(sem["h_res"], 1)
                dve.wait_ge(*at("h_res", blk + 1))
            nc.vector.tensor_tensor(x[:, bass.ts(g, GT)], xg[:, :], xn[:, :], ALU.add).then_inc(sem["x_done"], 1)

        def l1_ffn_pool(pool, at, g):
            for r in range(4):
                norm_pool(pool, at, r)

        def l2_attn_pe(pe, at, g):
            self_qkv_pe(pe, at, "L2a")
            for u in range(U):
                ins = nc.tensor.matmul(psT[:, 0, u * NSAMP:(u + 1) * NSAMP], un(xn, u), onehot[:, :],
                                       start=True, stop=True)
            ins.then_inc(sem["smp_psum"], 1)
            pe.wait_ge(*at("smp_ready", 1))
            nc.tensor.matmul(psT[:, 1, 0:U * NSAMP], w("L2a_wk"), xsT[:, :], start=True,
                             stop=True).then_inc(sem["smp_psum"], 1)
            pe.wait_ge(*at("smp_ready", 5))
            pe.wait_ge(*at("q_ready", 1))
            pe.wait_ge(*at("k_ready", 4))
            pe.wait_ge(*at("v_ready", 1))
            for u in range(U):
                if u >= 1:
                    pe.wait_ge(*at("smp_red", 4 * u))
                for gq in range(4):
                    rs = slice(32 * gq, 32 * gq + 32)
                    ins = nc.tensor.matmul(psS[gq // 2][:, gq % 2, 0:4 * NSAMP], qT[rs, u * S:(u + 1) * S],
                                           ksx[rs, u, :, :], start=True, stop=True)
                ins.then_inc(sem["smps_psum"], 1)
            pe.wait_ge(*at("m_step", 1))
            met_pe(pe)
            nc.tensor.transpose(psT[0:U * H, 0, 0:S], red[:, 2, :], ident).then_inc(sem["mT_psum"], 1)
            for u in range(U):
                ins = nc.tensor.matmul(psB[:, u * 128:(u + 1) * 128], mean_w[:, :],
                                       vx[:, u, :, 0:DH], start=True, stop=True)
            ins.then_inc(sem["vm_psum"], 1)
            pe.wait_ge(*at("top", 9))
            met_pe(pe)
            nc.tensor.transpose(psT[:, 1, 0:U * H], cand[:, 4, :], ident[0:U * H, 0:U * H]).then_inc(sem["sel_psum"], 1)
            pe.wait_ge(*at("sel_ready", 2))
            pe.wait_ge(*at("vm_ready", 1))
            heads_pe(pe, at, S)
            project_pe(pe, at, w("L2a_wo"), row("L2a_bo"))

        def l2_attn_act(act, at, g):
            flip_act(act, at, 0, xnT)
            act.wait_ge(*at("q_psum", 1))
            nc.scalar.activation(qT[:, :], psB[:, :], ACT.Identity, bias=col("L2a_bq")).then_inc(sem["q_ready"], 1)
            values_act(act, at, S, psS[1][:, 0, :])
            act.wait_ge(*at("smp_psum", 1))
            nc.scalar.copy(xsT[:, :], psT[:, 0, 0:U * NSAMP]).then_inc(sem["smp_ready"], 1)
            heads_act(act, at, S, SCALE8)
            project_act(act, at, col("L2a_bv"))

        def l2_attn_dve(dve, at, g):
            norm_in_dve(dve, at, g)
            expand_keys_dve(dve, at, S, psS[0][:, 0, :], col("L2a_bk"), at("k_psum", 1))
            dve.wait_ge(*at("smp_ready", 1))
            dve.wait_ge(*at("smp_psum", 2))
            for j in range(4):
                nc.vector.tensor_scalar(ksx[:, :, j, :], psT[:, 1, 0:U * NSAMP].rearrange("p (u k) -> p u k", u=U),
                                        col("L2a_bk"), heads4[:, j:j + 1], ALU.add,
                                        ALU.mult).then_inc(sem["smp_ready"], 1)
            for u in range(U):
                dve.wait_ge(*at("smps_psum", u + 1))
                for n, op in ((0, ALU.max), (1, ALU.add)):
                    for half in range(2):
                        c = u * H + half * 8
                        nc.vector.tensor_reduce(red[:, n, c:c + 8].rearrange("p (b j) -> p b j", b=2),
                                                s_view(half, NSAMP), AX.X, op).then_inc(sem["smp_red"], 1)
            dve.wait_ge(*at("smp_red", 16))
            nc.vector.scalar_tensor_tensor(out=red[:, 2, :], in0=red[:, 1, :], scalar=-1.0 / NSAMP,
                                           in1=red[:, 0, :], op0=ALU.mult, op1=ALU.add).then_inc(sem["m_step"], 1)
            dve.wait_ge(*at("mT_psum", 1))
            nc.vector.tensor_copy(cand[:, 0, :], psT[0:U * H, 0, 0:S]).then_inc(sem["top"], 1)
            dve.wait_ge(*at("top", 1))
            for r in range(3):
                met_dve(dve)
                nc.vector.max(top8[:, r, :], cand[:, r, :]).then_inc(sem["top"], 1)
                dve.wait_ge(*at("top", 2 + 2 * r))
                met_dve(dve)
                nc.vector.match_replace(cand[:, r + 1, :], top8[:, r, :], cand[:, r, :], GONE).then_inc(sem["top"], 1)
                dve.wait_ge(*at("top", 3 + 2 * r))
            met_dve(dve)
            nc.vector.max(top8[:, 3, :], cand[:, 3, :]).then_inc(sem["m_step"], 1)
            dve.wait_ge(*at("m_step", 2))
            nc.vector.memset(top8[:, 3, 1:8], GONE).then_inc(sem["m_step"], 1)
            dve.wait_ge(*at("m_step", 3))
            met_dve(dve)
            nc.vector.match_replace(cand[:, 4, :], top8[:, 3, :], cand[:, 3, :], GONE).then_inc(sem["top"], 1)
            dve.wait_ge(*at("top", 8))
            nc.vector.tensor_scalar(cand[:, 4, :], cand[:, 4, :], GONE, None, ALU.is_equal).then_inc(sem["top"], 1)
            dve.wait_ge(*at("sel_psum", 1))
            nc.vector.tensor_copy(sel[:, 0, :], psT[:, 1, 0:U * H]).then_inc(sem["sel_ready"], 1)
            nc.vector.tensor_scalar(sel[:, 1, :], psT[:, 1, 0:U * H], -1.0, 1.0, ALU.mult,
                                    ALU.add).then_inc(sem["sel_ready"], 1)
            dve.wait_ge(*at("sel_ready", 2))
            dve.wait_ge(*at("vm_psum", 1))
            nc.vector.tensor_tensor(vmean[:, :].rearrange("p (n e) -> p n e", e=DH),
                                    psB[:, :].rearrange("p (n e) -> p n e", e=DH),
                                    sel[:, 1, :].unsqueeze(2).broadcast_to([128, U * H, DH]),
                                    ALU.mult).then_inc(sem["vm_ready"], 1)

            def mix(u, dv, o, rb):
                nc.vector.tensor_tensor(rec[:, u % 2, :], rec[:, u % 2, :], sel[:, 0, u * H:(u + 1) * H],
                                        ALU.mult).then_inc(sem["o_mix"], 1)
                dve.wait_ge(*at("o_mix", 2 * u + 1))
                nc.vector.tensor_tensor(dv, o, rb, ALU.mult).then_inc(sem["o_mix"], 1)
                dve.wait_ge(*at("o_mix", 2 * u + 2))
                nc.vector.tensor_tensor(un(on, u), un(on, u), un(vmean, u), ALU.add).then_inc(sem["o_ready"], 1)

            heads_dve(dve, at, S, dst=mix)
            residual_dve(dve, at, g)

        def l2_xattn_pe(pe, at, g):
            pe.wait_ge(*at("ctx_ready", 1))
            for b in range(8):
                if b >= 2:
                    pe.wait_ge(*at("k_ready", b - 1))
                nc.tensor.matmul(psS[0][:, b % 2, 0:U * SC], w("L2x_wkv", b * 128, b * 128 + 128), ctxg[:, :],
                                 start=True, stop=True).then_inc(sem["k_psum"], 1)
            for n in range(8):
                u, c = divmod(n, 2)
                if n >= 2:
                    pe.wait_ge(*at("v_ready", n - 1))
                nc.tensor.matmul(psS[1][0:SC, c, :], ctxg[:, u * SC:(u + 1) * SC],
                                 w("L2x_wkv", 1024 + c * 512, 1024 + c * 512 + 512), start=True,
                                 stop=True).then_inc(sem["v_psum"], 1)
            flip_pe(pe, at, 0, xm, "xn_ready", U)
            pe.wait_ge(*at("xnT_ready", 1))
            for b in range(8):
                if b >= 2:
                    pe.wait_ge(*at("q_ready", b - 1))
                nc.tensor.matmul(psT[:, b % 2, :], w("L2x_wq", b * 128, b * 128 + 128), xmT[:, :],
                                 start=True, stop=True).then_inc(sem["q_psum"], 1)
            pe.wait_ge(*at("q_ready", 8))
            pe.wait_ge(*at("k_ready", 8))
            pe.wait_ge(*at("v_ready", 8))
            n = 4 * U

            def score(i):
                u, quarter = divmod(i, 4)
                if i >= 2:
                    pe.wait_ge(*at("s_sub", i - 1))
                for j in range(4):
                    h = quarter * 4 + j
                    rs = slice(64 * (h % 2), 64 * (h % 2) + 64)
                    ins = nc.tensor.matmul(psS[i % 2][:, h % 2, (j // 2) * SC:(j // 2 + 1) * SC],
                                           qT8[rs, h // 2, u * S:(u + 1) * S],
                                           kT8[rs, h // 2, u * SC:(u + 1) * SC], start=True, stop=True)
                ins.then_inc(sem["s_psum"], 1)

            def turn(i):
                pe.wait_ge(*at("s_nrm", i + 1))
                if i >= 2:
                    pe.wait_ge(*at("pt_ready", i - 1))
                for j in range(4):
                    ins = nc.tensor.transpose(psT[0:SC, i % 2, j * S:(j + 1) * S],
                                              p[:, i % 2, j * SC:(j + 1) * SC], ident)
                ins.then_inc(sem["pt_psum"], 1)

            def value(i):
                u, quarter = divmod(i, 4)
                pe.wait_ge(*at("pt_ready", i + 1))
                if i >= 1:
                    pe.wait_ge(*at("oT_ready", i))
                for j in range(4):
                    h = quarter * 4 + 2 * (j % 2) + j // 2
                    c0 = (j % 2) * S
                    ins = nc.tensor.matmul(psB[64 * (h % 2):64 * (h % 2) + 64, c0:c0 + S],
                                           v8[0:SC, u, h * DX:(h + 1) * DX], pT[0:SC, i % 2, j, :],
                                           start=True, stop=True)
                ins.then_inc(sem["o_psum"], 1)

            def out(u):
                pe.wait_ge(*at("oT_ready", 4 * u + 4))
                for b in range(8):
                    nc.tensor.matmul(un(psA, u), fT[:, u % 2, :, :].rearrange("p a t -> p (a t)")[:, b * S:(b + 1) * S],
                                     w("L2x_wo", b * 128, b * 128 + 128), start=(b == 0), stop=False)
                return nc.tensor.matmul(un(psA, u), ones_row, row("L2x_bo"), start=False, stop=True)

            for t in range(n + 2):
                if t < n:
                    score(t)
                if 1 <= t <= n:
                    turn(t - 1)
                if t >= 2:
                    value(t - 2)
                if t >= 6 and t % 4 == 2:
                    last = out((t - 6) // 4)
            last = out(U - 1)
            last.then_inc(sem["y_psum"], 1)

        def l2_xattn_act(act, at, g):
            for b in range(8):
                act.wait_ge(*at("k_psum", b + 1))
                nc.scalar.copy(kT8[:, b, :], psS[0][:, b % 2, 0:U * SC]).then_inc(sem["k_ready"], 1)
            for n in range(8):
                u, c = divmod(n, 2)
                act.wait_ge(*at("v_psum", n + 1))
                nc.scalar.copy(v8[0:SC, u, c * 512:(c + 1) * 512], psS[1][0:SC, c, :]).then_inc(sem["v_ready"], 1)
            act.wait_ge(*at("xnT_psum", 1))
            nc.scalar.activation(xmT[:, :], psA[:, :], ACT.Identity, bias=col("L2x_b"),
                                 scale=col("L2x_g")).then_inc(sem["xnT_ready"], 1)
            for b in range(8):
                act.wait_ge(*at("q_psum", b + 1))
                nc.scalar.mul(qT8[:, b, :], psT[:, b % 2, :], float(DX) ** -0.5).then_inc(sem["q_ready"], 1)
            n = 4 * U
            for t in range(n + 2):
                if t < n:
                    act.wait_ge(*at("s_sub", t + 1))
                    pv = p[:, t % 2, 0:4 * SC]
                    nc.scalar.activation(pv, pv, ACT.Exp).then_inc(sem["p_ready"], 1)
                if 1 <= t <= n:
                    i = t - 1
                    act.wait_ge(*at("pt_psum", i + 1))
                    if i >= 2:
                        act.wait_ge(*at("o_psum", i - 1))
                    nc.scalar.copy(pT[0:SC, i % 2, 0:4, :].rearrange("p j s -> p (j s)"),
                                   psT[0:SC, i % 2, :]).then_inc(sem["pt_ready"], 1)
                if t >= 2:
                    i = t - 2
                    u, quarter = divmod(i, 4)
                    act.wait_ge(*at("o_psum", i + 1))
                    dst = fT[:, u % 2, :, :].rearrange("p a t -> p (a t)")[:, quarter * 256:(quarter + 1) * 256]
                    nc.scalar.copy(dst, psB[:, 0:256]).then_inc(sem["oT_ready"], 1)

        def l2_xattn_dve(dve, at, g):
            norm_in_dve(dve, at, g)
            norm_dve(dve, at, 1, lambda u: un(xn, u), lambda u: un(xm, u), after=lambda u: at("xn_ready", u + 1))
            n = 4 * U

            def softmax(i):
                k = i % 2
                sv = psS[k][:, :, 0:2 * SC].rearrange("p b (j k) -> p b j k", j=2)
                mx = smx[:, k, 0:4].rearrange("p (b j) -> p b j", b=2)
                pv = p[:, k, 0:4 * SC].rearrange("p (b j k) -> p b j k", b=2, j=2)
                dve.wait_ge(*at("s_psum", i + 1))
                nc.vector.tensor_reduce(mx, sv, AX.X, ALU.max).then_inc(sem["s_max"], 1)
                dve.wait_ge(*at("s_max", i + 1))
                if i >= 2:
                    dve.wait_ge(*at("pt_psum", i - 1))
                nc.vector.tensor_tensor(pv, sv, mx.unsqueeze(3).broadcast_to([128, 2, 2, SC]),
                                        ALU.subtract).then_inc(sem["s_sub"], 1)

            def normalise(i):
                k = i % 2
                pv = p[:, k, 0:4 * SC].rearrange("p (j k) -> p j k", j=4)
                dve.wait_ge(*at("p_ready", i + 1))
                nc.vector.tensor_reduce(rec[:, k, 0:4], pv, AX.X, ALU.add).then_inc(sem["s_sum"], 1)
                dve.wait_ge(*at("s_sum", i + 1))
                nc.vector.reciprocal(rec[:, k, 4:8], rec[:, k, 0:4]).then_inc(sem["s_rec"], 1)
                dve.wait_ge(*at("s_rec", i + 1))
                nc.vector.tensor_tensor(pv, pv, rec[:, k, 4:8].unsqueeze(2).broadcast_to([128, 4, SC]),
                                        ALU.mult).then_inc(sem["s_nrm"], 1)

            for t in range(n + 1):
                if t < n:
                    softmax(t)
                if t >= 1:
                    normalise(t - 1)
            dve.wait_ge(*at("y_psum", 1))
            nc.vector.scalar_tensor_tensor(out=x[:, bass.ts(g, GT)], in0=psA[:, :], scalar=gate[:, 1:2],
                                           in1=xg[:, :], op0=ALU.mult, op1=ALU.add).then_inc(sem["x_done"], 1)

        def l2_xattn_pool(pool, at, g):
            ctx_pool(pool, at, g)
            norm_pool(pool, at, 0)
            norm_pool(pool, at, 1)

        def l2_ffn_pe(pe, at, g):
            flip_pe(pe, at, 0, xn, "xn_ready", 0)
            pe.wait_ge(*at("xnT_ready", 1))
            nc.tensor.matmul(psB[0:32, :], w("L2f_u1"), xnT[:, :], start=True, stop=True).then_inc(sem["q_psum"], 1)
            pe.wait_ge(*at("q_ready", 1))
            for b in range(4):
                nc.tensor.matmul(psS[b // 2][:, b % 2, :], w("L2f_v1", b * 128, b * 128 + 128)[0:32, :], qT[0:32, :],
                                 start=True, stop=True).then_inc(sem["f_psum"], 1)
            for b in range(4):
                pe.wait_ge(*at("f_ready", b + 1))
                ins = nc.tensor.matmul(psB[0:32, :], w("L2f_u2", b * 32, b * 32 + 32), fT[:, 0, b, :],
                                       start=(b == 0), stop=(b == 3))
            ins.then_inc(sem["o_psum"], 1)
            pe.wait_ge(*at("oT_ready", 1))
            for u in range(U):
                nc.tensor.matmul(un(psA, u), oT[0:32, u * S:(u + 1) * S], w("L2f_v2")[0:32, :], start=True, stop=False)
                ins = nc.tensor.matmul(un(psA, u), ones_row, row("L2f_b2"), start=False, stop=True)
            ins.then_inc(sem["y_psum"], 1)

        def l2_ffn_act(act, at, g):
            flip_act(act, at, 0, xnT)
            act.wait_ge(*at("q_psum", 1))
            nc.scalar.copy(qT[0:32, :], psB[0:32, :]).then_inc(sem["q_ready"], 1)
            for b in range(4):
                act.wait_ge(*at("f_psum", b + 1))
                nc.scalar.activation(fT[:, 0, b, :], psS[b // 2][:, b % 2, :], ACT.Gelu_apprx_tanh,
                                     bias=col("L2f_b1", b)).then_inc(sem["f_ready"], 1)
            act.wait_ge(*at("o_psum", 1))
            nc.scalar.copy(oT[0:32, :], psB[0:32, :]).then_inc(sem["oT_ready"], 1)

        def simple_dve(dve, at, g):
            norm_in_dve(dve, at, g)
            residual_dve(dve, at, g)

        def l3_attn_pe(pe, at, g):
            flip_pe(pe, at, 0, xn, "xn_ready", 0)
            pe.wait_ge(*at("xnT_ready", 1))
            nc.tensor.matmul(psB[:, :], w("L3a_wqkv", 0, 128), xnT[:, :], start=True, stop=True).then_inc(sem["q_psum"], 1)
            for half in range(2):
                for u in (2 * half, 2 * half + 1):
                    ins = nc.tensor.matmul(psS[half][:, 0, (u % 2) * 256:(u % 2) * 256 + 256], un(xnT, u),
                                           w("L3a_wqkv", 128, 384), start=True, stop=True)
                ins.then_inc(sem["k_psum"], 1)
            for u in range(U):
                pe.wait_ge(*at("k_ready", u // 2 + 1))
                pe.wait_ge(*at("v_ready", u // 2 + 1))
                if u >= 2:
                    pe.wait_ge(*at("kv_ready", 2 * u - 2))
                nc.tensor.matmul(psT[:, u % 2, 0:D], fT[:, 0, u // 2, (u % 2) * 256:(u % 2) * 256 + 128],
                                 fT[:, 0, u // 2, (u % 2) * 256 + 128:(u % 2) * 256 + 256],
                                 start=True, stop=True)
                nc.tensor.matmul(psT[:, u % 2, D:D + 2], fT[:, 0, u // 2, (u % 2) * 256:(u % 2) * 256 + 128],
                                 ones[:, 0:2], start=True, stop=True).then_inc(sem["s_psum"], 1)
            pe.wait_ge(*at("q_ready", 1))
            for u in range(U):
                pe.wait_ge(*at("kv_ready", 2 * u + 2))
                nc.tensor.matmul(psS[u // 2][:, 1, (u % 2) * 256:(u % 2) * 256 + D + H], un(qT, u),
                                 kvm[:, u % 2, :], start=True, stop=True).then_inc(sem["o_psum"], 1)
            project_pe(pe, at, w("L3a_wo"), None)

        def l3_attn_act(act, at, g):
            flip_act(act, at, 0, xnT)
            act.wait_ge(*at("elu_min", 1))
            nc.scalar.activation(rope1[:, 0, :], rope1[:, 0, :], ACT.Exp).then_inc(sem["elu_exp"], 1)
            for half in range(2):
                act.wait_ge(*at("elu_min", half + 2))
                dst = fT[:, 0, half, :].rearrange("p (u n) -> p u n", u=2)[:, :, 128:256]
                src = psS[half][:, 0, :].rearrange("p (u n) -> p u n", u=2)[:, :, 128:256]
                nc.scalar.copy(dst, src).then_inc(sem["v_ready"], 1)
                k = rope2[:, half, 0:256]
                nc.scalar.activation(k, k, ACT.Exp).then_inc(sem["elu_exp"], 1)
            project_act(act, at, None)

        def l3_attn_dve(dve, at, g):
            norm_in_dve(dve, at, g)
            dve.wait_ge(*at("q_psum", 1))
            nc.vector.tensor_scalar(rope1[:, 0, :], psB[:, :], 0.0, None, ALU.min).then_inc(sem["elu_min"], 1)
            for half in range(2):
                dve.wait_ge(*at("k_psum", half + 1))
                src = psS[half][:, 0, :].rearrange("p (u n) -> p u n", u=2)[:, :, 0:128]
                nc.vector.tensor_scalar(rope2[:, half, 0:256].rearrange("p (u n) -> p u n", u=2), src, 0.0, None,
                                        ALU.min).then_inc(sem["elu_min"], 1)
            dve.wait_ge(*at("elu_exp", 1))
            nc.vector.scalar_tensor_tensor(out=qT[:, :], in0=psB[:, :], scalar=0.0, in1=rope1[:, 0, :],
                                           op0=ALU.max, op1=ALU.add).then_inc(sem["q_ready"], 1)
            for half in range(2):
                dve.wait_ge(*at("v_ready", half + 1))
                dve.wait_ge(*at("elu_exp", half + 2))
                src = psS[half][:, 0, :].rearrange("p (u n) -> p u n", u=2)[:, :, 0:128]
                dst = fT[:, 0, half, :].rearrange("p (u n) -> p u n", u=2)[:, :, 0:128]
                nc.vector.scalar_tensor_tensor(out=dst, in0=src, scalar=0.0,
                                               in1=rope2[:, half, 0:256].rearrange("p (u n) -> p u n", u=2),
                                               op0=ALU.max, op1=ALU.add).then_inc(sem["k_ready"], 1)
            for u in range(U):
                dve.wait_ge(*at("s_psum", u + 1))
                if u >= 2:
                    dve.wait_ge(*at("o_psum", u - 1))
                nc.vector.tensor_tensor(kvm[:, u % 2, 0:D], psT[:, u % 2, 0:D], bdiag, ALU.mult).then_inc(sem["kv_ready"], 1)
                nc.vector.tensor_scalar(kvm[:, u % 2, D:D + H], bdiag16, psT[:, u % 2, D:D + 1], None,
                                        ALU.mult).then_inc(sem["kv_ready"], 1)
            for u in range(U):
                dve.wait_ge(*at("o_psum", 2 * (u // 2) + 2))
                o = psS[u // 2][:, 1, (u % 2) * 256:(u % 2) * 256 + D + H]
                nc.vector.tensor_scalar(rec[:, u % 2, :], o[:, D:D + H], 1e-6, None, ALU.max).then_inc(sem["o_recip"], 1)
                dve.wait_ge(*at("o_recip", 2 * u + 1))
                nc.vector.reciprocal(rec[:, u % 2, :], rec[:, u % 2, :]).then_inc(sem["o_recip"], 1)
                dve.wait_ge(*at("o_recip", 2 * u + 2))
                nc.vector.tensor_tensor(un(on, u).rearrange("p (h e) -> p h e", h=H),
                                        o[:, 0:D].rearrange("p (h e) -> p h e", h=H),
                                        rec[:, u % 2, :].unsqueeze(2).broadcast_to([128, H, DH]),
                                        ALU.mult).then_inc(sem["o_ready"], 1)
            residual_dve(dve, at, g)

        def l3_xattn_pe(pe, at, g):
            pe.wait_ge(*at("ctx_ready", 1))
            nc.tensor.matmul(psS[0][:, 0, 0:U * SC], w("L3x_wk"), ctxg[:, :], start=True,
                             stop=True).then_inc(sem["k_psum"], 1)
            for u in range(U):
                ins = nc.tensor.matmul(psS[1][0:SC, 0, u * 128:(u + 1) * 128], ctxg[:, u * SC:(u + 1) * SC],
                                       w("L3x_wv"), start=True, stop=True)
            ins.then_inc(sem["v_psum"], 1)
            flip_pe(pe, at, 0, xn, "xn_ready", 0)
            pe.wait_ge(*at("xnT_ready", 1))
            nc.tensor.matmul(psB[:, :], w("L3x_wq"), xnT[:, :], start=True, stop=True).then_inc(sem["q_psum"], 1)
            pe.wait_ge(*at("q_ready", 1))
            pe.wait_ge(*at("k_ready", 1))
            for u in range(U):
                ins = nc.tensor.matmul(psS[0][:, 1, u * SC:(u + 1) * SC], un(qT, u), kTr[:, u * SC:(u + 1) * SC],
                                       start=True, stop=True)
            ins.then_inc(sem["s_psum"], 1)
            pe.wait_ge(*at("s_nrm", 1))
            for u in range(U):
                ins = nc.tensor.transpose(psT[0:SC, 0, u * S:(u + 1) * S], p[:, 0, u * SC:(u + 1) * SC], ident)
            ins.then_inc(sem["pt_psum"], 1)
            pe.wait_ge(*at("pt_ready", 1))
            pe.wait_ge(*at("v_ready", 1))
            for u in range(U):
                ins = nc.tensor.matmul(un(psB, u), xm[0:SC, u * 128:(u + 1) * 128], pT[0:SC, 0, u, :],
                                       start=True, stop=True)
            ins.then_inc(sem["oT_psum"], 1)
            rows_pe(pe, at, oT, w("L3x_wo"), row("L3x_bo"), at("oT_ready", 1))

        def l3_xattn_act(act, at, g):
            act.wait_ge(*at("k_psum", 1))
            nc.scalar.copy(kTr[:, 0:U * SC], psS[0][:, 0, 0:U * SC]).then_inc(sem["k_ready"], 1)
            act.wait_ge(*at("v_psum", 1))
            nc.scalar.copy(xm[0:SC, :], psS[1][0:SC, 0, :]).then_inc(sem["v_ready"], 1)
            flip_act(act, at, 0, xnT)
            act.wait_ge(*at("q_psum", 1))
            nc.scalar.activation(qT[:, :], psB[:, :], ACT.Identity, bias=col("L3x_bq")).then_inc(sem["q_ready"], 1)
            act.wait_ge(*at("s_sub", 1))
            nc.scalar.activation(p[:, 0, 0:U * SC], p[:, 0, 0:U * SC], ACT.Exp,
                                 scale=float(np.float32(1.0) / np.sqrt(np.float32(D)))).then_inc(sem["p_ready"], 1)
            act.wait_ge(*at("pt_psum", 1))
            nc.scalar.copy(pT[0:SC, 0, 0:4, :].rearrange("p j s -> p (j s)"), psT[0:SC, 0, :]).then_inc(sem["pt_ready"], 1)
            project_act(act, at, col("L3x_bv"))

        def l3_xattn_dve(dve, at, g):
            norm_in_dve(dve, at, g)
            sv = psS[0][:, 1, 0:U * SC].rearrange("p (u k) -> p u k", u=U)
            pv = p[:, 0, 0:U * SC].rearrange("p (u k) -> p u k", u=U)
            dve.wait_ge(*at("s_psum", 1))
            nc.vector.tensor_reduce(smx[:, 0, 0:U], sv, AX.X, ALU.max).then_inc(sem["s_max"], 1)
            dve.wait_ge(*at("s_max", 1))
            nc.vector.tensor_tensor(pv, sv, smx[:, 0, 0:U].unsqueeze(2).broadcast_to([128, U, SC]),
                                    ALU.subtract).then_inc(sem["s_sub"], 1)
            dve.wait_ge(*at("p_ready", 1))
            nc.vector.tensor_reduce(rec[:, 0, 0:U], pv, AX.X, ALU.add).then_inc(sem["s_sum"], 1)
            dve.wait_ge(*at("s_sum", 1))
            nc.vector.reciprocal(rec[:, 0, 4:8], rec[:, 0, 0:4]).then_inc(sem["s_rec"], 1)
            dve.wait_ge(*at("s_rec", 1))
            nc.vector.tensor_tensor(pv, pv, rec[:, 0, 4:8].unsqueeze(2).broadcast_to([128, U, SC]),
                                    ALU.mult).then_inc(sem["s_nrm"], 1)
            residual_dve(dve, at, g)

        PROGRAM = {
            "L0_attn": (l0_attn_pe, l0_attn_act, l0_attn_dve, l0_attn_pool),
            "L0_xattn": (lambda pe, at, g: cross_pe(pe, at, g, "L0x", w("L0x_wo"), row("L0x_bo")),
                         lambda a, at, g: cross_act(a, at, g, "L0x", 1.0, q_on_act=False), l0_xattn_dve, cross_pool),
            "L0_ffn": (l0_ffn_pe, l0_ffn_act, l0_ffn_dve, norm_only_pool),
            "L1_attn": (l1_attn_pe, l1_attn_act, l1_attn_dve, norm_only_pool),
            "L1_xattn": (lambda pe, at, g: cross_pe(pe, at, g, "L1x", w("L1x_wo"), row("L1x_bo")),
                         lambda a, at, g: cross_act(a, at, g, "L1x", SCALE8), l1_xattn_dve, cross_pool),
            "L1_ffn": (l1_ffn_pe, l1_ffn_act, l1_ffn_dve, l1_ffn_pool),
            "L2_attn": (l2_attn_pe, l2_attn_act, l2_attn_dve, norm_only_pool),
            "L2_xattn": (l2_xattn_pe, l2_xattn_act, l2_xattn_dve, l2_xattn_pool),
            "L2_ffn": (l2_ffn_pe, l2_ffn_act, simple_dve, norm_only_pool),
            "L3_attn": (l3_attn_pe, l3_attn_act, l3_attn_dve, norm_only_pool),
            "L3_xattn": (l3_xattn_pe, l3_xattn_act, l3_xattn_dve, cross_pool),
            "L3_ffn": (l3_ffn_pe, l3_ffn_act, l3_ffn_dve, norm_only_pool),
        }

        @block.tensor
        def _(pe):
            pe.wait_ge(small_in, 16 * 12)
            pe.wait_ge(loaded["L1_ffn"], 16)
            pe.wait_ge(setup_v, 1)
            for i in range(6):
                bank = psS[i // 4][:, 0, (i % 4) * 128:(i % 4) * 128 + 128]
                ins = nc.tensor.matmul(bank, w("L1f_la", i * 128, i * 128 + 128)[0:32, :],
                                       w("L1f_lb", i * 128, i * 128 + 128)[0:32, :], start=True, stop=True)
            ins.then_inc(lora_psum, 1)
            for b in BLOCKS:
                pe.wait_ge(loaded[b], 16)
                with pe.Fori(0, NG) as g:
                    PROGRAM[b][0](pe, Counts(b, g), g)

        @block.scalar
        def _(act):
            act.wait_ge(small_in, 16 * 12)
            nc.scalar.activation(gate[:, 1:2], gate[:, 0:1], ACT.Tanh).then_inc(setup_a, 1)
            act.wait_ge(setup_v, 1)
            for b in BLOCKS:
                with act.Fori(0, NG) as g:
                    PROGRAM[b][1](act, Counts(b, g), g)

        @block.gpsimd
        def _(pool):
            nc.gpsimd.memset(neghalf[:, :], -0.5).then_inc(setup_g, 1)
            pool.wait_ge(setup_g, 1)
            pool.wait_ge(small_in, 16 * 12)
            for b in BLOCKS:
                with pool.Fori(0, NG) as g:
                    PROGRAM[b][3](pool, Counts(b, g), g)

        @block.vector
        def _(dve):
            nc.vector.memset(ones[:, :], 1.0)
            nc.vector.memset(mean_w[:, :], 1.0 / S)
            dve.wait_ge(small_in, 16 * 12)
            nc.vector.tensor_copy(window_bf[:, :], const("window"))
            nc.vector.tensor_copy(ident_bf[:, :], ident)
            nc.vector.memset(vx[:, :, :, :], 1.0).then_inc(setup_v, 1)
            nc.vector.tensor_scalar(cmask[:, :], pad_u8, -3.0e38, 4.0, ALU.mult, ALU.mult).then_inc(setup_v, 1)
            dve.wait_ge(setup_v, 2)
            nc.vector.tensor_tensor(cmask[:, :].rearrange("p (b k) -> p b k", b=NB),
                                    cmask[:, :].rearrange("p (b k) -> p b k", b=NB),
                                    amask[:, :].unsqueeze(1).broadcast_to([128, NB, SC]),
                                    ALU.add).then_inc(setup_v, 1)
            nc.vector.tensor_copy(idx_f[:, 0, :], idx_i[:, :]).then_inc(setup_v, 1)
            dve.wait_ge(setup_v, 4)
            nc.vector.tensor_scalar(idx_f[:, 1, :], idx_f[:, 0, :], 0.0, float(S), ALU.is_lt,
                                    ALU.mult).then_inc(setup_v, 1)
            dve.wait_ge(setup_v, 5)
            nc.vector.tensor_tensor(idx_f[:, 0, :], idx_f[:, 0, :], idx_f[:, 1, :], ALU.add).then_inc(setup_v, 1)
            dve.wait_ge(setup_v, 6)
            nc.vector.tensor_scalar(idx_f[:, 1, :], idx_f[:, 0, :], 0.0, float(S - 1), ALU.max,
                                    ALU.min).then_inc(setup_v, 1)
            dve.wait_ge(setup_v, 7)
            nc.vector.tensor_scalar(onehot[:, :], idx_f[:, 1, :], part, None, ALU.is_equal).then_inc(setup_v, 1)
            nc.vector.tensor_scalar(wt[:, :], qw, 1.0 / 7.5, -1.0, ALU.mult, ALU.add).then_inc(setup_v, 1)
            dve.wait_ge(setup_v, 9)
            nc.vector.tensor_tensor(wt[:, :], wt[:, :], scl, ALU.mult).then_inc(setup_v, 1)
            dve.wait_ge(setup_v, 10)
            dve.wait_ge(lora_psum, 1)
            nc.vector.tensor_tensor(wt[:, 0:512], wt[:, 0:512], psS[0][:, 0, :], ALU.add)
            nc.vector.tensor_tensor(wt[:, 512:768], wt[:, 512:768], psS[1][:, 0, 0:256], ALU.add).then_inc(setup_v, 1)
            dve.wait_ge(setup_v, 11)
            dve.wait_ge(setup_a, 1)
            dve.wait_ge(x_in, 16)
            dve.sem_inc(sem["x_done"], 1)
            for b in BLOCKS:
                with dve.Fori(0, NG) as g:
                    PROGRAM[b][2](dve, Counts(b, g), g)


def block_cols(wm, n):
    k, c = wm.shape
    return wm.reshape(n, k // n, c).transpose(1, 0, 2).reshape(k // n, n * c)


def pad_rows(a):
    return np.concatenate([a, np.zeros((128 - a.shape[0], a.shape[1]), a.dtype)], axis=0)


def shape_constants():
    i = np.arange(128)
    rot = np.zeros((128, 128), np.float32)
    cos = np.ones((128, S), np.float32)
    sin = np.zeros((128, S), np.float32)
    tok = np.arange(S)
    for c in range(128):
        e = c % DH
        if e < 6:
            pos = [np.zeros(S), tok // 16, tok % 16][e // 2].astype(np.float32)
            cos[c], sin[c] = np.cos(pos), np.sin(pos)
            if e % 2 == 0:
                rot[c + 1, c] = -1.0
            else:
                rot[c - 1, c] = 1.0
    parts = dict(
        ident=np.eye(128), bdiag=(i[:, None] // DH == i[None, :] // DH),
        bdiag16=(i[:, None] // DH == np.arange(H)[None, :]), heads4=((i[:, None] // DH) % 4 == np.arange(4)[None, :]),
        rot=rot, cos=cos, sin=sin, window=np.where(np.abs(i[:, None] - i[None, :]) <= WINDOW, 0.0, -1e9),
        rank=np.broadcast_to(8.0 - np.arange(8), (128, 8)), part=i[:, None])
    return np.concatenate([np.asarray(parts[n], np.float32) for n, _ in CONSTS], axis=1)


def lay_out(v):
    wp = {
        "L0a_w1": v["L0_attn_W1"], "L0a_w2": block_cols(v["L0_attn_W2"], 4),
        "L0x_wq": v["L0_xattn_Wq"].T, "L0x_wk": v["L0_xattn_Wk"].T, "L0x_wv": v["L0_xattn_Wv"].T,
        "L0x_wo": v["L0_xattn_Wout"].T,
        "L0f_rw": v["L0_ffn_router_w"], "L0f_w1": v["L0_ffn_w1"].transpose(1, 0, 2).reshape(D, -1),
        "L0f_w2": block_cols(v["L0_ffn_w2"].reshape(E0 * F0, D), E0 * 4),
        "L1a_wq": v["L1_attn_Wq"], "L1a_wk": v["L1_attn_Wk"], "L1a_wv": v["L1_attn_Wv"], "L1a_wo": v["L1_attn_Wo"],
        "L1x_wq": v["L1_xattn_Wq"], "L1x_wk": v["L1_xattn_Wk"], "L1x_wv": v["L1_xattn_Wv"],
        "L1x_wo": v["L1_xattn_Wo"],
        "L1f_la": pad_rows(v["L1_ffn_lora_a"].transpose(1, 0, 2).reshape(32, -1)),
        "L1f_lb": pad_rows(v["L1_ffn_lora_b"].transpose(2, 0, 1).reshape(32, -1)),
        "L2a_wq": v["L2_attn_Wq"], "L2a_wk": v["L2_attn_Wk"], "L2a_wv": v["L2_attn_Wv"], "L2a_wo": v["L2_attn_Wo"],
        "L2x_wq": v["L2_xattn_w_q"], "L2x_wkv": v["L2_xattn_w_kv"], "L2x_wo": block_cols(v["L2_xattn_w_out"], 8),
        "L2f_u1": v["L2_ffn_U1"], "L2f_v1": pad_rows(v["L2_ffn_V1"]), "L2f_u2": block_cols(v["L2_ffn_U2"], 4),
        "L2f_v2": pad_rows(v["L2_ffn_V2"]),
        "L3a_wqkv": v["L3_attn_w_qkv"].T, "L3a_wo": v["L3_attn_w_out"].T,
        "L3x_wq": v["L3_xattn_Wq"].T, "L3x_wk": v["L3_xattn_Wk"].T, "L3x_wv": v["L3_xattn_Wv"].T,
        "L3x_wo": v["L3_xattn_Wo"].T,
        "L3f_wg": v["L3_ffn_wg"].T, "L3f_w1": v["L3_ffn_w1"].reshape(-1, D).T,
        "L3f_w3": v["L3_ffn_w3"].reshape(-1, D).T,
        "L3f_w2": block_cols(v["L3_ffn_w2"].transpose(0, 2, 1).reshape(E3 * F3, D), E3 * 2),
    }
    cp = {
        "L0a_g1": v["L0_attn_ln1_g"], "L0a_b1": v["L0_attn_ln1_b"], "L0a_fb": v["L0_attn_b1"],
        "L0x_bq": v["L0_xattn_bq"], "L0x_bk": v["L0_xattn_bk"], "L0x_bv": v["L0_xattn_bv"],
        "L0f_b1": v["L0_ffn_b1"], "L1a_bq": v["L1_attn_bq"], "L1a_bk": v["L1_attn_bk"], "L1a_bv": v["L1_attn_bv"],
        "L1x_bq": v["L1_xattn_bq"], "L1x_bk": v["L1_xattn_bk"], "L1x_bv": v["L1_xattn_bv"],
        "L1f_g": v["L1_ffn_ln_gamma"], "L1f_b": v["L1_ffn_ln_beta"],
        "L2a_bq": v["L2_attn_bq"], "L2a_bk": v["L2_attn_bk"], "L2a_bv": v["L2_attn_bv"],
        "L2x_g": v["L2_xattn_ln_gamma"], "L2x_b": v["L2_xattn_ln_beta"], "L2f_b1": v["L2_ffn_b1"],
        "L3x_bq": v["L3_xattn_bq"], "L3x_bv": v["L3_xattn_bv"],
    }
    rp = {
        "L0a_b2": v["L0_attn_b2"], "L0x_bo": v["L0_xattn_bout"], "L0f_rb": v["L0_ffn_router_b"],
        "L0f_b2": v["L0_ffn_b2"], "L1a_bo": v["L1_attn_bo"], "L1x_bo": v["L1_xattn_bo"],
        "L1f_bias": v["L1_ffn_biases"], "L2a_bo": v["L2_attn_bo"], "L2x_bo": v["L2_xattn_b_out"],
        "L2f_b2": v["L2_ffn_b2"], "L3x_bo": v["L3_xattn_bo"],
    }
    return dict(
        x=v["x"].transpose(1, 0, 2).reshape(S, NB * D),
        ctxT=v["ctx_1024"].transpose(2, 0, 1).reshape(D, NB * SC),
        consts=shape_constants(),
        cols=np.concatenate([cp[n].reshape(-1, 128).T for n, _ in COLS], axis=1),
        rows=np.concatenate([rp[n].reshape(1, -1) for n, _ in ROWS], axis=1),
        w=np.concatenate([wp[n] for _, ps in WIDTHS for n, _ in ps], axis=1),
        amask=v["mask_SxS2_ff0"], pad=np.ascontiguousarray(v["mask_BxS2_bf0"]).reshape(-1).view(np.int32),
        ln2_g=v["L0_attn_ln2_g"], ln2_b=v["L0_attn_ln2_b"], gate=v["L2_xattn_gate"],
        idx=v["L2_attn_sample_idx"],
        qw=v["L1_ffn_qweights"].transpose(2, 0, 1).reshape(D, -1),
        scl=np.repeat(v["L1_ffn_scales"].transpose(2, 0, 1), 16, axis=0).reshape(D, -1),
    )


def kernel(**inputs):
    import concourse.bacc as _bacc
    from concourse.bass_utils import run_bass_kernel_spmd as _run

    arrays = {n: np.ascontiguousarray(a) for n, a in lay_out({k: np.asarray(a) for k, a in inputs.items()}).items()}
    nc = _bacc.Bacc("TRN2", target_bir_lowering=False, num_devices=1)
    io = {n: nc.dram_tensor("in_" + n, a.shape, mybir.dt.from_np(a.dtype), kind="ExternalInput").ap()
          for n, a in arrays.items()}
    io["out"] = nc.dram_tensor("out", (S, NB * D), F32, kind="ExternalOutput").ap()
    build(nc, io)
    r = _run(nc, [{"in_" + n: a for n, a in arrays.items()}], core_ids=[0])
    got = r.results[0]["out"]
    return np.ascontiguousarray(got.reshape(S, NB, D).transpose(1, 0, 2))
```

```python
from contextlib import ExitStack

import numpy as np
import concourse.bass as bass
from concourse import mybir

F32 = mybir.dt.float32
BF16 = mybir.dt.bfloat16
I32 = mybir.dt.int32
U8 = mybir.dt.uint8
ALU = mybir.AluOpType
ACT = mybir.ActivationFunctionType
AX = mybir.AxisListType

NB, S, D = 16, 128, 128
SC = 77
H, DH = 16, 8
U = 4
UA = 2
GA = UA * S
NG = NB // U
GT = U * S
WINDOW = 32
HX, DX = 16, 64
E0, F0 = 8, 512
E3, F3 = 8, 256
VXW = (H - 1) * (DH + 1) + 32
NSAMP = 35
NTOP = 25
EPS = 1e-5
SCALE8 = float(DH) ** -0.5
GONE = -3.0e38

WIDTHS = [
    ("L0_attn", [("L0a_w1", 512), ("L0a_w2", 512)]),
    ("L0_xattn", [("L0x_wq", 128), ("L0x_wk", 128), ("L0x_wv", 128), ("L0x_wo", 128)]),
    ("L0_ffn", [("L0f_rw", E0), ("L0f_w1", E0 * 2 * F0), ("L0f_w2", E0 * F0)]),
    ("L1_attn", [("L1a_wq", 128), ("L1a_wk", 128), ("L1a_wqr", 128), ("L1a_wkr", 128), ("L1a_wv", 128), ("L1a_wo", 128)]),
    ("L1_xattn", [("L1x_wq", 128), ("L1x_wk", 128), ("L1x_wv", 128), ("L1x_wo", 128)]),
    ("L1_ffn", [("L1f_la", 768), ("L1f_lb", 768)]),
    ("L2_attn", [("L2a_wq", 128), ("L2a_wk", 128), ("L2a_wv", 128), ("L2a_wo", 128)]),
    ("L2_xattn", [("L2x_wq", 1024), ("L2x_wkv", 2048), ("L2x_wo", 1024)]),
    ("L2_ffn", [("L2f_u1", 32), ("L2f_v1", 512), ("L2f_u2", 128), ("L2f_v2", 128)]),
    ("L3_attn", [("L3a_wqkv", 384), ("L3a_wo", 128)]),
    ("L3_xattn", [("L3x_wq", 128), ("L3x_wk", 128), ("L3x_wv", 128), ("L3x_wo", 128)]),
    ("L3_ffn", [("L3f_wg", E3), ("L3f_w1", E3 * F3), ("L3f_w3", E3 * F3), ("L3f_w2", E3 * F3)]),
]
WAT, WSPAN, _at = {}, {}, 0
for _block, _parts in WIDTHS:
    if _block == "L3_ffn":
        WHBM, WCOLS = _at + sum(n for _, n in _parts), _at
        _at = WSPAN["L0_ffn"][0]
    _first = _at
    for _name, _n in _parts:
        WAT[_name] = (_at, _n)
        _at += _n
    WSPAN[_block] = (_first, _at)
assert WSPAN["L3_ffn"][1] <= WSPAN["L0_ffn"][1]

COLS = [("L0a_g1", 1), ("L0a_b1", 1), ("L0a_fb", 4), ("L0x_bq", 1), ("L0x_bk", 1), ("L0x_bv", 1),
        ("L0f_b1", 64), ("L1a_bq", 1), ("L1a_bk", 1), ("L1a_bv", 1), ("L1a_bqr", 1), ("L1a_bkr", 1), ("L1x_bq", 1), ("L1x_bk", 1),
        ("L1x_bv", 1), ("L1f_g", 3), ("L1f_b", 3), ("L2a_bq", 1), ("L2a_bk", 1), ("L2a_bv", 1),
        ("L2x_g", 1), ("L2x_b", 1), ("L2f_b1", 4), ("L3x_bq", 1), ("L3x_bv", 1)]
ROWS = [("L0a_b2", 128), ("L0x_bo", 128), ("L0f_rb", E0), ("L0f_b2", E0 * 128), ("L1a_bo", 128),
        ("L1x_bo", 128), ("L1f_bias", 768), ("L2a_bo", 128), ("L2x_bo", 128), ("L2f_b2", 128),
        ("L3x_bo", 128)]
CONSTS = [("ident", 128), ("bdiag", 128), ("bdiag16", 16), ("heads4", 4), ("heads4s", 4), ("cos", 128),
          ("sin", 128), ("window", 128), ("quarters", 4), ("rank", 8), ("part", 1)]


def offsets(table):
    at, out = 0, {}
    for name, n in table:
        out[name] = (at, n)
        at += n
    return out, at


CAT, NCOLS = offsets(COLS)
RAT, NROWS = offsets(ROWS)
KAT, NCONST = offsets(CONSTS)

NORM = dict(xg_ready=1, stats=U, moments=U, vareps=1, rstd=1, xn_ready=U, xnT_psum=1, xnT_ready=1)
HEADS = dict(xg_ready=1, stats=UA, moments=UA, vareps=1, rstd=1, xn_ready=UA, xnT_psum=1, xnT_ready=1,
             k_ready=4, v_ready=1, s_psum=8, s_max=8, s_sub=8, p_ready=8, pt_psum=8, pt_ready=8, o_psum=8,
             ov_ready=8, ob_psum=8, qz_ready=4, o_recip=UA, o_ready=UA, x_done=1)
QKV = dict(q_psum=1, q_ready=1, k_psum=1, v_psum=1, oT_psum=1, oT_ready=1, y_psum=1)
PROJ = dict(oT_psum=1, oT_ready=1, y_psum=1, x_done=1)


def times(d, n):
    return {k: v * n for k, v in d.items()}


def merged(*parts):
    out = {}
    for p in parts:
        for k, v in p.items():
            out[k] = out.get(k, 0) + v
    return out


LN = dict(stats=U, moments=U, vareps=1, rstd=1, xn_ready=U)
LNT = dict(xnT_psum=1, xnT_ready=1)
EXPERTS0 = dict(gv_psum=E0 * 4, sg_ready=E0 * 4, h_ready=E0 * 4, ye_psum=E0, acc=E0 * U)
EXPERTS3 = dict(gv_psum=E3 * 2, sg_ready=E3 * 2, h_ready=E3 * 2, ye_psum=E3, acc=E3 * U)
PER = {
    "L0_attn": merged(HEADS, dict(hold_ready=1)),
    "L0_attn_ff": merged(NORM, LN, dict(hold_ready=1, f_psum=4, f_ready=4, y_psum=1, x_done=3)),
    "L0_xattn": merged(HEADS, QKV, dict(ctx_ready=1, s_mask=8)),
    "L0_ffn": merged(NORM, EXPERTS0, dict(r_psum=1, r_step=5, x_done=1)),
    "L1_attn": merged(HEADS, {k: v for k, v in QKV.items() if k != "q_ready"}, dict(rope=6, k_psum=1)),
    "L1_xattn": merged(HEADS, QKV, dict(ctx_ready=1)),
    "L1_ffn": merged(NORM, times(LN, 3), times(LNT, 5), dict(y_psum=6, h_res=3, x_done=1)),
    "L2_attn_pick": merged(NORM, dict(q_psum=1, q_ready=1, smp_psum=2, smp_ready=5, smps_psum=4, smp_red=16,
                                      m_step=3, mT_psum=1, top=9, sel_psum=1, sel_ready=2, x_done=1)),
    "L2_attn": merged(HEADS, QKV, dict(vm_psum=1, vm_ready=1, o_mix=2 * UA)),
    "L2_xattn": merged(NORM, LN, dict(ctx_ready=1, q_psum=8, q_ready=8, k_psum=8, k_ready=8, v_psum=8,
                                           v_ready=8, s_psum=16, s_max=16, s_sub=16, p_ready=16, s_sum=16,
                                           s_rec=16, s_nrm=16, pt_psum=16, pt_ready=16, o_psum=16,
                                           oT_ready=16, y_psum=1, x_done=1)),
    "L2_ffn": merged(NORM, dict(q_psum=1, q_ready=1, f_psum=4, f_ready=4, o_psum=1, oT_ready=1, y_psum=1,
                                x_done=1)),
    "L3_attn": merged(NORM, PROJ, dict(q_psum=1, q_ready=1, k_psum=2, v_ready=2, elu_min=3, elu_exp=3, k_ready=2,
                                       s_psum=U, kv_ready=2 * U, o_psum=U, o_recip=2 * U, o_ready=U)),
    "L3_xattn": merged(NORM, PROJ, dict(ctx_ready=1, q_psum=1, q_ready=1, k_psum=1, k_ready=1, v_psum=1,
                                        v_ready=1, s_psum=1, s_max=1, s_sub=1, p_ready=1, s_sum=1, s_rec=1,
                                        s_nrm=1, pt_psum=1, pt_ready=1), ),
    "L3_ffn": merged(NORM, EXPERTS3, dict(r_psum=1, r_step=16, g_step=3, r_exp=1, x_done=1)),
}
LOADS = [b for b, _ in WIDTHS]
BLOCKS = ["L0_attn", "L0_attn_ff"] + LOADS[1:6] + ["L2_attn_pick"] + LOADS[6:]
GROUPS = {b: NB // UA if b in ("L0_attn", "L0_xattn", "L1_attn", "L1_xattn", "L2_attn") else NG for b in BLOCKS}
NAMES = sorted({k for d in PER.values() for k in d})
BASE, _sum = {}, {n: 0 for n in NAMES}
_sum["x_done"] = 4
for _b in BLOCKS:
    BASE[_b] = dict(_sum)
    for _k, _v in PER[_b].items():
        _sum[_k] += GROUPS[_b] * _v


def build(nc, io):
    with ExitStack() as ctx:
        def sb(name, shape, dt=F32):
            return ctx.enter_context(nc.sbuf_tensor(name, shape, dt))

        def psum(name, shape, dt=F32):
            return ctx.enter_context(nc.psum_tensor(name, shape, dt))

        sem = {n: ctx.enter_context(nc.semaphore(n)) for n in NAMES}
        loaded = {b: ctx.enter_context(nc.semaphore("loaded_" + b)) for b in LOADS}
        first_in = ctx.enter_context(nc.semaphore("first_in"))
        small_in = ctx.enter_context(nc.semaphore("small_in"))
        x_in = ctx.enter_context(nc.semaphore("x_in"))
        setup_v = ctx.enter_context(nc.semaphore("setup_v"))
        setup_g = ctx.enter_context(nc.semaphore("setup_g"))
        setup_a = ctx.enter_context(nc.semaphore("setup_a"))
        lora_psum = ctx.enter_context(nc.semaphore("lora_psum"))
        passed_v = ctx.enter_context(nc.semaphore("passed_v"))
        passed_t = ctx.enter_context(nc.semaphore("passed_t"))
        passed_g = ctx.enter_context(nc.semaphore("passed_g"))
        stored = ctx.enter_context(nc.semaphore("stored"))

        class Counts:

            def __init__(self, block, g, par=None):
                self.block, self.g, self.par = block, g, par

            def has(self, k, per=8):
                return not isinstance(self.g, int) or self.g * per + k > 0

            def __call__(self, name, k):
                per, base = PER[self.block][name], BASE[self.block][name]
                return sem[name], self.g * per + (base + k)

        w_all = sb("w_all", [128, WCOLS])
        consts = sb("consts", [128, NCONST])
        cols = sb("cols", [128, NCOLS])
        rows = sb("rows", [1, NROWS])
        x = sb("x", [128, NB * D])
        ctxT = sb("ctxT", [128, NB * SC])
        ones = sb("ones", [128, 128])
        mean_w = sb("mean_w", [128, 128])
        neghalf = sb("neghalf", [128, U])
        window_bf = sb("window_bf", [128, S], BF16)
        ident_bf = sb("ident_bf", [128, 128], BF16)
        g2b = sb("g2b", [128, 2, D])
        gate = sb("gate", [128, 2])
        kb4 = sb("kb4", [128, 3, 4])
        heads4s = consts[:, KAT["heads4s"][0]:KAT["heads4s"][0] + 4]
        amask = sb("amask", [128, SC])
        pad_words = sb("pad_words", [128, NB * SC // 4], I32)
        pad_u8 = pad_words[:, :].bitcast(U8)
        cmask = sb("cmask", [128, NB * SC])
        idx_i = sb("idx_i", [128, NSAMP], I32)
        idx_f = sb("idx_f", [128, 2, NSAMP])
        onehot = sb("onehot", [128, NSAMP])
        wt = sb("wt", [128, 768])

        xg = sb("xg", [128, GT])
        st = sb("st", [128, U, 6])
        mv = sb("mv", [128, U, 2])
        ve = sb("ve", [128, U])
        rstd = sb("rstd", [128, U])
        xn = sb("xn", [128, GT])
        xm = sb("xm", [128, GT])
        xnT = sb("xnT", [128, GT])
        xmT = sb("xmT", [128, GT])
        qT = sb("qT", [128, GT])
        kTr = sb("kTr", [128, GT])
        kTx = sb("kTx", [128, U, 4, S])
        vx_all = sb("vx", [128, U, VXW])
        vx = vx_all[:, :, 0:H * (DH + 1)].rearrange("p u (h e) -> p u h e", h=H)
        smx = sb("smx", [128, 2, 8])
        p = sb("p", [128, 2, 8 * S])
        pT = sb("pT", [128, 2, 8, S])
        p4 = p[:, :, :].rearrange("p a (b k) -> p (a b) k", b=2)
        pT4 = pT[:, :, :, :].rearrange("p a (b j) s -> p (a b) j s", b=2)
        rec = sb("rec", [128, 2, H])
        on = sb("on", [128, GT])
        oT = sb("oT", [128, GT])
        on2, oT2 = on[:, 0:GA], oT[:, 0:GA]
        ctxg = sb("ctxg", [128, U * SC])
        ctxa = ctxg[:, :].rearrange("p (a k) -> p a k", a=2)
        xna, xnTa, qTa = [t[:, :].rearrange("p (a k) -> p a k", a=2) for t in (xn, xnT, qT)]
        fT = sb("fT", [128, 2, 4, GT])
        qz = fT[:, 0, :, :]
        ovT = xm[:, :].rearrange("p (i s) -> p i s", i=4)
        rope1, rope2 = fT[:, 1, 0:2, :], fT[:, 1, 2:4, :]
        sg = sb("sg", [128, 2, GT])
        qw = wt[:, :].bitcast(I32)
        scl = sg[:, :, :].rearrange("p a t -> p (a t)")[:, 0:768]
        acc = sb("acc", [128, GT])
        gates = sb("gates", [128, U, 8])
        rt = sb("rt", [128, 6, U, 8])
        rm = sb("rm", [128, 6, U])
        xsT = sb("xsT", [128, U * NSAMP])
        ksx = sb("ksx", [128, U, 4, NSAMP])
        red = sb("red", [128, 3, U * H])
        cand = sb("cand", [U * H, 5, S])
        top8 = sb("top8", [U * H, 4, 8])
        vmean = [on[:, GA:2 * GA], oT[:, GA:2 * GA]]
        sel_all = sb("sel_all", [128, 2, NB * H])
        kvm = sg[:, :, 0:D + H]

        a0 = WAT["L0f_w1"][0]
        qT8 = w_all[:, a0:a0 + 8 * GT].rearrange("p (b t) -> p b t", b=8)
        kT8 = w_all[:, a0 + 8 * GT:a0 + 8 * GT + 8 * U * SC].rearrange("p (b t) -> p b t", b=8)
        v8 = w_all[:, a0 + 7168:a0 + 7168 + U * 1024].rearrange("p (u n) -> p u n", u=U)
        hold = w_all[:, WAT["L2x_wkv"][0]:WAT["L2x_wkv"][0] + NB * D]
        assert 8 * GT + 8 * U * SC <= 7168 and a0 + 7168 + U * 1024 <= WSPAN["L0_ffn"][1]

        ps = psum("ps", [128, 8, 512])
        psS = [ps[:, 0:2, :], ps[:, 2:4, :]]
        psT = ps[:, 4:6, :]
        psA, psB = ps[:, 6, :], ps[:, 7, :]
        bankS, bankT, bankM = [ps[:, 0, :], ps[:, 1, :]], [ps[:, 2, :], ps[:, 3, :]], [ps[:, 6, :], ps[:, 7, :]]
        bankV, bankO = ps[:, 4, :], ps[:, 5, :]

        def w(name, a=0, b=None):
            at, n = WAT[name]
            return w_all[:, at + a:at + (n if b is None else b)]

        def col(name, i=0):
            return cols[:, CAT[name][0] + i:CAT[name][0] + i + 1]

        def row(name, a=0, b=None):
            at, n = RAT[name]
            return rows[0:1, at + a:at + (n if b is None else b)]

        def const(name):
            at, n = KAT[name]
            return consts[:, at:at + n]

        ident, bdiag, bdiag16 = const("ident"), const("bdiag"), const("bdiag16")
        heads4, rank, part = const("heads4"), const("rank"), const("part")
        ones_row = ones[0:1, 0:128]

        def un(t, u):
            return t[:, u * 128:(u + 1) * 128]

        block = ctx.enter_context(nc.Block())
        SMALL = 11
        SETUP_G = 13

        @block.sync
        def _(sp):
            sp.dma_start(consts[:, :], io["consts"]).then_inc(first_in, 16)
            sp.dma_start(x[:, :], io["x"]).then_inc(x_in, 16)
            sp.dma_start(cols[:, :], io["cols"]).then_inc(small_in, 16)
            sp.dma_start(rows[:, :], io["rows"]).then_inc(small_in, 16)
            a, z = WSPAN["L0_attn"]
            sp.dma_start(w_all[:, a:z], io["w"][:, a:z]).then_inc(loaded["L0_attn"], 16)
            sp.dma_start(amask[:, :], io["amask"]).then_inc(small_in, 16)
            sp.dma_start(pad_words[:, :], io["pad"].partition_broadcast(128)).then_inc(small_in, 16)
            sp.dma_start(g2b[:, 0, :], io["ln2_g"].partition_broadcast(128)).then_inc(small_in, 16)
            sp.dma_start(g2b[:, 1, :], io["ln2_b"].partition_broadcast(128)).then_inc(small_in, 16)
            sp.dma_start(gate[:, 0:1], io["gate"].partition_broadcast(128)).then_inc(small_in, 16)
            sp.dma_start(idx_i[:, :], io["idx"].partition_broadcast(128)).then_inc(small_in, 16)
            sp.dma_start(qw, io["qw"]).then_inc(small_in, 16)
            sp.dma_start(scl, io["scl"]).then_inc(small_in, 16)
            sp.dma_start(ctxT[:, :], io["ctxT"]).then_inc(small_in, 16)
            for b in LOADS:
                if b not in ("L0_attn", "L2_xattn", "L3_ffn"):
                    a, z = WSPAN[b]
                    sp.dma_start(w_all[:, a:z], io["w"][:, a:z]).then_inc(loaded[b], 16)
            sp.wait_ge(sem["x_done"], BASE["L0_xattn"]["x_done"])
            a, z = WSPAN["L2_xattn"]
            sp.dma_start(w_all[:, a:z], io["w"][:, a:z]).then_inc(loaded["L2_xattn"], 16)
            sp.wait_ge(sem["x_done"], BASE["L2_ffn"]["x_done"])
            a, z = WSPAN["L3_ffn"]
            sp.dma_start(w_all[:, a:z], io["w"][:, WCOLS:WHBM]).then_inc(loaded["L3_ffn"], 16)
            sp.wait_ge(sem["x_done"], _sum["x_done"])
            sp.dma_start(io["out"], x[:, :]).then_inc(stored, 16)
            sp.wait_ge(stored, 16)

        def norm_dve(dve, at, r, src, dst, after=None):
            for u in range(U):
                if after:
                    dve.wait_ge(*after(u))
                nc.vector.bn_stats(st[:, u, :], src(u)).then_inc(sem["stats"], 1)
            dve.wait_ge(*at("stats", r * U + U))
            met_dve(dve)
            for u in range(U):
                nc.vector.bn_aggr(mv[:, u, :], st[:, u, :]).then_inc(sem["moments"], 1)
            dve.wait_ge(*at("moments", (r + 1) * U))
            nc.vector.tensor_scalar(ve[:, :], mv[:, :, 1], EPS, None, ALU.add).then_inc(sem["vareps"], 1)
            dve.wait_ge(*at("rstd", r + 1))
            for u in range(U):
                nc.vector.tensor_scalar(dst(u), src(u), mv[:, u, 0:1], rstd[:, u:u + 1],
                                        ALU.subtract, ALU.mult).then_inc(sem["xn_ready"], 1)

        def norm_pool(pool, at, r):
            pool.wait_ge(*at("vareps", r + 1))
            nc.gpsimd.tensor_tensor(rstd[:, :], ve[:, :], neghalf[:, :], ALU.pow).then_inc(sem["rstd"], 1)

        def met_dve(dve):
            dve.sem_inc(passed_v, 1)

        def met_pe(pe):
            pe.sem_inc(passed_t, 1)

        def load_group_dve(dve, at, g):
            dve.wait_ge(*at("x_done", 0))
            met_dve(dve)
            nc.vector.tensor_copy(xg[:, :], x[:, bass.ts(g, GT)]).then_inc(sem["xg_ready"], 1)

        def norm_in_dve(dve, at, g):
            load_group_dve(dve, at, g)
            dve.wait_ge(*at("xg_ready", 1))
            norm_dve(dve, at, 0, lambda u: un(xg, u), lambda u: un(xn, u))

        def flip_pe(pe, at, r, src, ready, k0):
            for u in range(U):
                pe.wait_ge(*at(ready, k0 + u + 1))
                ins = nc.tensor.transpose(un(psA, u), un(src, u), ident)
            ins.then_inc(sem["xnT_psum"], 1)

        def flip_act(act, at, r, dst):
            act.wait_ge(*at("xnT_psum", r + 1))
            nc.scalar.copy(dst[:, :], psA[:, :]).then_inc(sem["xnT_ready"], 1)

        def ctx_pool(pool, at, g):
            pool.wait_ge(*at("x_done", 0))
            nc.gpsimd.tensor_copy(ctxg[:, :], ctxT[:, bass.ts(g, U * SC)]).then_inc(sem["ctx_ready"], 1)

        class Heads:

            def __init__(self, pre, nk, scale=SCALE8, kind="self", mask=False):
                self.pre, self.nk, self.scale, self.kind, self.mask = pre, nk, scale, kind, mask
                self.window = kind == "window"
                self.cross = kind == "cross"
                self.project = not self.window

        def score_pe(pe, c, cur, par, t):
            u, quarter = divmod(t, 4)
            if t == 0:
                pe.wait_ge(*cur("k_ready", 4))
                pe.wait_ge(*cur("qz_ready", 4))
            if cur.has(t - 1):
                pe.wait_ge(*cur("s_sub", t - 1))
            q = qz[:, quarter, par * GA + u * S:par * GA + (u + 1) * S]
            ins = nc.tensor.matmul(bankS[t % 2][:, 0:4 * c.nk], q, kTx[:, UA * par + u, :, 0:c.nk],
                                   start=True, stop=not c.window)
            if c.window:
                ins = nc.tensor.matmul(bankS[t % 2][:, :], ident_bf[:, :],
                                       window_bf[:, :].unsqueeze(1).broadcast_to([128, 4, S]),
                                       start=False, stop=True)
            ins.then_inc(sem["s_psum"], 1)

        def turn_pe(pe, c, at, t):
            pe.wait_ge(*at("p_ready", t + 1))
            if at.has(t - 1):
                pe.wait_ge(*at("pt_ready", t - 1))
            for j in range(4):
                ins = nc.tensor.transpose(bankT[t % 2][0:c.nk, j * S:(j + 1) * S],
                                          p4[:, t % 4, j * c.nk:(j + 1) * c.nk], ident)
            ins.then_inc(sem["pt_psum"], 1)

        def value_pe(pe, c, at, par, t):
            u, quarter = divmod(t, 4)
            pe.wait_ge(*at("pt_ready", t + 1))
            if t == 0:
                pe.wait_ge(*at("v_ready", 1))
            if at.has(t):
                pe.wait_ge(*at("ov_ready", t))
            for j in range(4):
                first = (4 * quarter + j) * (DH + 1)
                ins = nc.tensor.matmul(bankV[32 * j:32 * j + 32, 0:S],
                                       vx_all[0:c.nk, UA * par + u, first:first + 32], pT4[0:c.nk, t % 4, j, :],
                                       start=True, stop=True)
            ins.then_inc(sem["o_psum"], 1)

        def back_pe(pe, c, at, t):
            u, quarter = divmod(t, 4)
            pe.wait_ge(*at("ov_ready", t + 1))
            if quarter == 0 and at.has(t):
                pe.wait_ge(*at("o_ready", u))
            nc.tensor.transpose(bankO[:, quarter * 128:(quarter + 1) * 128], ovT[:, t % 4, :],
                                ident).then_inc(sem["ob_psum"], 1)

        def flip_next_pe(pe, c, nxt, cur, prev, o):
            if cur and c.project and c.kind != "rope":
                pe.wait_ge(*cur("vm_ready" if c.kind == "top" else "v_ready", 1))
            if prev and c.project:
                pe.wait_ge(*prev("x_done", 0))
            for u in range(UA):
                pe.wait_ge(*nxt("xn_ready", u + 1))
                ins = nc.tensor.transpose(bankM[0][:, u * S:(u + 1) * S], xna[:, o, u * S:(u + 1) * S], ident)
            ins.then_inc(sem["xnT_psum"], 1)

        def project_next_pe(pe, c, nxt, cur, o):
            if c.window:
                return
            pe.wait_ge(*nxt("xnT_ready", 1))
            if c.kind == "rope" and cur:
                pe.wait_ge(*cur("v_ready", 1))
            xt = xnTa[:, o, :]
            if c.cross:
                pe.wait_ge(*nxt("ctx_ready", 1))
                keys = ctxa[:, o, :]
            else:
                keys = xt
            nc.tensor.matmul(bankM[1][:, 0:UA * c.nk], w(c.pre + "_wk"), keys, start=True,
                             stop=True).then_inc(sem["k_psum"], 1)
            if c.kind == "rope":
                nc.tensor.matmul(bankM[1][:, 256:512], w("L1a_wkr"), keys, start=True,
                                 stop=True).then_inc(sem["k_psum"], 1)
                nc.tensor.matmul(bankM[0][:, 0:256], w("L1a_wqr"), xt, start=True, stop=True)
            nc.tensor.matmul(bankM[0][:, 256:512], w(c.pre + "_wq"), xt, start=True,
                             stop=True).then_inc(sem["q_psum"], 1)
            if c.kind != "rope":
                values_next_pe(pe, c, nxt, o)

        def values_next_pe(pe, c, nxt, o):
            keys = ctxa[:, o, :] if c.cross else xnTa[:, o, :]
            bank = bankM[1] if c.kind == "rope" else bankM[0]
            for u in range(UA):
                ins = nc.tensor.matmul(bank[0:c.nk, u * 128:(u + 1) * 128], keys[:, u * c.nk:(u + 1) * c.nk],
                                       w(c.pre + "_wv"), start=True, stop=True)
            ins.then_inc(sem["v_psum"], 1)

        def mean_next_pe(pe, c, nxt, o):
            pe.wait_ge(*nxt("v_ready", 1))
            pe.wait_ge(*nxt("q_ready", 1))
            for u in range(UA):
                ins = nc.tensor.matmul(bankM[0][:, u * 128:(u + 1) * 128], mean_w[:, :],
                                       vx[:, UA * o + u, :, 0:DH], start=True, stop=True)
            ins.then_inc(sem["vm_psum"], 1)

        def turn_out_pe(pe, c, prev, nxt):
            pe.wait_ge(*prev("o_ready", UA))
            if nxt and c.kind == "rope":
                pe.wait_ge(*nxt("rope", 3))
            elif nxt:
                pe.wait_ge(*nxt("k_ready", 4))
            for u in range(UA):
                ins = nc.tensor.transpose(bankM[1][:, u * S:(u + 1) * S], on2[:, u * S:(u + 1) * S], ident)
            ins.then_inc(sem["oT_psum"], 1)

        def out_pe(pe, c, prev, nxt):
            pe.wait_ge(*prev("oT_ready", 1))
            if nxt:
                if c.kind == "rope":
                    pe.wait_ge(*nxt("rope", 6))
                else:
                    pe.wait_ge(*nxt("vm_ready" if c.kind == "top" else "v_ready", 1))
            for u in range(UA):
                dst = bankM[0][:, u * S:(u + 1) * S]
                nc.tensor.matmul(dst, oT2[:, u * S:(u + 1) * S], w(c.pre + "_wo"), start=True, stop=False)
                ins = nc.tensor.matmul(dst, ones_row, row(c.pre + "_bo"), start=False, stop=True)
            ins.then_inc(sem["y_psum"], 1)

        def group_pe(pe, c, cur, prev, nxt, par):
            for t in range(8):
                if cur:
                    score_pe(pe, c, cur, par, t)
                if t >= 2 and cur:
                    turn_pe(pe, c, cur, t - 2)
                if t < 2 and prev:
                    turn_pe(pe, c, prev, t + 6)
                if t >= 3 and cur:
                    value_pe(pe, c, cur, par, t - 3)
                if t < 3 and prev:
                    value_pe(pe, c, prev, 1 - par, t + 5)
                if t >= 4 and cur:
                    back_pe(pe, c, cur, t - 4)
                if t < 4 and prev:
                    back_pe(pe, c, prev, t + 4)
                if t == 2 and nxt:
                    flip_next_pe(pe, c, nxt, cur, prev, 1 - par)
                if t == 3 and nxt:
                    project_next_pe(pe, c, nxt, cur, 1 - par)
                if t == 5 and nxt and c.kind == "top":
                    mean_next_pe(pe, c, nxt, 1 - par)
                if t == 5 and prev and c.project:
                    turn_out_pe(pe, c, prev, nxt)
                if t == 6 and prev and c.project:
                    out_pe(pe, c, prev, nxt)
                if t == 6 and nxt and c.kind == "rope":
                    if prev:
                        pe.wait_ge(*prev("oT_ready", 1))
                    pe.wait_ge(*nxt("rope", 3))
                    values_next_pe(pe, c, nxt, 1 - par)

        def v2(t, n=S):
            return t.rearrange("p (u k) -> p u k", u=UA)

        def expand_next_act(act, c, nxt, o, js):
            dst = kTx[:, UA * o:UA * o + UA, :, :]
            for j in js:
                if c.window:
                    src, scale, bias = v2(xnTa[:, o, :]), heads4, 0.0
                elif c.kind == "rope":
                    src, scale, bias = v2(rope1[:, 1, 0:GA]), heads4, 0.0
                else:
                    b = KBIAS.index(c.pre)
                    src, scale, bias = v2(bankM[1][:, 0:UA * c.nk]), heads4s if c.mask else heads4, kb4[:, b, j:j + 1]
                nc.scalar.activation(dst[:, :, j, 0:c.nk], src, ACT.Identity, bias=bias,
                                     scale=scale[:, j:j + 1]).then_inc(sem["k_ready"], 1)

        def group_act(act, c, cur, prev, nxt, par):
            o = 1 - par
            expand_at = 5 if c.kind == "rope" else 4
            for t in range(8):
                at, i = (cur, t - 4) if t >= 4 else (prev, t + 4)
                if at:
                    act.wait_ge(*at("o_psum", i + 1))
                    if at.has(i - 3):
                        act.wait_ge(*at("ob_psum", i - 3))
                    nc.scalar.copy(ovT[:, i % 4, :], bankV[:, 0:S]).then_inc(sem["ov_ready"], 1)
                at, i = (cur, t - 2) if t >= 2 else (prev, t + 6)
                if at:
                    act.wait_ge(*at("pt_psum", i + 1))
                    if at.has(i - 3):
                        act.wait_ge(*at("o_psum", i - 3))
                    nc.scalar.copy(pT4[0:c.nk, i % 4, :, :].rearrange("p j s -> p (j s)"),
                                   bankT[i % 2][0:c.nk, :]).then_inc(sem["pt_ready"], 1)
                if cur:
                    act.wait_ge(*cur("s_sub", t + 1))
                    pv = p4[:, t % 4, 0:4 * c.nk]
                    nc.scalar.activation(pv, pv, ACT.Exp, scale=c.scale).then_inc(sem["p_ready"], 1)
                if t == 2 and nxt:
                    act.wait_ge(*nxt("xnT_psum", 1))
                    nc.scalar.copy(xnTa[:, o, :], bankM[0][:, 0:GA]).then_inc(sem["xnT_ready"], 1)
                if t == 4 and nxt and c.kind in ("cross", "top"):
                    act.wait_ge(*nxt("v_psum", 1))
                    nc.scalar.activation(qTa[:, o, :], bankM[0][:, 256:512], ACT.Identity,
                                         bias=col(c.pre + "_bq")).then_inc(sem["q_ready"], 1)
                if nxt and expand_at <= t < expand_at + 2:
                    if t == expand_at:
                        if c.window:
                            act.wait_ge(*nxt("xnT_ready", 1))
                        elif c.kind == "rope":
                            act.wait_ge(*nxt("rope", 3))
                        else:
                            act.wait_ge(*nxt("k_psum", 1))
                    a = 2 * (t - expand_at)
                    expand_next_act(act, c, nxt, o, (a, a + 1))
                if t == (7 if c.kind == "rope" else 4) and nxt:
                    if prev:
                        act.wait_ge(*prev("o_psum", 8))
                    if c.window:
                        act.wait_ge(*nxt("xn_ready", UA))
                        src = xna[:, o, :]
                    else:
                        act.wait_ge(*nxt("v_psum", 1))
                        src = bankM[1 if c.kind == "rope" else 0][0:c.nk, 0:GA]
                    nc.scalar.copy(vx[0:c.nk, UA * o:UA * o + UA, :, 0:DH],
                                   src.rearrange("p (u h e) -> p u h e", u=UA, e=DH)).then_inc(sem["v_ready"], 1)
                if t == 5 and prev and c.project:
                    act.wait_ge(*prev("oT_psum", 1))
                    nc.scalar.activation(oT2[:, :], bankM[1][:, 0:GA], ACT.Identity,
                                         bias=col(c.pre + "_bv")).then_inc(sem["oT_ready"], 1)

        def softmax_dve(dve, c, cur, t):
            u = t // 4
            sv = bankS[t % 2][:, 0:4 * c.nk].rearrange("p (j k) -> p j k", j=4)
            mx = smx[:, t % 2, 0:4]
            dve.wait_ge(*cur("s_psum", t + 1))
            if c.mask:
                m = cmask[:, bass.ts(cur.g * UA + u, SC)].unsqueeze(1).broadcast_to([128, 4, SC])
                nc.vector.tensor_tensor(sv, sv, m, ALU.add).then_inc(sem["s_mask"], 1)
                dve.wait_ge(*cur("s_mask", t + 1))
            nc.vector.tensor_reduce(mx, sv, AX.X, ALU.max).then_inc(sem["s_max"], 1)
            dve.wait_ge(*cur("s_max", t + 1))
            if cur.has(t - 3):
                dve.wait_ge(*cur("pt_psum", t - 3))
            nc.vector.tensor_tensor(p4[:, t % 4, 0:4 * c.nk].rearrange("p (j k) -> p j k", j=4), sv,
                                    mx.unsqueeze(2).broadcast_to([128, 4, c.nk]),
                                    ALU.subtract).then_inc(sem["s_sub"], 1)

        def finish_dve(dve, c, at, u):
            dve.wait_ge(*at("ob_psum", 4 * u + 4))
            ov = bankO[:, :].rearrange("p (h e) -> p h e", h=H)
            nc.vector.reciprocal(rec[:, u, :], ov[:, :, DH]).then_inc(sem["o_recip"], 1)
            dve.wait_ge(*at("o_recip", u + 1))
            dv = on2[:, u * S:(u + 1) * S]
            dh = dv.rearrange("p (h e) -> p h e", h=H)
            rb = rec[:, u, :].unsqueeze(2).broadcast_to([128, H, DH])
            if c.kind == "top":
                nc.vector.tensor_tensor(rec[:, u, :], rec[:, u, :], sel_all[:, 0, bass.ts(at.g * UA + u, H)],
                                        ALU.mult).then_inc(sem["o_mix"], 1)
                dve.wait_ge(*at("o_mix", 2 * u + 1))
                nc.vector.tensor_tensor(dh, ov[:, :, 0:DH], rb, ALU.mult).then_inc(sem["o_mix"], 1)
                dve.wait_ge(*at("o_mix", 2 * u + 2))
                nc.vector.tensor_tensor(dv, dv, vmean[at.par][:, u * S:(u + 1) * S],
                                        ALU.add).then_inc(sem["o_ready"], 1)
            else:
                nc.vector.tensor_tensor(dh, ov[:, :, 0:DH], rb, ALU.mult).then_inc(sem["o_ready"], 1)

        def load_next_dve(dve, c, nxt, cur):
            if cur is None:
                dve.wait_ge(*nxt("x_done", 0))
            else:
                dve.wait_ge(*cur("xn_ready", UA))
            met_dve(dve)
            nc.vector.tensor_copy(xg[:, 0:GA], x[:, bass.ts(nxt.g, GA)]).then_inc(sem["xg_ready"], 1)
            dve.wait_ge(*nxt("xg_ready", 1))
            for u in range(UA):
                nc.vector.bn_stats(st[:, u, :], xg[:, u * S:(u + 1) * S]).then_inc(sem["stats"], 1)
            dve.wait_ge(*nxt("stats", UA))
            met_dve(dve)
            for u in range(UA):
                nc.vector.bn_aggr(mv[:, u, :], st[:, u, :]).then_inc(sem["moments"], 1)
            dve.wait_ge(*nxt("moments", UA))
            nc.vector.tensor_scalar(ve[:, 0:UA], mv[:, 0:UA, 1], EPS, None, ALU.add).then_inc(sem["vareps"], 1)

        def norm_next_dve(dve, c, nxt, o):
            dve.wait_ge(*nxt("rstd", 1))
            for u in range(UA):
                nc.vector.tensor_scalar(xna[:, o, u * S:(u + 1) * S], xg[:, u * S:(u + 1) * S], mv[:, u, 0:1],
                                        rstd[:, u:u + 1], ALU.subtract, ALU.mult).then_inc(sem["xn_ready"], 1)

        def rope_next_dve(dve, c, nxt, o, q):
            cosb = const("cos").unsqueeze(1).broadcast_to([128, UA, S])
            sinb = const("sin").unsqueeze(1).broadcast_to([128, UA, S])
            if q:
                dve.wait_ge(*nxt("q_psum", 1))
                bank, rbank, a, b, k, to = bankM[0][:, 256:512], bankM[0][:, 0:256], "L1a_bq", "L1a_bqr", 3, qTa[:, o, :]
            else:
                dve.wait_ge(*nxt("k_psum", 2))
                bank, rbank, a, b, k, to = (bankM[1][:, 0:256], bankM[1][:, 256:512], "L1a_bk", "L1a_bkr", 0,
                                            rope1[:, 1, 0:GA])
            nc.vector.scalar_tensor_tensor(out=v2(rope1[:, 0, 0:GA]), in0=v2(bank),
                                           scalar=col(a), in1=cosb, op0=ALU.add, op1=ALU.mult).then_inc(sem["rope"], 1)
            nc.vector.scalar_tensor_tensor(out=v2(rope2[:, q, 0:GA]), in0=v2(rbank), scalar=col(b),
                                           in1=sinb, op0=ALU.add, op1=ALU.mult).then_inc(sem["rope"], 1)
            dve.wait_ge(*nxt("rope", k + 2))
            nc.vector.tensor_tensor(to, rope1[:, 0, 0:GA], rope2[:, q, 0:GA], ALU.add).then_inc(sem["rope"], 1)

        def mean_next_dve(dve, c, nxt, o):
            dve.wait_ge(*nxt("vm_psum", 1))
            nc.vector.tensor_tensor(vmean[o].rearrange("p (n e) -> p n e", e=DH),
                                    bankM[0][:, 0:GA].rearrange("p (n e) -> p n e", e=DH),
                                    sel_all[:, 1, bass.ts(nxt.g, UA * H)].unsqueeze(2).broadcast_to([128, UA * H, DH]),
                                    ALU.mult).then_inc(sem["vm_ready"], 1)

        def group_dve(dve, c, cur, prev, nxt, par):
            for t in range(8):
                if t == 0 and prev:
                    finish_dve(dve, c, prev, 0)
                if t == 4 and prev:
                    finish_dve(dve, c, prev, 1)
                if cur:
                    softmax_dve(dve, c, cur, t)
                if t == 0 and nxt:
                    load_next_dve(dve, c, nxt, cur)
                if t == 1 and nxt:
                    norm_next_dve(dve, c, nxt, 1 - par)
                if t in (4, 5) and nxt and c.kind == "rope":
                    if t == 5:
                        dve.wait_ge(*nxt("rope", 3))
                    rope_next_dve(dve, c, nxt, 1 - par, t - 4)
                if t == 5 and prev and c.window:
                    dve.wait_ge(*prev("o_ready", UA))
                    dve.wait_ge(*prev("hold_ready", 1))
                    hs = hold[:, bass.ts(prev.g, GA)]
                    nc.vector.tensor_tensor(hs, hs, on2[:, :], ALU.add).then_inc(sem["x_done"], 1)
                if t == 5 and nxt and c.kind == "top":
                    mean_next_dve(dve, c, nxt, 1 - par)
                if t == 7 and prev and c.project:
                    dve.wait_ge(*prev("y_psum", 1))
                    xs = x[:, bass.ts(prev.g, GA)]
                    nc.vector.tensor_tensor(xs, xs, bankM[0][:, 0:GA], ALU.add).then_inc(sem["x_done"], 1)

        def group_pool(pool, c, cur, prev, nxt, par):
            if nxt:
                if c.cross:
                    if nxt.has(-1, per=1):
                        pool.wait_ge(*nxt("v_psum", -1))
                    nc.gpsimd.tensor_copy(ctxa[:, 1 - par, :],
                                          ctxT[:, bass.ts(nxt.g, UA * SC)]).then_inc(sem["ctx_ready"], 1)
                pool.wait_ge(*nxt("vareps", 1))
                nc.gpsimd.tensor_tensor(rstd[:, 0:UA], ve[:, 0:UA], neghalf[:, 0:UA], ALU.pow).then_inc(sem["rstd"], 1)
                if c.window:
                    pool.wait_ge(*nxt("xn_ready", UA))
                    nc.gpsimd.tensor_copy(hold[:, bass.ts(nxt.g, GA)],
                                          xna[:, 1 - par, :]).then_inc(sem["hold_ready"], 1)
                o = 1 - par
                if c.window:
                    pool.wait_ge(*nxt("xnT_ready", 1))
                elif c.kind == "rope":
                    pool.wait_ge(*nxt("rope", 6))
                else:
                    pool.wait_ge(*nxt("q_ready", 1))
                pool.sem_inc(passed_g, 1)
                for quarter in range(4):
                    nc.gpsimd.tensor_scalar(qz[:, quarter, o * GA:(o + 1) * GA], (xnTa if c.window else qTa)[:, o, :],
                                            const("quarters")[:, quarter:quarter + 1], None,
                                            ALU.mult).then_inc(sem["qz_ready"], 1)

        def run_heads(eng, block_name, body, c):
            n = GROUPS[block_name]

            def counts(g, par):
                return Counts(block_name, g, par)

            body(eng, c, None, None, counts(0, 0), 1)
            body(eng, c, counts(0, 0), None, counts(1, 1), 0)
            with eng.Fori(0, (n - 2) // 2) as i:
                for k in range(2):
                    par = (1 + k) % 2
                    body(eng, c, counts(2 * i + (k + 1), par), counts(2 * i + k, 1 - par),
                         counts(2 * i + (k + 2), 1 - par), par)
            last = (n - 1) % 2
            body(eng, c, counts(n - 1, last), counts(n - 2, 1 - last), None, last)
            body(eng, c, None, counts(n - 1, last), None, 1 - last)

        KBIAS = ["L0x", "L1x", "L2a"]
        HEADS_OF = {
            "L0_attn": Heads("L0a", S, 1.0, "window"),
            "L0_xattn": Heads("L0x", SC, 1.0, "cross", mask=True),
            "L1_attn": Heads("L1a", S, kind="rope"),
            "L1_xattn": Heads("L1x", SC, kind="cross"),
            "L2_attn": Heads("L2a", S, kind="top"),
        }
        HEADS_PROGRAM = (group_pe, group_act, group_dve, group_pool)

        def s_view(half, nk):
            return psS[half][:, :, 0:4 * nk].rearrange("p b (j k) -> p b j k", j=4)

        def project_pe(pe, at, wo, bo):
            pe.wait_ge(*at("o_ready", U))
            for u in range(U):
                ins = nc.tensor.transpose(un(psB, u), un(on, u), ident)
            ins.then_inc(sem["oT_psum"], 1)
            rows_pe(pe, at, oT, wo, bo, at("oT_ready", 1))

        def rows_pe(pe, at, lhs, wo, bo, ready, dst=psA):
            pe.wait_ge(*ready)
            for u in range(U):
                ins = nc.tensor.matmul(un(dst, u), un(lhs, u), wo, start=True, stop=bo is None)
                if bo is not None:
                    ins = nc.tensor.matmul(un(dst, u), ones_row, bo, start=False, stop=True)
            ins.then_inc(sem["y_psum"], 1)

        def project_act(act, at, bv):
            act.wait_ge(*at("oT_psum", 1))
            if bv is None:
                nc.scalar.copy(oT[:, :], psB[:, :]).then_inc(sem["oT_ready"], 1)
            else:
                nc.scalar.activation(oT[:, :], psB[:, :], ACT.Identity, bias=bv).then_inc(sem["oT_ready"], 1)

        def residual_dve(dve, at, g, k=1, bank=psA):
            dve.wait_ge(*at("y_psum", k))
            nc.vector.tensor_tensor(x[:, bass.ts(g, GT)], xg[:, :], bank[:, :], ALU.add).then_inc(sem["x_done"], 1)

        def l0_ff_pe(pe, at, g):
            flip_pe(pe, at, 0, xm, "xn_ready", 0)
            pe.wait_ge(*at("xnT_ready", 1))
            for b in range(4):
                nc.tensor.matmul(psS[b // 2][:, b % 2, :], w("L0a_w1", b * 128, b * 128 + 128), xmT[:, :],
                                 start=True, stop=True).then_inc(sem["f_psum"], 1)
            pe.wait_ge(*at("f_ready", 4))
            for u in range(U):
                for b in range(4):
                    nc.tensor.matmul(un(psB, u), un(fT[:, 0, b, :], u), w("L0a_w2", b * 128, b * 128 + 128),
                                     start=(b == 0), stop=False)
                nc.tensor.matmul(un(psB, u), un(xmT, u), ident, start=False, stop=False)
                ins = nc.tensor.matmul(un(psB, u), ones_row, row("L0a_b2"), start=False, stop=True)
            ins.then_inc(sem["y_psum"], 1)

        def l0_ff_act(act, at, g):
            act.wait_ge(*at("xnT_psum", 1))
            nc.scalar.activation(xmT[:, :], psA[:, :], ACT.Identity, bias=col("L0a_b1"),
                                 scale=col("L0a_g1")).then_inc(sem["xnT_ready"], 1)
            for b in range(4):
                act.wait_ge(*at("f_psum", b + 1))
                nc.scalar.activation(fT[:, 0, b, :], psS[b // 2][:, b % 2, :], ACT.Relu,
                                     bias=col("L0a_fb", b)).then_inc(sem["f_ready"], 1)

        def l0_ff_dve(dve, at, g):
            dve.wait_ge(*at("x_done", 0))
            met_dve(dve)
            nc.vector.tensor_copy(xg[:, :], x[:, bass.ts(g, GT)]).then_inc(sem["xg_ready"], 1)
            nc.vector.tensor_copy(on[:, :], hold[:, bass.ts(g, GT)]).then_inc(sem["hold_ready"], 1)
            dve.wait_ge(*at("hold_ready", 1))
            norm_dve(dve, at, 0, lambda u: un(on, u), lambda u: un(xm, u))
            norm_dve(dve, at, 1, lambda u: un(psB, u), lambda u: un(xn, u), after=lambda u: at("y_psum", 1))
            dve.wait_ge(*at("xn_ready", 2 * U))
            v3 = xn[:, :].rearrange("p (u d) -> p u d", u=U)
            gain = g2b[:, 0, :].unsqueeze(1).broadcast_to([128, U, D])
            shift = g2b[:, 1, :].unsqueeze(1).broadcast_to([128, U, D])
            nc.vector.tensor_tensor(v3, v3, gain, ALU.mult).then_inc(sem["x_done"], 1)
            dve.wait_ge(*at("x_done", 1))
            nc.vector.tensor_tensor(v3, v3, shift, ALU.add).then_inc(sem["x_done"], 1)
            dve.wait_ge(*at("x_done", 2))
            nc.vector.tensor_tensor(x[:, bass.ts(g, GT)], xg[:, :], xn[:, :], ALU.add).then_inc(sem["x_done"], 1)

        def l0_ff_pool(pool, at, g):
            norm_pool(pool, at, 0)
            norm_pool(pool, at, 1)

        def cross_pool(pool, at, g):
            ctx_pool(pool, at, g)
            norm_pool(pool, at, 0)

        def experts_pe(pe, at, g, ne, nb, wgate, wval, wout, bout):
            for e in range(ne):
                for b in range(nb):
                    j = e * nb + b
                    if j >= 2:
                        pe.wait_ge(*at("h_ready", j - 1))
                    nc.tensor.matmul(psS[0][:, j % 2, :], wgate(e, b), xnT[:, :], start=True, stop=True)
                    nc.tensor.matmul(psS[1][:, j % 2, :], wval(e, b), xnT[:, :], start=True,
                                     stop=True).then_inc(sem["gv_psum"], 1)
                if e >= 1:
                    expert_out_pe(pe, at, e - 1, nb, wout, bout)
            expert_out_pe(pe, at, ne - 1, nb, wout, bout)

        def expert_out_pe(pe, at, e, nb, wout, bout):
            pe.wait_ge(*at("h_ready", (e + 1) * nb))
            if e >= 2:
                pe.wait_ge(*at("acc", (e - 1) * U))
            for u in range(U):
                for b in range(nb):
                    ins = nc.tensor.matmul(un(psT[:, e % 2, :], u), un(fT[:, e % 2, b, :], u), wout(e, b),
                                           start=(b == 0), stop=(b == nb - 1 and bout is None))
                if bout is not None:
                    ins = nc.tensor.matmul(un(psT[:, e % 2, :], u), ones_row, bout(e), start=False, stop=True)
            ins.then_inc(sem["ye_psum"], 1)

        def experts_act(act, at, ne, nb, func, bgate):
            for j in range(ne * nb):
                act.wait_ge(*at("gv_psum", j + 1))
                if j >= 2:
                    act.wait_ge(*at("h_ready", j - 1))
                bias = bgate(j // nb, j % nb) if bgate else 0.0
                nc.scalar.activation(sg[:, j % 2, :], psS[0][:, j % 2, :], func, bias=bias).then_inc(sem["sg_ready"], 1)

        def experts_dve(dve, at, g, ne, nb, bval):
            for e in range(ne):
                for b in range(nb):
                    j = e * nb + b
                    dve.wait_ge(*at("sg_ready", j + 1))
                    if e >= 2 and b == 0:
                        dve.wait_ge(*at("ye_psum", e - 1))
                    hv = psS[1][:, j % 2, :]
                    if bval:
                        ins = nc.vector.scalar_tensor_tensor(out=fT[:, e % 2, b, :], in0=hv, scalar=bval(e, b),
                                                             in1=sg[:, j % 2, :], op0=ALU.add, op1=ALU.mult)
                    else:
                        ins = nc.vector.tensor_tensor(fT[:, e % 2, b, :], hv, sg[:, j % 2, :], ALU.mult)
                    ins.then_inc(sem["h_ready"], 1)
                if e >= 1:
                    gather_dve(dve, at, g, e - 1, ne)
            gather_dve(dve, at, g, ne - 1, ne)

        def gather_dve(dve, at, g, e, ne):
            dve.wait_ge(*at("ye_psum", e + 1))
            for u in range(U):
                if e >= 1:
                    dve.wait_ge(*at("acc", (e - 1) * U + u + 1))
                base = xg if e == 0 else acc
                nc.vector.scalar_tensor_tensor(out=un(acc, u), in0=un(psT[:, e % 2, :], u),
                                               scalar=gates[:, u, e:e + 1], in1=un(base, u), op0=ALU.mult,
                                               op1=ALU.add).then_inc(sem["acc"], 1)
            if e == ne - 1:
                dve.wait_ge(*at("acc", ne * U))
                met_dve(dve)
                nc.vector.tensor_copy(x[:, bass.ts(g, GT)], acc[:, :]).then_inc(sem["x_done"], 1)

        def router_pe(pe, at, wr, br):
            for u in range(U):
                ins = nc.tensor.matmul(psB[:, u * 8:(u + 1) * 8], un(xnT, u), wr, start=True, stop=br is None)
                if br is not None:
                    ins = nc.tensor.matmul(psB[:, u * 8:(u + 1) * 8], ones_row, br, start=False, stop=True)
            ins.then_inc(sem["r_psum"], 1)

        logits = psB[:, 0:U * 8].rearrange("p (u e) -> p u e", u=U)

        def b8(t):
            return t.unsqueeze(2).broadcast_to([128, U, 8])

        rank4 = rank.unsqueeze(1).broadcast_to([128, U, 8])

        def first_max_dve(dve, at, k, src, m, t, dst):
            nc.vector.tensor_reduce(rm[:, m, :], src, AX.X, ALU.max).then_inc(sem["r_step"], 1)
            dve.wait_ge(*at("r_step", k + 1))
            nc.vector.tensor_tensor(rt[:, t, :, :], src, b8(rm[:, m, :]), ALU.is_equal).then_inc(sem["r_step"], 1)
            dve.wait_ge(*at("r_step", k + 2))
            nc.vector.tensor_tensor(rt[:, t, :, :], rt[:, t, :, :], rank4, ALU.mult).then_inc(sem["r_step"], 1)
            dve.wait_ge(*at("r_step", k + 3))
            nc.vector.tensor_reduce(rm[:, 5, :], rt[:, t, :, :], AX.X, ALU.max).then_inc(sem["r_step"], 1)
            dve.wait_ge(*at("r_step", k + 4))
            nc.vector.tensor_tensor(dst, rt[:, t, :, :], b8(rm[:, 5, :]), ALU.is_equal).then_inc(sem["r_step"], 1)
            dve.wait_ge(*at("r_step", k + 5))

        def l0_ffn_pe(pe, at, g):
            flip_pe(pe, at, 0, xn, "xn_ready", 0)
            pe.wait_ge(*at("xnT_ready", 1))
            router_pe(pe, at, w("L0f_rw"), row("L0f_rb"))
            experts_pe(pe, at, g, E0, 4,
                       lambda e, b: w("L0f_w1", e * 1024 + 512 + b * 128, e * 1024 + 512 + b * 128 + 128),
                       lambda e, b: w("L0f_w1", e * 1024 + b * 128, e * 1024 + b * 128 + 128),
                       lambda e, b: w("L0f_w2", (e * 4 + b) * 128, (e * 4 + b) * 128 + 128),
                       lambda e: row("L0f_b2", e * 128, e * 128 + 128))

        def l0_ffn_act(act, at, g):
            flip_act(act, at, 0, xnT)
            experts_act(act, at, E0, 4, ACT.Sigmoid, lambda e, b: col("L0f_b1", e * 8 + 4 + b))

        def l0_ffn_dve(dve, at, g):
            norm_in_dve(dve, at, g)
            dve.wait_ge(*at("r_psum", 1))
            first_max_dve(dve, at, 0, logits, 0, 0, gates[:, :, :])
            experts_dve(dve, at, g, E0, 4, lambda e, b: col("L0f_b1", e * 8 + b))

        def norm_only_pool(pool, at, g):
            norm_pool(pool, at, 0)

        def l3_ffn_pe(pe, at, g):
            flip_pe(pe, at, 0, xn, "xn_ready", 0)
            pe.wait_ge(*at("xnT_ready", 1))
            router_pe(pe, at, w("L3f_wg"), None)
            experts_pe(pe, at, g, E3, 2,
                       lambda e, b: w("L3f_w1", (e * 2 + b) * 128, (e * 2 + b) * 128 + 128),
                       lambda e, b: w("L3f_w3", (e * 2 + b) * 128, (e * 2 + b) * 128 + 128),
                       lambda e, b: w("L3f_w2", (e * 2 + b) * 128, (e * 2 + b) * 128 + 128), None)

        def l3_ffn_act(act, at, g):
            flip_act(act, at, 0, xnT)
            act.wait_ge(*at("r_step", 2))
            nc.scalar.activation(rt[:, 1, :, :], rt[:, 0, :, :], ACT.Exp).then_inc(sem["r_exp"], 1)
            experts_act(act, at, E3, 2, ACT.Silu, None)

        def l3_ffn_dve(dve, at, g):
            norm_in_dve(dve, at, g)
            dve.wait_ge(*at("r_psum", 1))
            step = [0]

            def inc(ins):
                step[0] += 1
                ins.then_inc(sem["r_step"], 1)
                dve.wait_ge(*at("r_step", step[0]))

            inc(nc.vector.tensor_reduce(rm[:, 0, :], logits, AX.X, ALU.max))
            inc(nc.vector.tensor_tensor(rt[:, 0, :, :], logits, b8(rm[:, 0, :]), ALU.subtract))
            dve.wait_ge(*at("r_exp", 1))
            first_max_dve(dve, at, 2, rt[:, 1, :, :], 1, 2, rt[:, 3, :, :])
            step[0] = 7
            inc(nc.vector.tensor_scalar(rt[:, 4, :, :], rt[:, 3, :, :], -2.0, None, ALU.mult))
            inc(nc.vector.tensor_tensor(rt[:, 4, :, :], rt[:, 4, :, :], rt[:, 1, :, :], ALU.add))
            first_max_dve(dve, at, 9, rt[:, 4, :, :], 2, 2, rt[:, 5, :, :])
            step[0] = 14
            inc(nc.vector.tensor_tensor(rm[:, 3, :], rm[:, 1, :], rm[:, 2, :], ALU.add))
            nc.vector.reciprocal(rm[:, 4, :], rm[:, 3, :]).then_inc(sem["r_step"], 1)
            dve.wait_ge(*at("r_step", 16))
            inc2 = sem["g_step"]
            nc.vector.tensor_tensor(rt[:, 3, :, :], rt[:, 3, :, :], rt[:, 5, :, :], ALU.add).then_inc(inc2, 1)
            dve.wait_ge(*at("g_step", 1))
            nc.vector.tensor_tensor(rt[:, 3, :, :], rt[:, 3, :, :], rt[:, 1, :, :], ALU.mult).then_inc(inc2, 1)
            dve.wait_ge(*at("g_step", 2))
            nc.vector.tensor_tensor(gates[:, :, :], rt[:, 3, :, :], b8(rm[:, 4, :]), ALU.mult).then_inc(inc2, 1)
            dve.wait_ge(*at("g_step", 3))
            experts_dve(dve, at, g, E3, 2, None)

        def l1_ffn_pe(pe, at, g):
            flip_pe(pe, at, 0, xn, "xn_ready", 0)
            for blk in range(3):
                def wl(i):
                    return wt[:, i * 128:(i + 1) * 128]

                def bl(i):
                    return row("L1f_bias", i * 128, i * 128 + 128)
                rows_pe(pe, at, xnT, wl(2 * blk), bl(2 * blk), at("xnT_ready", 2 * blk + 1), dst=psB)
                flip_pe(pe, at, 0, xm, "xn_ready", U * (blk + 1))
                rows_pe(pe, at, xmT, wl(2 * blk + 1), bl(2 * blk + 1), at("xnT_ready", 2 * blk + 2), dst=psB)
                if blk < 2:
                    pe.wait_ge(*at("h_res", blk + 1))
                    for u in range(U):
                        ins = nc.tensor.transpose(un(psA, u), un(xn, u), ident)
                    ins.then_inc(sem["xnT_psum"], 1)

        def l1_ffn_act(act, at, g):
            flip_act(act, at, 0, xnT)
            for blk in range(3):
                act.wait_ge(*at("xnT_psum", 2 * blk + 2))
                nc.scalar.activation(xmT[:, :], psA[:, :], ACT.Gelu, bias=col("L1f_b", blk),
                                     scale=col("L1f_g", blk)).then_inc(sem["xnT_ready"], 1)
                if blk < 2:
                    flip_act(act, at, 2 * blk + 2, xnT)

        def l1_ffn_dve(dve, at, g):
            norm_in_dve(dve, at, g)
            for blk in range(3):
                norm_dve(dve, at, blk + 1, lambda u: un(psB, u), lambda u: un(xm, u),
                         after=lambda u: at("y_psum", 2 * blk + 1))
                dve.wait_ge(*at("y_psum", 2 * blk + 2))
                nc.vector.tensor_tensor(xn[:, :], xn[:, :], psB[:, :], ALU.add).then_inc(sem["h_res"], 1)
                dve.wait_ge(*at("h_res", blk + 1))
            nc.vector.tensor_tensor(x[:, bass.ts(g, GT)], xg[:, :], xn[:, :], ALU.add).then_inc(sem["x_done"], 1)

        def l1_ffn_pool(pool, at, g):
            for r in range(4):
                norm_pool(pool, at, r)

        def pick_pe(pe, at, g):
            pe.wait_ge(*at("xn_ready", U))
            for u in range(U):
                ins = nc.tensor.matmul(psT[:, 0, u * NSAMP:(u + 1) * NSAMP], un(xn, u), onehot[:, :],
                                       start=True, stop=True)
            ins.then_inc(sem["smp_psum"], 1)
            flip_pe(pe, at, 0, xn, "xn_ready", 0)
            pe.wait_ge(*at("smp_ready", 1))
            nc.tensor.matmul(psT[:, 1, 0:U * NSAMP], w("L2a_wk"), xsT[:, :], start=True,
                             stop=True).then_inc(sem["smp_psum"], 1)
            pe.wait_ge(*at("xnT_ready", 1))
            nc.tensor.matmul(psB[:, :], w("L2a_wq"), xnT[:, :], start=True, stop=True).then_inc(sem["q_psum"], 1)
            pe.wait_ge(*at("smp_ready", 5))
            pe.wait_ge(*at("q_ready", 1))
            for u in range(U):
                if u >= 1:
                    pe.wait_ge(*at("smp_red", 4 * u))
                for gq in range(4):
                    rs = slice(32 * gq, 32 * gq + 32)
                    ins = nc.tensor.matmul(psS[gq // 2][:, gq % 2, 0:4 * NSAMP], qT[rs, u * S:(u + 1) * S],
                                           ksx[rs, u, :, :], start=True, stop=True)
                ins.then_inc(sem["smps_psum"], 1)
            pe.wait_ge(*at("m_step", 1))
            met_pe(pe)
            nc.tensor.transpose(psT[0:U * H, 0, 0:S], red[:, 2, :], ident).then_inc(sem["mT_psum"], 1)
            pe.wait_ge(*at("top", 9))
            met_pe(pe)
            nc.tensor.transpose(psT[:, 1, 0:U * H], cand[:, 4, :], ident[0:U * H, 0:U * H]).then_inc(sem["sel_psum"], 1)

        def pick_act(act, at, g):
            act.wait_ge(*at("smp_psum", 1))
            nc.scalar.copy(xsT[:, :], psT[:, 0, 0:U * NSAMP]).then_inc(sem["smp_ready"], 1)
            flip_act(act, at, 0, xnT)
            act.wait_ge(*at("q_psum", 1))
            nc.scalar.activation(qT[:, :], psB[:, :], ACT.Identity, bias=col("L2a_bq")).then_inc(sem["q_ready"], 1)

        def pick_dve(dve, at, g):
            norm_in_dve(dve, at, g)
            dve.wait_ge(*at("smp_ready", 1))
            dve.wait_ge(*at("smp_psum", 2))
            for j in range(4):
                nc.vector.tensor_scalar(ksx[:, :, j, :], psT[:, 1, 0:U * NSAMP].rearrange("p (u k) -> p u k", u=U),
                                        col("L2a_bk"), heads4[:, j:j + 1], ALU.add,
                                        ALU.mult).then_inc(sem["smp_ready"], 1)
            for u in range(U):
                dve.wait_ge(*at("smps_psum", u + 1))
                for n, op in ((0, ALU.max), (1, ALU.add)):
                    for half in range(2):
                        c = u * H + half * 8
                        nc.vector.tensor_reduce(red[:, n, c:c + 8].rearrange("p (b j) -> p b j", b=2),
                                                s_view(half, NSAMP), AX.X, op).then_inc(sem["smp_red"], 1)
            dve.wait_ge(*at("smp_red", 16))
            nc.vector.scalar_tensor_tensor(out=red[:, 2, :], in0=red[:, 1, :], scalar=-1.0 / NSAMP,
                                           in1=red[:, 0, :], op0=ALU.mult, op1=ALU.add).then_inc(sem["m_step"], 1)
            dve.wait_ge(*at("mT_psum", 1))
            nc.vector.tensor_copy(cand[:, 0, :], psT[0:U * H, 0, 0:S]).then_inc(sem["top"], 1)
            dve.wait_ge(*at("top", 1))
            for r in range(3):
                met_dve(dve)
                nc.vector.max(top8[:, r, :], cand[:, r, :]).then_inc(sem["top"], 1)
                dve.wait_ge(*at("top", 2 + 2 * r))
                met_dve(dve)
                nc.vector.match_replace(cand[:, r + 1, :], top8[:, r, :], cand[:, r, :], GONE).then_inc(sem["top"], 1)
                dve.wait_ge(*at("top", 3 + 2 * r))
            met_dve(dve)
            nc.vector.max(top8[:, 3, :], cand[:, 3, :]).then_inc(sem["m_step"], 1)
            dve.wait_ge(*at("m_step", 2))
            nc.vector.memset(top8[:, 3, 1:8], GONE).then_inc(sem["m_step"], 1)
            dve.wait_ge(*at("m_step", 3))
            met_dve(dve)
            nc.vector.match_replace(cand[:, 4, :], top8[:, 3, :], cand[:, 3, :], GONE).then_inc(sem["top"], 1)
            dve.wait_ge(*at("top", 8))
            nc.vector.tensor_scalar(cand[:, 4, :], cand[:, 4, :], GONE, None, ALU.is_equal).then_inc(sem["top"], 1)
            dve.wait_ge(*at("sel_psum", 1))
            nc.vector.tensor_scalar(sel_all[:, 0, bass.ts(g, U * H)], psT[:, 1, 0:U * H], 1.0, None,
                                    ALU.mult).then_inc(sem["sel_ready"], 1)
            nc.vector.tensor_scalar(sel_all[:, 1, bass.ts(g, U * H)], psT[:, 1, 0:U * H], -1.0, 1.0, ALU.mult,
                                    ALU.add).then_inc(sem["sel_ready"], 1)
            dve.wait_ge(*at("sel_ready", 2))
            dve.sem_inc(sem["x_done"], 1)

        def l2_xattn_pe(pe, at, g):
            pe.wait_ge(*at("ctx_ready", 1))
            for b in range(8):
                if b >= 2:
                    pe.wait_ge(*at("k_ready", b - 1))
                nc.tensor.matmul(psS[0][:, b % 2, 0:U * SC], w("L2x_wkv", b * 128, b * 128 + 128), ctxg[:, :],
                                 start=True, stop=True).then_inc(sem["k_psum"], 1)
            for n in range(8):
                u, c = divmod(n, 2)
                if n >= 2:
                    pe.wait_ge(*at("v_ready", n - 1))
                nc.tensor.matmul(psS[1][0:SC, c, :], ctxg[:, u * SC:(u + 1) * SC],
                                 w("L2x_wkv", 1024 + c * 512, 1024 + c * 512 + 512), start=True,
                                 stop=True).then_inc(sem["v_psum"], 1)
            flip_pe(pe, at, 0, xm, "xn_ready", U)
            pe.wait_ge(*at("xnT_ready", 1))
            for b in range(8):
                if b >= 2:
                    pe.wait_ge(*at("q_ready", b - 1))
                nc.tensor.matmul(psT[:, b % 2, :], w("L2x_wq", b * 128, b * 128 + 128), xmT[:, :],
                                 start=True, stop=True).then_inc(sem["q_psum"], 1)
            pe.wait_ge(*at("q_ready", 8))
            pe.wait_ge(*at("k_ready", 8))
            pe.wait_ge(*at("v_ready", 8))
            n = 4 * U

            def score(i):
                u, quarter = divmod(i, 4)
                if i >= 2:
                    pe.wait_ge(*at("s_sub", i - 1))
                for j in range(4):
                    h = quarter * 4 + j
                    rs = slice(64 * (h % 2), 64 * (h % 2) + 64)
                    ins = nc.tensor.matmul(psS[i % 2][:, h % 2, (j // 2) * SC:(j // 2 + 1) * SC],
                                           qT8[rs, h // 2, u * S:(u + 1) * S],
                                           kT8[rs, h // 2, u * SC:(u + 1) * SC], start=True, stop=True)
                ins.then_inc(sem["s_psum"], 1)

            def turn(i):
                pe.wait_ge(*at("s_nrm", i + 1))
                if i >= 2:
                    pe.wait_ge(*at("pt_ready", i - 1))
                for j in range(4):
                    ins = nc.tensor.transpose(psT[0:SC, i % 2, j * S:(j + 1) * S],
                                              p4[:, i % 4, j * SC:(j + 1) * SC], ident)
                ins.then_inc(sem["pt_psum"], 1)

            def value(i):
                u, quarter = divmod(i, 4)
                pe.wait_ge(*at("pt_ready", i + 1))
                if i >= 1:
                    pe.wait_ge(*at("oT_ready", i))
                for j in range(4):
                    h = quarter * 4 + 2 * (j % 2) + j // 2
                    c0 = (j % 2) * S
                    ins = nc.tensor.matmul(psB[64 * (h % 2):64 * (h % 2) + 64, c0:c0 + S],
                                           v8[0:SC, u, h * DX:(h + 1) * DX], pT4[0:SC, i % 4, j, :],
                                           start=True, stop=True)
                ins.then_inc(sem["o_psum"], 1)

            def out(u):
                pe.wait_ge(*at("oT_ready", 4 * u + 4))
                for b in range(8):
                    nc.tensor.matmul(un(psA, u), fT[:, u % 2, :, :].rearrange("p a t -> p (a t)")[:, b * S:(b + 1) * S],
                                     w("L2x_wo", b * 128, b * 128 + 128), start=(b == 0), stop=False)
                return nc.tensor.matmul(un(psA, u), ones_row, row("L2x_bo"), start=False, stop=True)

            for t in range(n + 5):
                if t < n:
                    score(t)
                if 2 <= t < n + 2:
                    turn(t - 2)
                if 3 <= t < n + 3:
                    value(t - 3)
                if t >= 8 and t % 4 == 0:
                    ins = out(t // 4 - 2)
            ins.then_inc(sem["y_psum"], 1)

        def l2_xattn_act(act, at, g):
            for b in range(8):
                act.wait_ge(*at("k_psum", b + 1))
                nc.scalar.copy(kT8[:, b, :], psS[0][:, b % 2, 0:U * SC]).then_inc(sem["k_ready"], 1)
            for n in range(8):
                u, c = divmod(n, 2)
                act.wait_ge(*at("v_psum", n + 1))
                nc.scalar.copy(v8[0:SC, u, c * 512:(c + 1) * 512], psS[1][0:SC, c, :]).then_inc(sem["v_ready"], 1)
            act.wait_ge(*at("xnT_psum", 1))
            nc.scalar.activation(xmT[:, :], psA[:, :], ACT.Identity, bias=col("L2x_b"),
                                 scale=col("L2x_g")).then_inc(sem["xnT_ready"], 1)
            for b in range(8):
                act.wait_ge(*at("q_psum", b + 1))
                nc.scalar.mul(qT8[:, b, :], psT[:, b % 2, :], float(DX) ** -0.5).then_inc(sem["q_ready"], 1)
            n = 4 * U
            for t in range(n + 4):
                if t >= 4:
                    i = t - 4
                    u, quarter = divmod(i, 4)
                    act.wait_ge(*at("o_psum", i + 1))
                    dst = fT[:, u % 2, :, :].rearrange("p a t -> p (a t)")[:, quarter * 256:(quarter + 1) * 256]
                    nc.scalar.copy(dst, psB[:, 0:256]).then_inc(sem["oT_ready"], 1)
                if 2 <= t < n + 2:
                    i = t - 2
                    act.wait_ge(*at("pt_psum", i + 1))
                    if i >= 4:
                        act.wait_ge(*at("o_psum", i - 3))
                    nc.scalar.copy(pT4[0:SC, i % 4, :, :].rearrange("p j s -> p (j s)"),
                                   psT[0:SC, i % 2, :]).then_inc(sem["pt_ready"], 1)
                if t < n:
                    act.wait_ge(*at("s_sub", t + 1))
                    pv = p4[:, t % 4, 0:4 * SC]
                    nc.scalar.activation(pv, pv, ACT.Exp).then_inc(sem["p_ready"], 1)

        def l2_xattn_dve(dve, at, g):
            norm_in_dve(dve, at, g)
            norm_dve(dve, at, 1, lambda u: un(xn, u), lambda u: un(xm, u), after=lambda u: at("xn_ready", u + 1))
            n = 4 * U

            def softmax(i):
                k = i % 2
                sv = psS[k][:, :, 0:2 * SC].rearrange("p b (j k) -> p b j k", j=2)
                mx = smx[:, k, 0:4].rearrange("p (b j) -> p b j", b=2)
                pv = p4[:, i % 4, 0:4 * SC].rearrange("p (b j k) -> p b j k", b=2, j=2)
                dve.wait_ge(*at("s_psum", i + 1))
                nc.vector.tensor_reduce(mx, sv, AX.X, ALU.max).then_inc(sem["s_max"], 1)
                dve.wait_ge(*at("s_max", i + 1))
                if i >= 4:
                    dve.wait_ge(*at("pt_psum", i - 3))
                nc.vector.tensor_tensor(pv, sv, mx.unsqueeze(3).broadcast_to([128, 2, 2, SC]),
                                        ALU.subtract).then_inc(sem["s_sub"], 1)

            def normalise(i):
                k = i % 2
                pv = p4[:, i % 4, 0:4 * SC].rearrange("p (j k) -> p j k", j=4)
                dve.wait_ge(*at("p_ready", i + 1))
                nc.vector.tensor_reduce(rec[:, k, 0:4], pv, AX.X, ALU.add).then_inc(sem["s_sum"], 1)
                dve.wait_ge(*at("s_sum", i + 1))
                nc.vector.reciprocal(rec[:, k, 4:8], rec[:, k, 0:4]).then_inc(sem["s_rec"], 1)
                dve.wait_ge(*at("s_rec", i + 1))
                nc.vector.tensor_tensor(pv, pv, rec[:, k, 4:8].unsqueeze(2).broadcast_to([128, 4, SC]),
                                        ALU.mult).then_inc(sem["s_nrm"], 1)

            for t in range(n + 1):
                if t < n:
                    softmax(t)
                if t >= 1:
                    normalise(t - 1)
            dve.wait_ge(*at("y_psum", 1))
            nc.vector.scalar_tensor_tensor(out=x[:, bass.ts(g, GT)], in0=psA[:, :], scalar=gate[:, 1:2],
                                           in1=xg[:, :], op0=ALU.mult, op1=ALU.add).then_inc(sem["x_done"], 1)

        def l2_xattn_pool(pool, at, g):
            ctx_pool(pool, at, g)
            norm_pool(pool, at, 0)
            norm_pool(pool, at, 1)

        def l2_ffn_pe(pe, at, g):
            flip_pe(pe, at, 0, xn, "xn_ready", 0)
            pe.wait_ge(*at("xnT_ready", 1))
            nc.tensor.matmul(psB[0:32, :], w("L2f_u1"), xnT[:, :], start=True, stop=True).then_inc(sem["q_psum"], 1)
            pe.wait_ge(*at("q_ready", 1))
            for b in range(4):
                nc.tensor.matmul(psS[b // 2][:, b % 2, :], w("L2f_v1", b * 128, b * 128 + 128)[0:32, :], qT[0:32, :],
                                 start=True, stop=True).then_inc(sem["f_psum"], 1)
            for b in range(4):
                pe.wait_ge(*at("f_ready", b + 1))
                ins = nc.tensor.matmul(psB[0:32, :], w("L2f_u2", b * 32, b * 32 + 32), fT[:, 0, b, :],
                                       start=(b == 0), stop=(b == 3))
            ins.then_inc(sem["o_psum"], 1)
            pe.wait_ge(*at("oT_ready", 1))
            for u in range(U):
                nc.tensor.matmul(un(psA, u), oT[0:32, u * S:(u + 1) * S], w("L2f_v2")[0:32, :], start=True, stop=False)
                ins = nc.tensor.matmul(un(psA, u), ones_row, row("L2f_b2"), start=False, stop=True)
            ins.then_inc(sem["y_psum"], 1)

        def l2_ffn_act(act, at, g):
            flip_act(act, at, 0, xnT)
            act.wait_ge(*at("q_psum", 1))
            nc.scalar.copy(qT[0:32, :], psB[0:32, :]).then_inc(sem["q_ready"], 1)
            for b in range(4):
                act.wait_ge(*at("f_psum", b + 1))
                nc.scalar.activation(fT[:, 0, b, :], psS[b // 2][:, b % 2, :], ACT.Gelu_apprx_tanh,
                                     bias=col("L2f_b1", b)).then_inc(sem["f_ready"], 1)
            act.wait_ge(*at("o_psum", 1))
            nc.scalar.copy(oT[0:32, :], psB[0:32, :]).then_inc(sem["oT_ready"], 1)

        def simple_dve(dve, at, g):
            norm_in_dve(dve, at, g)
            residual_dve(dve, at, g)

        def l3_attn_pe(pe, at, g):
            flip_pe(pe, at, 0, xn, "xn_ready", 0)
            pe.wait_ge(*at("xnT_ready", 1))
            nc.tensor.matmul(psB[:, :], w("L3a_wqkv", 0, 128), xnT[:, :], start=True, stop=True).then_inc(sem["q_psum"], 1)
            for half in range(2):
                for u in (2 * half, 2 * half + 1):
                    ins = nc.tensor.matmul(psS[half][:, 0, (u % 2) * 256:(u % 2) * 256 + 256], un(xnT, u),
                                           w("L3a_wqkv", 128, 384), start=True, stop=True)
                ins.then_inc(sem["k_psum"], 1)
            for u in range(U):
                pe.wait_ge(*at("k_ready", u // 2 + 1))
                pe.wait_ge(*at("v_ready", u // 2 + 1))
                if u >= 2:
                    pe.wait_ge(*at("kv_ready", 2 * u - 2))
                nc.tensor.matmul(psT[:, u % 2, 0:D], fT[:, 0, u // 2, (u % 2) * 256:(u % 2) * 256 + 128],
                                 fT[:, 0, u // 2, (u % 2) * 256 + 128:(u % 2) * 256 + 256],
                                 start=True, stop=True)
                nc.tensor.matmul(psT[:, u % 2, D:D + 2], fT[:, 0, u // 2, (u % 2) * 256:(u % 2) * 256 + 128],
                                 ones[:, 0:2], start=True, stop=True).then_inc(sem["s_psum"], 1)
            pe.wait_ge(*at("q_ready", 1))
            for u in range(U):
                pe.wait_ge(*at("kv_ready", 2 * u + 2))
                nc.tensor.matmul(psS[u // 2][:, 1, (u % 2) * 256:(u % 2) * 256 + D + H], un(qT, u),
                                 kvm[:, u % 2, :], start=True, stop=True).then_inc(sem["o_psum"], 1)
            project_pe(pe, at, w("L3a_wo"), None)

        def l3_attn_act(act, at, g):
            flip_act(act, at, 0, xnT)
            act.wait_ge(*at("elu_min", 1))
            nc.scalar.activation(rope1[:, 0, :], rope1[:, 0, :], ACT.Exp).then_inc(sem["elu_exp"], 1)
            for half in range(2):
                act.wait_ge(*at("elu_min", half + 2))
                dst = fT[:, 0, half, :].rearrange("p (u n) -> p u n", u=2)[:, :, 128:256]
                src = psS[half][:, 0, :].rearrange("p (u n) -> p u n", u=2)[:, :, 128:256]
                nc.scalar.copy(dst, src).then_inc(sem["v_ready"], 1)
                k = rope2[:, half, 0:256]
                nc.scalar.activation(k, k, ACT.Exp).then_inc(sem["elu_exp"], 1)
            project_act(act, at, None)

        def l3_attn_dve(dve, at, g):
            norm_in_dve(dve, at, g)
            dve.wait_ge(*at("q_psum", 1))
            nc.vector.tensor_scalar(rope1[:, 0, :], psB[:, :], 0.0, None, ALU.min).then_inc(sem["elu_min"], 1)
            for half in range(2):
                dve.wait_ge(*at("k_psum", half + 1))
                src = psS[half][:, 0, :].rearrange("p (u n) -> p u n", u=2)[:, :, 0:128]
                nc.vector.tensor_scalar(rope2[:, half, 0:256].rearrange("p (u n) -> p u n", u=2), src, 0.0, None,
                                        ALU.min).then_inc(sem["elu_min"], 1)
            dve.wait_ge(*at("elu_exp", 1))
            nc.vector.scalar_tensor_tensor(out=qT[:, :], in0=psB[:, :], scalar=0.0, in1=rope1[:, 0, :],
                                           op0=ALU.max, op1=ALU.add).then_inc(sem["q_ready"], 1)
            for half in range(2):
                dve.wait_ge(*at("v_ready", half + 1))
                dve.wait_ge(*at("elu_exp", half + 2))
                src = psS[half][:, 0, :].rearrange("p (u n) -> p u n", u=2)[:, :, 0:128]
                dst = fT[:, 0, half, :].rearrange("p (u n) -> p u n", u=2)[:, :, 0:128]
                nc.vector.scalar_tensor_tensor(out=dst, in0=src, scalar=0.0,
                                               in1=rope2[:, half, 0:256].rearrange("p (u n) -> p u n", u=2),
                                               op0=ALU.max, op1=ALU.add).then_inc(sem["k_ready"], 1)
            for u in range(U):
                dve.wait_ge(*at("s_psum", u + 1))
                if u >= 2:
                    dve.wait_ge(*at("o_psum", u - 1))
                nc.vector.tensor_tensor(kvm[:, u % 2, 0:D], psT[:, u % 2, 0:D], bdiag, ALU.mult).then_inc(sem["kv_ready"], 1)
                nc.vector.tensor_scalar(kvm[:, u % 2, D:D + H], bdiag16, psT[:, u % 2, D:D + 1], None,
                                        ALU.mult).then_inc(sem["kv_ready"], 1)
            for u in range(U):
                dve.wait_ge(*at("o_psum", 2 * (u // 2) + 2))
                o = psS[u // 2][:, 1, (u % 2) * 256:(u % 2) * 256 + D + H]
                nc.vector.tensor_scalar(rec[:, u % 2, :], o[:, D:D + H], 1e-6, None, ALU.max).then_inc(sem["o_recip"], 1)
                dve.wait_ge(*at("o_recip", 2 * u + 1))
                nc.vector.reciprocal(rec[:, u % 2, :], rec[:, u % 2, :]).then_inc(sem["o_recip"], 1)
                dve.wait_ge(*at("o_recip", 2 * u + 2))
                nc.vector.tensor_tensor(un(on, u).rearrange("p (h e) -> p h e", h=H),
                                        o[:, 0:D].rearrange("p (h e) -> p h e", h=H),
                                        rec[:, u % 2, :].unsqueeze(2).broadcast_to([128, H, DH]),
                                        ALU.mult).then_inc(sem["o_ready"], 1)
            residual_dve(dve, at, g)

        def l3_xattn_pe(pe, at, g):
            pe.wait_ge(*at("ctx_ready", 1))
            nc.tensor.matmul(psS[0][:, 0, 0:U * SC], w("L3x_wk"), ctxg[:, :], start=True,
                             stop=True).then_inc(sem["k_psum"], 1)
            for u in range(U):
                ins = nc.tensor.matmul(psS[1][0:SC, 0, u * 128:(u + 1) * 128], ctxg[:, u * SC:(u + 1) * SC],
                                       w("L3x_wv"), start=True, stop=True)
            ins.then_inc(sem["v_psum"], 1)
            flip_pe(pe, at, 0, xn, "xn_ready", 0)
            pe.wait_ge(*at("xnT_ready", 1))
            nc.tensor.matmul(psB[:, :], w("L3x_wq"), xnT[:, :], start=True, stop=True).then_inc(sem["q_psum"], 1)
            pe.wait_ge(*at("q_ready", 1))
            pe.wait_ge(*at("k_ready", 1))
            for u in range(U):
                ins = nc.tensor.matmul(psS[0][:, 1, u * SC:(u + 1) * SC], un(qT, u), kTr[:, u * SC:(u + 1) * SC],
                                       start=True, stop=True)
            ins.then_inc(sem["s_psum"], 1)
            pe.wait_ge(*at("s_nrm", 1))
            for u in range(U):
                ins = nc.tensor.transpose(psT[0:SC, 0, u * S:(u + 1) * S], p[:, 0, u * SC:(u + 1) * SC], ident)
            ins.then_inc(sem["pt_psum"], 1)
            pe.wait_ge(*at("pt_ready", 1))
            pe.wait_ge(*at("v_ready", 1))
            for u in range(U):
                ins = nc.tensor.matmul(un(psB, u), xm[0:SC, u * 128:(u + 1) * 128], pT[0:SC, 0, u, :],
                                       start=True, stop=True)
            ins.then_inc(sem["oT_psum"], 1)
            rows_pe(pe, at, oT, w("L3x_wo"), row("L3x_bo"), at("oT_ready", 1))

        def l3_xattn_act(act, at, g):
            act.wait_ge(*at("k_psum", 1))
            nc.scalar.copy(kTr[:, 0:U * SC], psS[0][:, 0, 0:U * SC]).then_inc(sem["k_ready"], 1)
            act.wait_ge(*at("v_psum", 1))
            nc.scalar.copy(xm[0:SC, :], psS[1][0:SC, 0, :]).then_inc(sem["v_ready"], 1)
            flip_act(act, at, 0, xnT)
            act.wait_ge(*at("q_psum", 1))
            nc.scalar.activation(qT[:, :], psB[:, :], ACT.Identity, bias=col("L3x_bq")).then_inc(sem["q_ready"], 1)
            act.wait_ge(*at("s_sub", 1))
            nc.scalar.activation(p[:, 0, 0:U * SC], p[:, 0, 0:U * SC], ACT.Exp,
                                 scale=float(np.float32(1.0) / np.sqrt(np.float32(D)))).then_inc(sem["p_ready"], 1)
            act.wait_ge(*at("pt_psum", 1))
            nc.scalar.copy(pT[0:SC, 0, 0:4, :].rearrange("p j s -> p (j s)"), psT[0:SC, 0, :]).then_inc(sem["pt_ready"], 1)
            project_act(act, at, col("L3x_bv"))

        def l3_xattn_dve(dve, at, g):
            norm_in_dve(dve, at, g)
            sv = psS[0][:, 1, 0:U * SC].rearrange("p (u k) -> p u k", u=U)
            pv = p[:, 0, 0:U * SC].rearrange("p (u k) -> p u k", u=U)
            dve.wait_ge(*at("s_psum", 1))
            nc.vector.tensor_reduce(smx[:, 0, 0:U], sv, AX.X, ALU.max).then_inc(sem["s_max"], 1)
            dve.wait_ge(*at("s_max", 1))
            nc.vector.tensor_tensor(pv, sv, smx[:, 0, 0:U].unsqueeze(2).broadcast_to([128, U, SC]),
                                    ALU.subtract).then_inc(sem["s_sub"], 1)
            dve.wait_ge(*at("p_ready", 1))
            nc.vector.tensor_reduce(rec[:, 0, 0:U], pv, AX.X, ALU.add).then_inc(sem["s_sum"], 1)
            dve.wait_ge(*at("s_sum", 1))
            nc.vector.reciprocal(rec[:, 0, 4:8], rec[:, 0, 0:4]).then_inc(sem["s_rec"], 1)
            dve.wait_ge(*at("s_rec", 1))
            nc.vector.tensor_tensor(pv, pv, rec[:, 0, 4:8].unsqueeze(2).broadcast_to([128, U, SC]),
                                    ALU.mult).then_inc(sem["s_nrm"], 1)
            residual_dve(dve, at, g)

        PROGRAM = {
            "L0_attn_ff": (l0_ff_pe, l0_ff_act, l0_ff_dve, l0_ff_pool),
            "L0_ffn": (l0_ffn_pe, l0_ffn_act, l0_ffn_dve, norm_only_pool),
            "L1_ffn": (l1_ffn_pe, l1_ffn_act, l1_ffn_dve, l1_ffn_pool),
            "L2_attn_pick": (pick_pe, pick_act, pick_dve, norm_only_pool),
            "L2_xattn": (l2_xattn_pe, l2_xattn_act, l2_xattn_dve, l2_xattn_pool),
            "L2_ffn": (l2_ffn_pe, l2_ffn_act, simple_dve, norm_only_pool),
            "L3_attn": (l3_attn_pe, l3_attn_act, l3_attn_dve, norm_only_pool),
            "L3_xattn": (l3_xattn_pe, l3_xattn_act, l3_xattn_dve, cross_pool),
            "L3_ffn": (l3_ffn_pe, l3_ffn_act, l3_ffn_dve, norm_only_pool),
        }

        @block.tensor
        def _(pe):
            pe.wait_ge(first_in, 16)
            pe.wait_ge(setup_v, 1)
            pe.wait_ge(setup_g, 1)
            for b in BLOCKS:
                if b == "L0_attn_ff":
                    pe.wait_ge(small_in, 16 * SMALL)
                if b == "L1_ffn":
                    pe.wait_ge(loaded[b], 16)
                    pe.wait_ge(sem["x_done"], BASE[b]["x_done"])
                    for i in range(6):
                        bank = psS[i // 4][:, 0, (i % 4) * 128:(i % 4) * 128 + 128]
                        ins = nc.tensor.matmul(bank, w("L1f_la", i * 128, i * 128 + 128)[0:32, :],
                                               w("L1f_lb", i * 128, i * 128 + 128)[0:32, :], start=True, stop=True)
                    ins.then_inc(lora_psum, 1)
                    pe.wait_ge(setup_v, 3)
                if b in loaded and b != "L0_attn":
                    pe.wait_ge(loaded[b], 16)
                if b == "L0_attn_ff":
                    pe.wait_ge(loaded["L0_attn"], 16)
                if b == "L2_attn_pick":
                    pe.wait_ge(loaded["L2_attn"], 16)
                if b in HEADS_OF:
                    run_heads(pe, b, HEADS_PROGRAM[0], HEADS_OF[b])
                    continue
                with pe.Fori(0, NG) as g:
                    PROGRAM[b][0](pe, Counts(b, g), g)

        @block.scalar
        def _(act):
            act.wait_ge(first_in, 16)
            act.wait_ge(setup_g, 1)
            for b in BLOCKS:
                if b == "L0_attn_ff":
                    act.wait_ge(small_in, 16 * SMALL)
                    nc.scalar.activation(gate[:, 1:2], gate[:, 0:1], ACT.Tanh).then_inc(setup_a, 1)
                if b == "L0_xattn":
                    act.wait_ge(setup_g, SETUP_G)
                if b in HEADS_OF:
                    run_heads(act, b, HEADS_PROGRAM[1], HEADS_OF[b])
                    continue
                with act.Fori(0, NG) as g:
                    PROGRAM[b][1](act, Counts(b, g), g)

        def setup_pool(pool):
            pool.wait_ge(small_in, 16 * SMALL)
            for i, pre in enumerate(KBIAS):
                h4 = heads4s if pre == "L0x" else heads4
                nc.gpsimd.tensor_scalar(kb4[:, i, :], h4, col(pre + "_bk"), None, ALU.mult).then_inc(setup_g, 1)
            nc.gpsimd.tensor_scalar(cmask[:, :], pad_u8, -3.0e38, 4.0, ALU.mult, ALU.mult).then_inc(setup_g, 1)
            pool.wait_ge(setup_g, 5)
            nc.gpsimd.tensor_tensor(cmask[:, :].rearrange("p (b k) -> p b k", b=NB),
                                    cmask[:, :].rearrange("p (b k) -> p b k", b=NB),
                                    amask[:, :].unsqueeze(1).broadcast_to([128, NB, SC]),
                                    ALU.add).then_inc(setup_g, 1)
            nc.gpsimd.tensor_copy(idx_f[:, 0, :], idx_i[:, :]).then_inc(setup_g, 1)
            pool.wait_ge(setup_g, 7)
            nc.gpsimd.tensor_scalar(idx_f[:, 1, :], idx_f[:, 0, :], 0.0, float(S), ALU.is_lt,
                                    ALU.mult).then_inc(setup_g, 1)
            pool.wait_ge(setup_g, 8)
            nc.gpsimd.tensor_tensor(idx_f[:, 0, :], idx_f[:, 0, :], idx_f[:, 1, :], ALU.add).then_inc(setup_g, 1)
            pool.wait_ge(setup_g, 9)
            nc.gpsimd.tensor_scalar(idx_f[:, 1, :], idx_f[:, 0, :], 0.0, float(S - 1), ALU.max,
                                    ALU.min).then_inc(setup_g, 1)
            pool.wait_ge(setup_g, 10)
            nc.gpsimd.tensor_scalar(onehot[:, :], idx_f[:, 1, :], part, None, ALU.is_equal).then_inc(setup_g, 1)
            nc.gpsimd.tensor_scalar(wt[:, :], qw, 1.0 / 7.5, -1.0, ALU.mult, ALU.add).then_inc(setup_g, 1)
            pool.wait_ge(setup_g, 12)
            nc.gpsimd.tensor_tensor(wt[:, :], wt[:, :], scl, ALU.mult).then_inc(setup_g, 1)

        @block.gpsimd
        def _(pool):
            nc.gpsimd.memset(neghalf[:, :], -0.5)
            nc.gpsimd.memset(mean_w[:, :], 1.0 / S)
            nc.gpsimd.memset(vx_all[:, :, :], 1.0).then_inc(setup_g, 1)
            pool.wait_ge(setup_g, 1)
            for b in BLOCKS:
                if b == "L0_attn_ff":
                    setup_pool(pool)
                if b in HEADS_OF:
                    run_heads(pool, b, HEADS_PROGRAM[3], HEADS_OF[b])
                    continue
                with pool.Fori(0, NG) as g:
                    PROGRAM[b][3](pool, Counts(b, g), g)

        @block.vector
        def _(dve):
            nc.vector.memset(ones[:, :], 1.0)
            dve.wait_ge(first_in, 16)
            nc.vector.tensor_copy(window_bf[:, :], const("window"))
            nc.vector.tensor_copy(ident_bf[:, :], ident).then_inc(setup_v, 1)
            dve.wait_ge(setup_g, 1)
            dve.wait_ge(x_in, 16)
            dve.sem_inc(sem["x_done"], 4)
            for b in BLOCKS:
                if b == "L0_attn_ff":
                    dve.wait_ge(small_in, 16 * SMALL)
                    dve.wait_ge(setup_a, 1)
                if b == "L0_xattn":
                    dve.wait_ge(setup_g, SETUP_G)
                if b == "L1_ffn":
                    dve.wait_ge(lora_psum, 1)
                    nc.vector.tensor_tensor(wt[:, 0:512], wt[:, 0:512], psS[0][:, 0, :], ALU.add).then_inc(setup_v, 1)
                    nc.vector.tensor_tensor(wt[:, 512:768], wt[:, 512:768], psS[1][:, 0, 0:256],
                                            ALU.add).then_inc(setup_v, 1)
                if b in HEADS_OF:
                    run_heads(dve, b, HEADS_PROGRAM[2], HEADS_OF[b])
                    continue
                with dve.Fori(0, NG) as g:
                    PROGRAM[b][2](dve, Counts(b, g), g)


def block_cols(wm, n):
    k, c = wm.shape
    return wm.reshape(n, k // n, c).transpose(1, 0, 2).reshape(k // n, n * c)


def pad_rows(a):
    return np.concatenate([a, np.zeros((128 - a.shape[0], a.shape[1]), a.dtype)], axis=0)


ROT = np.array([c + 1 - 2 * (c % 2) for c in range(D)])


def shape_constants():
    i = np.arange(128)
    cos = np.ones((128, S), np.float32)
    sin = np.zeros((128, S), np.float32)
    tok = np.arange(S)
    for c in range(128):
        e = c % DH
        if e < 6:
            pos = [np.zeros(S), tok // 16, tok % 16][e // 2].astype(np.float32)
            cos[c], sin[c] = np.cos(pos), np.sin(pos)
            if e % 2 == 0:
                sin[c] = -sin[c]
    parts = dict(
        ident=np.eye(128), bdiag=(i[:, None] // DH == i[None, :] // DH),
        bdiag16=(i[:, None] // DH == np.arange(H)[None, :]), heads4=((i[:, None] // DH) % 4 == np.arange(4)[None, :]),
        heads4s=((i[:, None] // DH) % 4 == np.arange(4)[None, :]) * SCALE8, cos=cos, sin=sin, window=np.where(np.abs(i[:, None] - i[None, :]) <= WINDOW, 0.0, -1e9),
        quarters=(i[:, None] // 32 == np.arange(4)[None, :]), rank=np.broadcast_to(8.0 - np.arange(8), (128, 8)), part=i[:, None])
    return np.concatenate([np.asarray(parts[n], np.float32) for n, _ in CONSTS], axis=1)


def lay_out(v):
    wp = {
        "L0a_w1": v["L0_attn_W1"], "L0a_w2": block_cols(v["L0_attn_W2"], 4),
        "L0x_wq": v["L0_xattn_Wq"].T, "L0x_wk": v["L0_xattn_Wk"].T, "L0x_wv": v["L0_xattn_Wv"].T,
        "L0x_wo": v["L0_xattn_Wout"].T,
        "L0f_rw": v["L0_ffn_router_w"], "L0f_w1": v["L0_ffn_w1"].transpose(1, 0, 2).reshape(D, -1),
        "L0f_w2": block_cols(v["L0_ffn_w2"].reshape(E0 * F0, D), E0 * 4),
        "L1a_wqr": v["L1_attn_Wq"][:, ROT], "L1a_wkr": v["L1_attn_Wk"][:, ROT],
        "L1a_wq": v["L1_attn_Wq"], "L1a_wk": v["L1_attn_Wk"], "L1a_wv": v["L1_attn_Wv"], "L1a_wo": v["L1_attn_Wo"],
        "L1x_wq": v["L1_xattn_Wq"], "L1x_wk": v["L1_xattn_Wk"], "L1x_wv": v["L1_xattn_Wv"],
        "L1x_wo": v["L1_xattn_Wo"],
        "L1f_la": pad_rows(v["L1_ffn_lora_a"].transpose(1, 0, 2).reshape(32, -1)),
        "L1f_lb": pad_rows(v["L1_ffn_lora_b"].transpose(2, 0, 1).reshape(32, -1)),
        "L2a_wq": v["L2_attn_Wq"], "L2a_wk": v["L2_attn_Wk"], "L2a_wv": v["L2_attn_Wv"], "L2a_wo": v["L2_attn_Wo"],
        "L2x_wq": v["L2_xattn_w_q"], "L2x_wkv": v["L2_xattn_w_kv"], "L2x_wo": block_cols(v["L2_xattn_w_out"], 8),
        "L2f_u1": v["L2_ffn_U1"], "L2f_v1": pad_rows(v["L2_ffn_V1"]), "L2f_u2": block_cols(v["L2_ffn_U2"], 4),
        "L2f_v2": pad_rows(v["L2_ffn_V2"]),
        "L3a_wqkv": v["L3_attn_w_qkv"].T, "L3a_wo": v["L3_attn_w_out"].T,
        "L3x_wq": v["L3_xattn_Wq"].T, "L3x_wk": v["L3_xattn_Wk"].T, "L3x_wv": v["L3_xattn_Wv"].T,
        "L3x_wo": v["L3_xattn_Wo"].T,
        "L3f_wg": v["L3_ffn_wg"].T, "L3f_w1": v["L3_ffn_w1"].reshape(-1, D).T,
        "L3f_w3": v["L3_ffn_w3"].reshape(-1, D).T,
        "L3f_w2": block_cols(v["L3_ffn_w2"].transpose(0, 2, 1).reshape(E3 * F3, D), E3 * 2),
    }
    cp = {
        "L0a_g1": v["L0_attn_ln1_g"], "L0a_b1": v["L0_attn_ln1_b"], "L0a_fb": v["L0_attn_b1"],
        "L0x_bq": v["L0_xattn_bq"], "L0x_bk": v["L0_xattn_bk"], "L0x_bv": v["L0_xattn_bv"],
        "L0f_b1": v["L0_ffn_b1"], "L1a_bq": v["L1_attn_bq"], "L1a_bk": v["L1_attn_bk"], "L1a_bv": v["L1_attn_bv"],
        "L1a_bqr": v["L1_attn_bq"][ROT], "L1a_bkr": v["L1_attn_bk"][ROT],
        "L1x_bq": v["L1_xattn_bq"], "L1x_bk": v["L1_xattn_bk"], "L1x_bv": v["L1_xattn_bv"],
        "L1f_g": v["L1_ffn_ln_gamma"], "L1f_b": v["L1_ffn_ln_beta"],
        "L2a_bq": v["L2_attn_bq"], "L2a_bk": v["L2_attn_bk"], "L2a_bv": v["L2_attn_bv"],
        "L2x_g": v["L2_xattn_ln_gamma"], "L2x_b": v["L2_xattn_ln_beta"], "L2f_b1": v["L2_ffn_b1"],
        "L3x_bq": v["L3_xattn_bq"], "L3x_bv": v["L3_xattn_bv"],
    }
    rp = {
        "L0a_b2": v["L0_attn_b2"], "L0x_bo": v["L0_xattn_bout"], "L0f_rb": v["L0_ffn_router_b"],
        "L0f_b2": v["L0_ffn_b2"], "L1a_bo": v["L1_attn_bo"], "L1x_bo": v["L1_xattn_bo"],
        "L1f_bias": v["L1_ffn_biases"], "L2a_bo": v["L2_attn_bo"], "L2x_bo": v["L2_xattn_b_out"],
        "L2f_b2": v["L2_ffn_b2"], "L3x_bo": v["L3_xattn_bo"],
    }
    return dict(
        x=v["x"].transpose(1, 0, 2).reshape(S, NB * D),
        ctxT=v["ctx_1024"].transpose(2, 0, 1).reshape(D, NB * SC),
        consts=shape_constants(),
        cols=np.concatenate([cp[n].reshape(-1, 128).T for n, _ in COLS], axis=1),
        rows=np.concatenate([rp[n].reshape(1, -1) for n, _ in ROWS], axis=1),
        w=np.concatenate([wp[n] for _, ps in WIDTHS for n, _ in ps], axis=1),
        amask=v["mask_SxS2_ff0"], pad=np.ascontiguousarray(v["mask_BxS2_bf0"]).reshape(-1).view(np.int32),
        ln2_g=v["L0_attn_ln2_g"], ln2_b=v["L0_attn_ln2_b"], gate=v["L2_xattn_gate"],
        idx=v["L2_attn_sample_idx"],
        qw=v["L1_ffn_qweights"].transpose(2, 0, 1).reshape(D, -1),
        scl=np.repeat(v["L1_ffn_scales"].transpose(2, 0, 1), 16, axis=0).reshape(D, -1),
    )


def kernel(**inputs):
    import concourse.bacc as _bacc
    from concourse.bass_utils import run_bass_kernel_spmd as _run

    arrays = {n: np.ascontiguousarray(a) for n, a in lay_out({k: np.asarray(a) for k, a in inputs.items()}).items()}
    nc = _bacc.Bacc("TRN2", target_bir_lowering=False, num_devices=1)
    io = {n: nc.dram_tensor("in_" + n, a.shape, mybir.dt.from_np(a.dtype), kind="ExternalInput").ap()
          for n, a in arrays.items()}
    io["out"] = nc.dram_tensor("out", (S, NB * D), F32, kind="ExternalOutput").ap()
    build(nc, io)
    r = _run(nc, [{"in_" + n: a for n, a in arrays.items()}], core_ids=[0])
    got = r.results[0]["out"]
    return np.ascontiguousarray(got.reshape(S, NB, D).transpose(1, 0, 2))
```

```python
from contextlib import ExitStack

import numpy as np
import concourse.bass as bass
from concourse import mybir

F32 = mybir.dt.float32
BF16 = mybir.dt.bfloat16
I32 = mybir.dt.int32
U8 = mybir.dt.uint8
ALU = mybir.AluOpType
ACT = mybir.ActivationFunctionType
AX = mybir.AxisListType

NB, S, D = 16, 128, 128
SC = 77
H, DH = 16, 8
U = 4
UA = 2
GA = UA * S
NG = NB // U
GT = U * S
WINDOW = 32
HX, DX = 16, 64
E0, F0 = 8, 512
E3, F3 = 8, 256
VXW = (H - 1) * (DH + 1) + 32
NSAMP = 35
NTOP = 25
EPS = 1e-5
SCALE8 = float(DH) ** -0.5
GONE = -3.0e38

WIDTHS = [
    ("L0_attn", [("L0a_w1", 512), ("L0a_w2", 512)]),
    ("L0_xattn", [("L0x_wq", 128), ("L0x_wk", 128), ("L0x_wv", 128), ("L0x_wo", 128)]),
    ("L0_ffn", [("L0f_rw", E0), ("L0f_w1", E0 * 2 * F0), ("L0f_w2", E0 * F0)]),
    ("L1_attn", [("L1a_wq", 128), ("L1a_wk", 128), ("L1a_wqr", 128), ("L1a_wkr", 128), ("L1a_wv", 128), ("L1a_wo", 128)]),
    ("L1_xattn", [("L1x_wq", 128), ("L1x_wk", 128), ("L1x_wv", 128), ("L1x_wo", 128)]),
    ("L1_ffn", [("L1f_la", 768), ("L1f_lb", 768)]),
    ("L2_attn", [("L2a_wq", 128), ("L2a_wk", 128), ("L2a_wv", 128), ("L2a_wo", 128)]),
    ("L2_xattn", [("L2x_wq", 1024), ("L2x_wkv", 2048), ("L2x_wo", 1024)]),
    ("L2_ffn", [("L2f_u1", 32), ("L2f_v1", 512), ("L2f_u2", 128), ("L2f_v2", 128)]),
    ("L3_attn", [("L3a_wqkv", 384), ("L3a_wo", 128)]),
    ("L3_xattn", [("L3x_wq", 128), ("L3x_wk", 128), ("L3x_wv", 128), ("L3x_wo", 128)]),
    ("L3_ffn", [("L3f_wg", E3), ("L3f_w1", E3 * F3), ("L3f_w3", E3 * F3), ("L3f_w2", E3 * F3)]),
]
WAT, WSPAN, _at = {}, {}, 0
for _block, _parts in WIDTHS:
    if _block == "L3_ffn":
        WHBM, WCOLS = _at + sum(n for _, n in _parts), _at
        _at = WSPAN["L0_ffn"][0]
    _first = _at
    for _name, _n in _parts:
        WAT[_name] = (_at, _n)
        _at += _n
    WSPAN[_block] = (_first, _at)
assert WSPAN["L3_ffn"][1] <= WSPAN["L0_ffn"][1]

COLS = [("L0a_g1", 1), ("L0a_b1", 1), ("L0a_fb", 4), ("L0x_bq", 1), ("L0x_bk", 1), ("L0x_bv", 1),
        ("L0f_b1", 64), ("L1a_bq", 1), ("L1a_bk", 1), ("L1a_bv", 1), ("L1a_bqr", 1), ("L1a_bkr", 1), ("L1x_bq", 1), ("L1x_bk", 1),
        ("L1x_bv", 1), ("L1f_g", 3), ("L1f_b", 3), ("L2a_bq", 1), ("L2a_bk", 1), ("L2a_bv", 1),
        ("L2x_g", 1), ("L2x_b", 1), ("L2f_b1", 4), ("L3x_bq", 1), ("L3x_bv", 1), ("L0f_b2", 128)]
ROWS = [("L0a_b2", 128), ("L0x_bo", 128), ("L0f_rb", E0), ("L1a_bo", 128),
        ("L1x_bo", 128), ("L1f_bias", 768), ("L2a_bo", 128), ("L2x_bo", 128), ("L2f_b2", 128),
        ("L3x_bo", 128)]
CONSTS = [("ident", 128), ("bdiag", 128), ("bdiag16", 16), ("heads4", 4), ("heads4s", 4), ("cos", 128),
          ("sin", 128), ("window", 128), ("quarters", 4), ("rank", 8), ("part", 1), ("drop", 2)]


def offsets(table):
    at, out = 0, {}
    for name, n in table:
        out[name] = (at, n)
        at += n
    return out, at


CAT, NCOLS = offsets(COLS)
RAT, NROWS = offsets(ROWS)
KAT, NCONST = offsets(CONSTS)

NORM = dict(xg_ready=1, stats=U, moments=U, vareps=1, rstd=1, xn_ready=U, xnT_psum=1, xnT_ready=1)
HEADS = dict(xg_ready=1, stats=UA, moments=UA, vareps=1, rstd=1, xn_ready=UA, xnT_psum=1, xnT_ready=1,
             k_ready=4, v_ready=1, s_psum=8, s_max=8, s_sub=8, p_ready=8, pt_psum=8, pt_ready=8, o_psum=8,
             ov_ready=8, ob_psum=8, qz_ready=4, o_recip=UA, o_ready=UA, x_done=1)
QKV = dict(q_psum=1, q_ready=1, k_psum=1, v_psum=1, oT_psum=1, oT_ready=1, y_psum=1)
PROJ = dict(oT_psum=1, oT_ready=1, y_psum=1, x_done=1)


def times(d, n):
    return {k: v * n for k, v in d.items()}


def merged(*parts):
    out = {}
    for p in parts:
        for k, v in p.items():
            out[k] = out.get(k, 0) + v
    return out


PRE = dict(stats=NB, moments=NB, vareps=1, rstd=1, xn_ready=NB, xnT_psum=NG, xnT_ready=NG, r_psum=1)
LN = dict(stats=U, moments=U, vareps=1, rstd=1, xn_ready=U)
LNT = dict(xnT_psum=1, xnT_ready=1)
EXPERTS0 = dict(gv_psum=E0 * 4, sg_ready=E0 * 4, h_ready=E0 * 4, ye_psum=E0, acc=E0 * U)
EXPERTS3 = dict(gv_psum=E3 * 2, sg_ready=E3 * 2, h_ready=E3 * 2, ye_psum=E3, acc=E3 * U)


def streams(*parts):
    one = merged(NORM, dict(g_done=1), *parts)
    return merged(one, {k + "2": v for k, v in one.items()}, dict(x_done=1))


STREAMED = ("L0_attn_ff", "L1_ffn", "L2_attn_pick", "L2_ffn", "L3_attn", "L3_xattn")
PER = {
    "L0_attn": merged(HEADS, dict(hold_ready=1)),
    "L0_attn_ff": streams(LN, dict(hold_ready=1, f_psum=4, f_ready=4, y_psum=1, h_res=2)),
    "L0_xattn": merged(HEADS, QKV, dict(ctx_ready=1, s_mask=8)),
    "L0_ffn_pre": merged(PRE, dict(r_step=5, pt_psum=NG, pt_ready=NG, y_psum=NG, x_done=NG)),
    "L0_ffn": merged(EXPERTS0, dict(xg_ready=2, x_done=1)),
    "L1_attn": merged(HEADS, {k: v for k, v in QKV.items() if k != "q_ready"}, dict(rope=6, k_psum=1)),
    "L1_xattn": merged(HEADS, QKV, dict(ctx_ready=1)),
    "L1_ffn": streams(times(LN, 3), times(LNT, 5), dict(y_psum=6, h_res=3)),
    "L2_attn_pick": streams(dict(q_psum=1, q_ready=1, smp_psum=2, smp_ready=5, smps_psum=4, smp_red=16,
                                 m_step=3, mT_psum=1, top=9, sel_psum=1, sel_ready=2)),
    "L2_attn": merged(HEADS, QKV, dict(vm_psum=1, vm_ready=1, o_mix=2 * UA)),
    "L2_xattn": merged(NORM, LN, dict(ctx_ready=1, q_psum=8, q_ready=8, k_psum=8, k_ready=8, v_psum=8,
                                           v_ready=8, s_psum=16, s_max=16, s_sub=16, p_ready=16, s_sum=16,
                                           s_rec=16, s_nrm=16, pt_psum=16, pt_ready=16, o_psum=16,
                                           oT_ready=16, y_psum=1, x_done=1)),
    "L2_ffn": streams(dict(q_psum=1, q_ready=1, f_psum=4, f_ready=4, o_psum=1, oT_ready=1, y_psum=1)),
    "L3_attn": streams(dict(q_psum=1, q_ready=1, k_psum=2, v_ready=2, elu_min=3, elu_exp=3, k_ready=2, s_psum=2,
                            kv_ready=6, o_psum=2, o_recip=4, o_ready=U, oT_psum=1, oT_ready=1, y_psum=1)),
    "L3_xattn": streams({n: 1 for n in ("ctx_ready", "q_psum", "q_ready", "k_psum", "k_ready", "v_psum", "v_ready",
                                        "s_psum", "s_max", "s_sub", "p_ready", "s_sum", "s_rec", "s_nrm", "pt_psum",
                                        "pt_ready", "oT_psum", "oT_ready", "y_psum")}),
    "L3_ffn_pre": merged(PRE, dict(r_step=16, g_step=3, r_exp=1, x_done=1)),
    "L3_ffn": merged(EXPERTS3, dict(xg_ready=2, x_done=1)),
}
LOADS = [b for b, _ in WIDTHS]
BLOCKS = (["L0_attn", "L0_attn_ff", "L0_xattn", "L0_ffn_pre"] + LOADS[2:6] + ["L2_attn_pick"] + LOADS[6:11]
          + ["L3_ffn_pre", "L3_ffn"])
GROUPS = {b: NB // UA if b in ("L0_attn", "L0_xattn", "L1_attn", "L1_xattn", "L2_attn") else 1 if b.endswith("_pre") else NG // 2 if b in STREAMED else NG
          for b in BLOCKS}
NAMES = sorted({k for d in PER.values() for k in d})
BASE, _sum = {}, {n: 0 for n in NAMES}
SETUP_COUNTS = dict(g_done=1, g_done2=1, x_done=4, h_ready=2, ye_psum=2, acc=2 * U)
_sum.update(SETUP_COUNTS)
for _b in BLOCKS:
    BASE[_b] = dict(_sum)
    for _k, _v in PER[_b].items():
        _sum[_k] += GROUPS[_b] * _v


def build(nc, io):
    with ExitStack() as ctx:
        def sb(name, shape, dt=F32):
            return ctx.enter_context(nc.sbuf_tensor(name, shape, dt))

        def psum(name, shape, dt=F32):
            return ctx.enter_context(nc.psum_tensor(name, shape, dt))

        sem = {n: ctx.enter_context(nc.semaphore(n)) for n in NAMES}
        loaded = {b: ctx.enter_context(nc.semaphore("loaded_" + b)) for b in LOADS}
        first_in = ctx.enter_context(nc.semaphore("first_in"))
        small_in = ctx.enter_context(nc.semaphore("small_in"))
        x_in = ctx.enter_context(nc.semaphore("x_in"))
        setup_v = ctx.enter_context(nc.semaphore("setup_v"))
        setup_g = ctx.enter_context(nc.semaphore("setup_g"))
        setup_a = ctx.enter_context(nc.semaphore("setup_a"))
        lora_psum = ctx.enter_context(nc.semaphore("lora_psum"))
        passed_v = ctx.enter_context(nc.semaphore("passed_v"))
        passed_t = ctx.enter_context(nc.semaphore("passed_t"))
        passed_g = ctx.enter_context(nc.semaphore("passed_g"))
        stored = ctx.enter_context(nc.semaphore("stored"))

        class Counts:

            def __init__(self, block, g, par=None, suffix=""):
                self.block, self.g, self.par, self.suffix = block, g, par, suffix

            def has(self, k, per=8):
                return not isinstance(self.g, int) or self.g * per + k > 0

            def __call__(self, name, k):
                name += self.suffix
                per, base = PER[self.block][name], BASE[self.block][name]
                return sem[name], self.g * per + (base + k)

        w_all = sb("w_all", [128, WCOLS])
        consts = sb("consts", [128, NCONST])
        cols = sb("cols", [128, NCOLS])
        rows = sb("rows", [3, NROWS])
        rows_bf = sb("rows_bf", [3, NROWS], BF16)
        ones_bf = sb("ones_bf", [3, 128], BF16)
        x = sb("x", [128, NB * D])
        ctxT = sb("ctxT", [128, NB * SC])
        ones = sb("ones", [128, 128])
        mean_w = sb("mean_w", [128, 128])
        neghalf = sb("neghalf", [128, NB])
        window_bf = sb("window_bf", [128, S], BF16)
        ident_bf = sb("ident_bf", [128, 128], BF16)
        g2b = sb("g2b", [128, 2, D])
        gate = sb("gate", [128, 2])
        kb4 = sb("kb4", [128, 3, 4])
        heads4s = consts[:, KAT["heads4s"][0]:KAT["heads4s"][0] + 4]
        amask = sb("amask", [128, SC])
        pad_words = sb("pad_words", [128, NB * SC // 4], I32)
        pad_u8 = pad_words[:, :].bitcast(U8)
        cmask = sb("cmask", [128, NB * SC])
        idx_i = sb("idx_i", [128, NSAMP], I32)
        idx_f = sb("idx_f", [128, 2, NSAMP])
        onehot = sb("onehot", [128, NSAMP])
        wt = sb("wt", [128, 768])

        xg = sb("xg", [128, GT])
        st = sb("st", [128, U, 6])
        mv = sb("mv", [128, U, 2])
        ve = sb("ve", [128, U])
        rstd = sb("rstd", [128, U])
        xn = sb("xn", [128, GT])
        xm = sb("xm", [128, GT])
        xnT = sb("xnT", [128, GT])
        xmT = sb("xmT", [128, GT])
        qT = sb("qT", [128, GT])
        kTx = sb("kTx", [128, U, 4, S])
        vx_all = sb("vx", [128, U, VXW])
        vx = vx_all[:, :, 0:H * (DH + 1)].rearrange("p u (h e) -> p u h e", h=H)
        smx = sb("smx", [128, 2, 8])
        p = sb("p", [128, 2, 8 * S])
        pT = sb("pT", [128, 2, 8, S])
        p4 = p[:, :, :].rearrange("p a (b k) -> p (a b) k", b=2)
        pT4 = pT[:, :, :, :].rearrange("p a (b j) s -> p (a b) j s", b=2)
        rec = sb("rec", [128, 2, H])
        on = sb("on", [128, GT])
        oT = sb("oT", [128, GT])
        on2, oT2 = on[:, 0:GA], oT[:, 0:GA]
        ctxg = sb("ctxg", [128, U * SC])
        ctxa = ctxg[:, :].rearrange("p (a k) -> p a k", a=2)
        xna, xnTa, qTa = [t[:, :].rearrange("p (a k) -> p a k", a=2) for t in (xn, xnT, qT)]
        fT = sb("fT", [128, 2, 4, GT])
        qz = fT[:, 0, :, :]
        ovT = xm[:, :].rearrange("p (i s) -> p i s", i=4)
        rope1, rope2 = fT[:, 1, 0:2, :], fT[:, 1, 2:4, :]
        sg = sb("sg", [128, 2, GT])
        qw = wt[:, :].bitcast(I32)
        scl = sg[:, :, :].rearrange("p a t -> p (a t)")[:, 0:768]
        acc = sb("acc", [128, GT])
        gates = sb("gates", [128, U, 8])
        gates_all = sb("gates_all", [128, NB, 8])
        rt = fT[:, 1, 0:2, :].rearrange("p a t -> p (a t)")[:, 0:6 * NB * 8].rearrange("p (i s e) -> p i s e", i=6, s=NB)
        rm = fT[:, 1, 2, 0:6 * NB].rearrange("p (i s) -> p i s", i=6)
        st16 = fT[:, 1, 3, 0:6 * NB].rearrange("p (s c) -> p s c", s=NB)
        mv16 = fT[:, 1, 3, 6 * NB:8 * NB].rearrange("p (s c) -> p s c", s=NB)
        ve16, rstd16 = fT[:, 1, 3, 8 * NB:9 * NB], fT[:, 1, 3, 9 * NB:10 * NB]
        xn_all = p[:, :, :].rearrange("p a n -> p (a n)")
        xnT_all = kTx[:, :, :, :].rearrange("p u j s -> p (u j s)")
        gT = pT[:, :, :, :].rearrange("p a j s -> p (a j s)")
        vmean = [on[:, GA:2 * GA], oT[:, GA:2 * GA]]
        sel_all = sb("sel_all", [128, 2, NB * H])

        a0 = WAT["L0f_w1"][0]
        qT8 = w_all[:, a0:a0 + 8 * GT].rearrange("p (b t) -> p b t", b=8)
        kT8 = w_all[:, a0 + 8 * GT:a0 + 8 * GT + 8 * U * SC].rearrange("p (b t) -> p b t", b=8)
        v8 = w_all[:, a0 + 7168:a0 + 7168 + U * 1024].rearrange("p (u n) -> p u n", u=U)
        hold = w_all[:, WAT["L2x_wkv"][0]:WAT["L2x_wkv"][0] + NB * D]
        assert 8 * GT + 8 * U * SC <= 7168 and a0 + 7168 + U * 1024 <= WSPAN["L0_ffn"][1]

        ps = psum("ps", [128, 8, 512])
        psS = [ps[:, 0:2, :], ps[:, 2:4, :]]
        psT = ps[:, 4:6, :]
        psA, psB = ps[:, 6, :], ps[:, 7, :]
        bankS, bankT, bankM = [ps[:, 0, :], ps[:, 1, :]], [ps[:, 2, :], ps[:, 3, :]], [ps[:, 6, :], ps[:, 7, :]]
        bankV, bankO = ps[:, 4, :], ps[:, 5, :]

        def w(name, a=0, b=None):
            at, n = WAT[name]
            return w_all[:, at + a:at + (n if b is None else b)]

        def col(name, i=0):
            return cols[:, CAT[name][0] + i:CAT[name][0] + i + 1]

        def row(name, a=0, b=None):
            at, n = RAT[name]
            return rows[0:1, at + a:at + (n if b is None else b)]

        def bias_pe(dst, name, n, a=0):
            at, _ = RAT[name]
            nc.tensor.matmul(dst[:, 0:n * D], ones_bf[:, :],
                             rows_bf[:, at + a:at + a + D].unsqueeze(1).broadcast_to([3, n, D]), start=True, stop=False)

        def const(name):
            at, n = KAT[name]
            return consts[:, at:at + n]

        ident, bdiag, bdiag16 = const("ident"), const("bdiag"), const("bdiag16")
        heads4, rank, part = const("heads4"), const("rank"), const("part")
        ones_row = ones[0:1, 0:128]

        def un(t, u):
            return t[:, u * 128:(u + 1) * 128]

        block = ctx.enter_context(nc.Block())
        SMALL = 10
        SETUP_G = 13

        @block.sync
        def _(sp):
            sp.dma_start(consts[:, :], io["consts"]).then_inc(first_in, 16)
            sp.dma_start(rows[:, :], io["rows3"]).then_inc(first_in, 16)
            sp.dma_start(x[:, :], io["x"]).then_inc(x_in, 16)
            sp.dma_start(cols[:, :], io["cols"]).then_inc(small_in, 16)
            a, z = WSPAN["L0_attn"]
            sp.dma_start(w_all[:, a:z], io["w"][:, a:z]).then_inc(loaded["L0_attn"], 16)
            sp.dma_start(amask[:, :], io["amask"]).then_inc(small_in, 16)
            sp.dma_start(pad_words[:, :], io["pad"].partition_broadcast(128)).then_inc(small_in, 16)
            sp.dma_start(g2b[:, 0, :], io["ln2_g"].partition_broadcast(128)).then_inc(small_in, 16)
            sp.dma_start(g2b[:, 1, :], io["ln2_b"].partition_broadcast(128)).then_inc(small_in, 16)
            sp.dma_start(gate[:, 0:1], io["gate"].partition_broadcast(128)).then_inc(small_in, 16)
            sp.dma_start(idx_i[:, :], io["idx"].partition_broadcast(128)).then_inc(small_in, 16)
            sp.dma_start(qw, io["qw"]).then_inc(small_in, 16)
            sp.dma_start(scl, io["scl"]).then_inc(small_in, 16)
            sp.dma_start(ctxT[:, :], io["ctxT"]).then_inc(small_in, 16)
            for b in LOADS:
                if b not in ("L0_attn", "L2_xattn", "L3_ffn"):
                    a, z = WSPAN[b]
                    sp.dma_start(w_all[:, a:z], io["w"][:, a:z]).then_inc(loaded[b], 16)
            sp.wait_ge(sem["x_done"], BASE["L0_xattn"]["x_done"])
            a, z = WSPAN["L2_xattn"]
            sp.dma_start(w_all[:, a:z], io["w"][:, a:z]).then_inc(loaded["L2_xattn"], 16)
            sp.wait_ge(sem["x_done"], BASE["L2_ffn"]["x_done"])
            a, z = WSPAN["L3_ffn"]
            sp.dma_start(w_all[:, a:z], io["w"][:, WCOLS:WHBM]).then_inc(loaded["L3_ffn"], 16)
            sp.wait_ge(sem["x_done"], _sum["x_done"])
            sp.dma_start(io["out"], x[:, :]).then_inc(stored, 16)
            sp.wait_ge(stored, 16)

        def norm_dve(dve, at, r, src, dst, after=None):
            for u in range(U):
                if after:
                    dve.wait_ge(*after(u))
                nc.vector.bn_stats(st[:, u, :], src(u)).then_inc(sem["stats"], 1)
            dve.wait_ge(*at("stats", r * U + U))
            met_dve(dve)
            for u in range(U):
                nc.vector.bn_aggr(mv[:, u, :], st[:, u, :]).then_inc(sem["moments"], 1)
            dve.wait_ge(*at("moments", (r + 1) * U))
            nc.vector.tensor_scalar(ve[:, :], mv[:, :, 1], EPS, None, ALU.add).then_inc(sem["vareps"], 1)
            dve.wait_ge(*at("rstd", r + 1))
            for u in range(U):
                nc.vector.tensor_scalar(dst(u), src(u), mv[:, u, 0:1], rstd[:, u:u + 1],
                                        ALU.subtract, ALU.mult).then_inc(sem["xn_ready"], 1)

        def norm_pool(pool, at, r):
            pool.wait_ge(*at("vareps", r + 1))
            nc.gpsimd.tensor_tensor(rstd[:, :], ve[:, :], neghalf[:, 0:U], ALU.pow).then_inc(sem["rstd"], 1)

        def met_dve(dve):
            dve.sem_inc(passed_v, 1)

        def met_pe(pe):
            pe.sem_inc(passed_t, 1)

        def load_group_dve(dve, at, g):
            dve.wait_ge(*at("x_done", 0))
            met_dve(dve)
            nc.vector.tensor_copy(xg[:, :], x[:, bass.ts(g, GT)]).then_inc(sem["xg_ready"], 1)

        def norm_in_dve(dve, at, g):
            load_group_dve(dve, at, g)
            dve.wait_ge(*at("xg_ready", 1))
            norm_dve(dve, at, 0, lambda u: un(xg, u), lambda u: un(xn, u))

        def flip_pe(pe, at, r, src, ready, k0):
            for u in range(U):
                pe.wait_ge(*at(ready, k0 + u + 1))
                ins = nc.tensor.transpose(un(psA, u), un(src, u), ident)
            ins.then_inc(sem["xnT_psum"], 1)

        def flip_act(act, at, r, dst):
            act.wait_ge(*at("xnT_psum", r + 1))
            nc.scalar.copy(dst[:, :], psA[:, :]).then_inc(sem["xnT_ready"], 1)

        def ctx_pool(pool, at, g):
            pool.wait_ge(*at("x_done", 0))
            nc.gpsimd.tensor_copy(ctxg[:, :], ctxT[:, bass.ts(g, U * SC)]).then_inc(sem["ctx_ready"], 1)

        class Heads:

            def __init__(self, pre, nk, scale=SCALE8, kind="self", mask=False):
                self.pre, self.nk, self.scale, self.kind, self.mask = pre, nk, scale, kind, mask
                self.window = kind == "window"
                self.cross = kind == "cross"
                self.project = not self.window

        def score_pe(pe, c, cur, par, t):
            u, quarter = divmod(t, 4)
            if t == 0:
                pe.wait_ge(*cur("k_ready", 4))
                pe.wait_ge(*cur("qz_ready", 4))
            if cur.has(t - 1):
                pe.wait_ge(*cur("s_sub", t - 1))
            q = qz[:, quarter, par * GA + u * S:par * GA + (u + 1) * S]
            ins = nc.tensor.matmul(bankS[t % 2][:, 0:4 * c.nk], q, kTx[:, UA * par + u, :, 0:c.nk],
                                   start=True, stop=not c.window)
            if c.window:
                ins = nc.tensor.matmul(bankS[t % 2][:, :], ident_bf[:, :],
                                       window_bf[:, :].unsqueeze(1).broadcast_to([128, 4, S]),
                                       start=False, stop=True)
            ins.then_inc(sem["s_psum"], 1)

        def turn_pe(pe, c, at, t):
            pe.wait_ge(*at("p_ready", t + 1))
            if at.has(t - 1):
                pe.wait_ge(*at("pt_ready", t - 1))
            for j in range(4):
                ins = nc.tensor.transpose(bankT[t % 2][0:c.nk, j * S:(j + 1) * S],
                                          p4[:, t % 4, j * c.nk:(j + 1) * c.nk], ident)
            ins.then_inc(sem["pt_psum"], 1)

        def value_pe(pe, c, at, par, t):
            u, quarter = divmod(t, 4)
            pe.wait_ge(*at("pt_ready", t + 1))
            if t == 0:
                pe.wait_ge(*at("v_ready", 1))
            if at.has(t):
                pe.wait_ge(*at("ov_ready", t))
            for j in range(4):
                first = (4 * quarter + j) * (DH + 1)
                ins = nc.tensor.matmul(bankV[32 * j:32 * j + 32, 0:S],
                                       vx_all[0:c.nk, UA * par + u, first:first + 32], pT4[0:c.nk, t % 4, j, :],
                                       start=True, stop=True)
            ins.then_inc(sem["o_psum"], 1)

        def back_pe(pe, c, at, t):
            u, quarter = divmod(t, 4)
            pe.wait_ge(*at("ov_ready", t + 1))
            if quarter == 0 and at.has(t):
                pe.wait_ge(*at("o_ready", u))
            nc.tensor.transpose(bankO[:, quarter * 128:(quarter + 1) * 128], ovT[:, t % 4, :],
                                ident).then_inc(sem["ob_psum"], 1)

        def flip_next_pe(pe, c, nxt, cur, prev, o):
            if cur and c.project and c.kind != "rope":
                pe.wait_ge(*cur("vm_ready" if c.kind == "top" else "v_ready", 1))
            if prev and c.project:
                pe.wait_ge(*prev("x_done", 0))
            for u in range(UA):
                pe.wait_ge(*nxt("xn_ready", u + 1))
                ins = nc.tensor.transpose(bankM[0][:, u * S:(u + 1) * S], xna[:, o, u * S:(u + 1) * S], ident)
            ins.then_inc(sem["xnT_psum"], 1)

        def project_next_pe(pe, c, nxt, cur, o):
            if c.window:
                return
            pe.wait_ge(*nxt("xnT_ready", 1))
            if c.kind == "rope" and cur:
                pe.wait_ge(*cur("v_ready", 1))
            xt = xnTa[:, o, :]
            if c.cross:
                pe.wait_ge(*nxt("ctx_ready", 1))
                keys = ctxa[:, o, :]
            else:
                keys = xt
            nc.tensor.matmul(bankM[1][:, 0:UA * c.nk], w(c.pre + "_wk"), keys, start=True,
                             stop=True).then_inc(sem["k_psum"], 1)
            if c.kind == "rope":
                nc.tensor.matmul(bankM[1][:, 256:512], w("L1a_wkr"), keys, start=True,
                                 stop=True).then_inc(sem["k_psum"], 1)
                nc.tensor.matmul(bankM[0][:, 0:256], w("L1a_wqr"), xt, start=True, stop=True)
            nc.tensor.matmul(bankM[0][:, 256:512], w(c.pre + "_wq"), xt, start=True,
                             stop=True).then_inc(sem["q_psum"], 1)
            if c.kind != "rope":
                values_next_pe(pe, c, nxt, o)

        def values_next_pe(pe, c, nxt, o):
            keys = ctxa[:, o, :] if c.cross else xnTa[:, o, :]
            bank = bankM[1] if c.kind == "rope" else bankM[0]
            for u in range(UA):
                ins = nc.tensor.matmul(bank[0:c.nk, u * 128:(u + 1) * 128], keys[:, u * c.nk:(u + 1) * c.nk],
                                       w(c.pre + "_wv"), start=True, stop=True)
            ins.then_inc(sem["v_psum"], 1)

        def mean_next_pe(pe, c, nxt, o):
            pe.wait_ge(*nxt("v_ready", 1))
            pe.wait_ge(*nxt("q_ready", 1))
            for u in range(UA):
                ins = nc.tensor.matmul(bankM[0][:, u * 128:(u + 1) * 128], mean_w[:, :],
                                       vx[:, UA * o + u, :, 0:DH], start=True, stop=True)
            ins.then_inc(sem["vm_psum"], 1)

        def turn_out_pe(pe, c, prev, nxt):
            pe.wait_ge(*prev("o_ready", UA))
            if nxt and c.kind == "rope":
                pe.wait_ge(*nxt("rope", 3))
            elif nxt:
                pe.wait_ge(*nxt("k_ready", 4))
            for u in range(UA):
                ins = nc.tensor.transpose(bankM[1][:, u * S:(u + 1) * S], on2[:, u * S:(u + 1) * S], ident)
            ins.then_inc(sem["oT_psum"], 1)

        def out_pe(pe, c, prev, nxt):
            pe.wait_ge(*prev("oT_ready", 1))
            if nxt:
                if c.kind == "rope":
                    pe.wait_ge(*nxt("rope", 6))
                else:
                    pe.wait_ge(*nxt("vm_ready" if c.kind == "top" else "v_ready", 1))
            bias_pe(bankM[0], c.pre + "_bo", UA)
            for u in range(UA):
                ins = nc.tensor.matmul(bankM[0][:, u * S:(u + 1) * S], oT2[:, u * S:(u + 1) * S], w(c.pre + "_wo"),
                                       start=False, stop=(u == UA - 1))
            ins.then_inc(sem["y_psum"], 1)

        def group_pe(pe, c, cur, prev, nxt, par):
            for t in range(8):
                if cur:
                    score_pe(pe, c, cur, par, t)
                if t >= 2 and cur:
                    turn_pe(pe, c, cur, t - 2)
                if t < 2 and prev:
                    turn_pe(pe, c, prev, t + 6)
                if t >= 3 and cur:
                    value_pe(pe, c, cur, par, t - 3)
                if t < 3 and prev:
                    value_pe(pe, c, prev, 1 - par, t + 5)
                if t >= 4 and cur:
                    back_pe(pe, c, cur, t - 4)
                if t < 4 and prev:
                    back_pe(pe, c, prev, t + 4)
                if t == 2 and nxt:
                    flip_next_pe(pe, c, nxt, cur, prev, 1 - par)
                if t == 3 and nxt:
                    project_next_pe(pe, c, nxt, cur, 1 - par)
                if t == 5 and nxt and c.kind == "top":
                    mean_next_pe(pe, c, nxt, 1 - par)
                if t == 5 and prev and c.project:
                    turn_out_pe(pe, c, prev, nxt)
                if t == 6 and prev and c.project:
                    out_pe(pe, c, prev, nxt)
                if t == 6 and nxt and c.kind == "rope":
                    if prev:
                        pe.wait_ge(*prev("oT_ready", 1))
                    pe.wait_ge(*nxt("rope", 3))
                    values_next_pe(pe, c, nxt, 1 - par)

        def v2(t, n=S):
            return t.rearrange("p (u k) -> p u k", u=UA)

        def expand_next_act(act, c, nxt, o, js):
            dst = kTx[:, UA * o:UA * o + UA, :, :]
            for j in js:
                if c.window:
                    src, scale, bias = v2(xnTa[:, o, :]), heads4, 0.0
                elif c.kind == "rope":
                    src, scale, bias = v2(rope1[:, 1, 0:GA]), heads4, 0.0
                else:
                    b = KBIAS.index(c.pre)
                    src, scale, bias = v2(bankM[1][:, 0:UA * c.nk]), heads4s if c.mask else heads4, kb4[:, b, j:j + 1]
                nc.scalar.activation(dst[:, :, j, 0:c.nk], src, ACT.Identity, bias=bias,
                                     scale=scale[:, j:j + 1]).then_inc(sem["k_ready"], 1)

        def group_act(act, c, cur, prev, nxt, par):
            o = 1 - par
            expand_at = 5 if c.kind == "rope" else 4
            for t in range(8):
                at, i = (cur, t - 4) if t >= 4 else (prev, t + 4)
                if at:
                    act.wait_ge(*at("o_psum", i + 1))
                    if at.has(i - 3):
                        act.wait_ge(*at("ob_psum", i - 3))
                    nc.scalar.copy(ovT[:, i % 4, :], bankV[:, 0:S]).then_inc(sem["ov_ready"], 1)
                at, i = (cur, t - 2) if t >= 2 else (prev, t + 6)
                if at:
                    act.wait_ge(*at("pt_psum", i + 1))
                    if at.has(i - 3):
                        act.wait_ge(*at("o_psum", i - 3))
                    nc.scalar.copy(pT4[0:c.nk, i % 4, :, :].rearrange("p j s -> p (j s)"),
                                   bankT[i % 2][0:c.nk, :]).then_inc(sem["pt_ready"], 1)
                if cur:
                    act.wait_ge(*cur("s_sub", t + 1))
                    pv = p4[:, t % 4, 0:4 * c.nk]
                    nc.scalar.activation(pv, pv, ACT.Exp, scale=c.scale).then_inc(sem["p_ready"], 1)
                if t == 2 and nxt:
                    act.wait_ge(*nxt("xnT_psum", 1))
                    nc.scalar.copy(xnTa[:, o, :], bankM[0][:, 0:GA]).then_inc(sem["xnT_ready"], 1)
                if t == 4 and nxt and c.kind in ("cross", "top"):
                    act.wait_ge(*nxt("v_psum", 1))
                    nc.scalar.activation(qTa[:, o, :], bankM[0][:, 256:512], ACT.Identity,
                                         bias=col(c.pre + "_bq")).then_inc(sem["q_ready"], 1)
                if nxt and expand_at <= t < expand_at + 2:
                    if t == expand_at:
                        if c.window:
                            act.wait_ge(*nxt("xnT_ready", 1))
                        elif c.kind == "rope":
                            act.wait_ge(*nxt("rope", 3))
                        else:
                            act.wait_ge(*nxt("k_psum", 1))
                    a = 2 * (t - expand_at)
                    expand_next_act(act, c, nxt, o, (a, a + 1))
                if t == (7 if c.kind == "rope" else 4) and nxt:
                    if prev:
                        act.wait_ge(*prev("o_psum", 8))
                    if c.window:
                        act.wait_ge(*nxt("xn_ready", UA))
                        src = xna[:, o, :]
                    else:
                        act.wait_ge(*nxt("v_psum", 1))
                        src = bankM[1 if c.kind == "rope" else 0][0:c.nk, 0:GA]
                    nc.scalar.copy(vx[0:c.nk, UA * o:UA * o + UA, :, 0:DH],
                                   src.rearrange("p (u h e) -> p u h e", u=UA, e=DH)).then_inc(sem["v_ready"], 1)
                if t == 5 and prev and c.project:
                    act.wait_ge(*prev("oT_psum", 1))
                    nc.scalar.activation(oT2[:, :], bankM[1][:, 0:GA], ACT.Identity,
                                         bias=col(c.pre + "_bv")).then_inc(sem["oT_ready"], 1)

        def softmax_dve(dve, c, cur, t):
            u = t // 4
            sv = bankS[t % 2][:, 0:4 * c.nk].rearrange("p (j k) -> p j k", j=4)
            mx = smx[:, t % 2, 0:4]
            dve.wait_ge(*cur("s_psum", t + 1))
            if c.mask:
                m = cmask[:, bass.ts(cur.g * UA + u, SC)].unsqueeze(1).broadcast_to([128, 4, SC])
                nc.vector.tensor_tensor(sv, sv, m, ALU.add).then_inc(sem["s_mask"], 1)
                dve.wait_ge(*cur("s_mask", t + 1))
            nc.vector.tensor_reduce(mx, sv, AX.X, ALU.max).then_inc(sem["s_max"], 1)
            dve.wait_ge(*cur("s_max", t + 1))
            if cur.has(t - 3):
                dve.wait_ge(*cur("pt_psum", t - 3))
            nc.vector.tensor_tensor(p4[:, t % 4, 0:4 * c.nk].rearrange("p (j k) -> p j k", j=4), sv,
                                    mx.unsqueeze(2).broadcast_to([128, 4, c.nk]),
                                    ALU.subtract).then_inc(sem["s_sub"], 1)

        def finish_dve(dve, c, at, u):
            dve.wait_ge(*at("ob_psum", 4 * u + 4))
            ov = bankO[:, :].rearrange("p (h e) -> p h e", h=H)
            nc.vector.reciprocal(rec[:, u, :], ov[:, :, DH]).then_inc(sem["o_recip"], 1)
            dve.wait_ge(*at("o_recip", u + 1))
            dv = on2[:, u * S:(u + 1) * S]
            dh = dv.rearrange("p (h e) -> p h e", h=H)
            rb = rec[:, u, :].unsqueeze(2).broadcast_to([128, H, DH])
            if c.kind == "top":
                nc.vector.tensor_tensor(rec[:, u, :], rec[:, u, :], sel_all[:, 0, bass.ts(at.g * UA + u, H)],
                                        ALU.mult).then_inc(sem["o_mix"], 1)
                dve.wait_ge(*at("o_mix", 2 * u + 1))
                nc.vector.tensor_tensor(dh, ov[:, :, 0:DH], rb, ALU.mult).then_inc(sem["o_mix"], 1)
                dve.wait_ge(*at("o_mix", 2 * u + 2))
                nc.vector.tensor_tensor(dv, dv, vmean[at.par][:, u * S:(u + 1) * S],
                                        ALU.add).then_inc(sem["o_ready"], 1)
            else:
                nc.vector.tensor_tensor(dh, ov[:, :, 0:DH], rb, ALU.mult).then_inc(sem["o_ready"], 1)

        def load_next_dve(dve, c, nxt, cur):
            if cur is None:
                dve.wait_ge(*nxt("x_done", 0))
            else:
                dve.wait_ge(*cur("xn_ready", UA))
            met_dve(dve)
            nc.vector.tensor_copy(xg[:, 0:GA], x[:, bass.ts(nxt.g, GA)]).then_inc(sem["xg_ready"], 1)
            dve.wait_ge(*nxt("xg_ready", 1))
            for u in range(UA):
                nc.vector.bn_stats(st[:, u, :], xg[:, u * S:(u + 1) * S]).then_inc(sem["stats"], 1)
            dve.wait_ge(*nxt("stats", UA))
            met_dve(dve)
            for u in range(UA):
                nc.vector.bn_aggr(mv[:, u, :], st[:, u, :]).then_inc(sem["moments"], 1)
            dve.wait_ge(*nxt("moments", UA))
            nc.vector.tensor_scalar(ve[:, 0:UA], mv[:, 0:UA, 1], EPS, None, ALU.add).then_inc(sem["vareps"], 1)

        def norm_next_dve(dve, c, nxt, o):
            dve.wait_ge(*nxt("rstd", 1))
            for u in range(UA):
                nc.vector.tensor_scalar(xna[:, o, u * S:(u + 1) * S], xg[:, u * S:(u + 1) * S], mv[:, u, 0:1],
                                        rstd[:, u:u + 1], ALU.subtract, ALU.mult).then_inc(sem["xn_ready"], 1)

        def rope_next_dve(dve, c, nxt, o, q):
            cosb = const("cos").unsqueeze(1).broadcast_to([128, UA, S])
            sinb = const("sin").unsqueeze(1).broadcast_to([128, UA, S])
            if q:
                dve.wait_ge(*nxt("q_psum", 1))
                bank, rbank, a, b, k, to = bankM[0][:, 256:512], bankM[0][:, 0:256], "L1a_bq", "L1a_bqr", 3, qTa[:, o, :]
            else:
                dve.wait_ge(*nxt("k_psum", 2))
                bank, rbank, a, b, k, to = (bankM[1][:, 0:256], bankM[1][:, 256:512], "L1a_bk", "L1a_bkr", 0,
                                            rope1[:, 1, 0:GA])
            nc.vector.scalar_tensor_tensor(out=v2(rope1[:, 0, 0:GA]), in0=v2(bank),
                                           scalar=col(a), in1=cosb, op0=ALU.add, op1=ALU.mult).then_inc(sem["rope"], 1)
            nc.vector.scalar_tensor_tensor(out=v2(rope2[:, q, 0:GA]), in0=v2(rbank), scalar=col(b),
                                           in1=sinb, op0=ALU.add, op1=ALU.mult).then_inc(sem["rope"], 1)
            dve.wait_ge(*nxt("rope", k + 2))
            nc.vector.tensor_tensor(to, rope1[:, 0, 0:GA], rope2[:, q, 0:GA], ALU.add).then_inc(sem["rope"], 1)

        def mean_next_dve(dve, c, nxt, o):
            dve.wait_ge(*nxt("vm_psum", 1))
            nc.vector.tensor_tensor(vmean[o].rearrange("p (n e) -> p n e", e=DH),
                                    bankM[0][:, 0:GA].rearrange("p (n e) -> p n e", e=DH),
                                    sel_all[:, 1, bass.ts(nxt.g, UA * H)].unsqueeze(2).broadcast_to([128, UA * H, DH]),
                                    ALU.mult).then_inc(sem["vm_ready"], 1)

        def group_dve(dve, c, cur, prev, nxt, par):
            for t in range(8):
                if t == 0 and prev:
                    finish_dve(dve, c, prev, 0)
                if t == 4 and prev:
                    finish_dve(dve, c, prev, 1)
                if cur:
                    softmax_dve(dve, c, cur, t)
                if t == 0 and nxt:
                    load_next_dve(dve, c, nxt, cur)
                if t == 1 and nxt:
                    norm_next_dve(dve, c, nxt, 1 - par)
                if t in (4, 5) and nxt and c.kind == "rope":
                    if t == 5:
                        dve.wait_ge(*nxt("rope", 3))
                    rope_next_dve(dve, c, nxt, 1 - par, t - 4)
                if t == 5 and prev and c.window:
                    dve.wait_ge(*prev("o_ready", UA))
                    dve.wait_ge(*prev("hold_ready", 1))
                    hs = hold[:, bass.ts(prev.g, GA)]
                    nc.vector.tensor_tensor(hs, hs, on2[:, :], ALU.add).then_inc(sem["x_done"], 1)
                if t == 5 and nxt and c.kind == "top":
                    mean_next_dve(dve, c, nxt, 1 - par)
                if t == 7 and prev and c.project:
                    dve.wait_ge(*prev("y_psum", 1))
                    xs = x[:, bass.ts(prev.g, GA)]
                    nc.vector.tensor_tensor(xs, xs, bankM[0][:, 0:GA], ALU.add).then_inc(sem["x_done"], 1)

        def group_pool(pool, c, cur, prev, nxt, par):
            if nxt:
                if c.cross:
                    if nxt.has(-1, per=1):
                        pool.wait_ge(*nxt("v_psum", -1))
                    nc.gpsimd.tensor_copy(ctxa[:, 1 - par, :],
                                          ctxT[:, bass.ts(nxt.g, UA * SC)]).then_inc(sem["ctx_ready"], 1)
                pool.wait_ge(*nxt("vareps", 1))
                nc.gpsimd.tensor_tensor(rstd[:, 0:UA], ve[:, 0:UA], neghalf[:, 0:UA], ALU.pow).then_inc(sem["rstd"], 1)
                if c.window:
                    pool.wait_ge(*nxt("xn_ready", UA))
                    nc.gpsimd.tensor_copy(hold[:, bass.ts(nxt.g, GA)],
                                          xna[:, 1 - par, :]).then_inc(sem["hold_ready"], 1)
                o = 1 - par
                if c.window:
                    pool.wait_ge(*nxt("xnT_ready", 1))
                elif c.kind == "rope":
                    pool.wait_ge(*nxt("rope", 6))
                else:
                    pool.wait_ge(*nxt("q_ready", 1))
                pool.sem_inc(passed_g, 1)
                for quarter in range(4):
                    nc.gpsimd.tensor_scalar(qz[:, quarter, o * GA:(o + 1) * GA], (xnTa if c.window else qTa)[:, o, :],
                                            const("quarters")[:, quarter:quarter + 1], None,
                                            ALU.mult).then_inc(sem["qz_ready"], 1)

        def run_heads(eng, block_name, body, c):
            n = GROUPS[block_name]

            def counts(g, par):
                return Counts(block_name, g, par)

            body(eng, c, None, None, counts(0, 0), 1)
            body(eng, c, counts(0, 0), None, counts(1, 1), 0)
            with eng.Fori(0, (n - 2) // 2) as i:
                for k in range(2):
                    par = (1 + k) % 2
                    body(eng, c, counts(2 * i + (k + 1), par), counts(2 * i + k, 1 - par),
                         counts(2 * i + (k + 2), 1 - par), par)
            last = (n - 1) % 2
            body(eng, c, counts(n - 1, last), counts(n - 2, 1 - last), None, last)
            body(eng, c, None, counts(n - 1, last), None, 1 - last)

        KBIAS = ["L0x", "L1x", "L2a"]
        HEADS_OF = {
            "L0_attn": Heads("L0a", S, 1.0, "window"),
            "L0_xattn": Heads("L0x", SC, 1.0, "cross", mask=True),
            "L1_attn": Heads("L1a", S, kind="rope"),
            "L1_xattn": Heads("L1x", SC, kind="cross"),
            "L2_attn": Heads("L2a", S, kind="top"),
        }
        HEADS_PROGRAM = (group_pe, group_act, group_dve, group_pool)

        class Stream:
            def __init__(self, suffix, tokens, small, banks):
                self.suffix = suffix
                self.xg, self.xn, self.xm, self.xnT, self.xmT, self.on, self.qT, self.oT, self.f = tokens
                self.st, self.mv, self.ve, self.rstd = small
                self.psA, self.psB = ps[:, banks[0], :], ps[:, banks[0] + 1, :]
                self.psF = [ps[:, banks[1], :], ps[:, banks[1] + 1, :]]
                self.pairs = [ps[:, b:b + 2, :] for b in (banks[1], banks[0])]

            def sem(self, name):
                return sem[name + self.suffix]

        p_all, pT_all = [t.rearrange("p a n -> p (a n)") for t in (p[:, :, :], pT[:, :, :, :].rearrange("p a j s -> p a (j s)"))]
        STREAMS = [
            Stream("", (xg, xn, xm, xnT, xmT, on, qT, oT, fT[:, 0, :, :]), (st, mv, ve, rstd),
                   (6, 0)),
            Stream("2", [p_all[:, i * GT:(i + 1) * GT] for i in range(4)] + [pT_all[:, i * GT:(i + 1) * GT] for i in range(4)]
                   + [kTx[:, :, :, :].rearrange("p u j s -> p u (j s)")],
                   (acc[:, 0:6 * U].rearrange("p (u c) -> p u c", u=U),
                    acc[:, 6 * U:8 * U].rearrange("p (u c) -> p u c", u=U),
                    acc[:, 8 * U:9 * U], acc[:, 9 * U:10 * U]),
                   (4, 2)),
        ]

        def in_turns(first, second):
            for _ in zip(first, second):
                pass

        def z_flip_pe(pe, at, z, src, k0):
            for u in range(U):
                pe.wait_ge(*at("xn_ready", k0 + u + 1))
                ins = nc.tensor.transpose(un(z.psA, u), un(src, u), ident)
            ins.then_inc(z.sem("xnT_psum"), 1)

        def z_norm_dve(dve, at, z, r, src, dst):
            for u in range(U):
                nc.vector.bn_stats(z.st[:, u, :], un(src, u)).then_inc(z.sem("stats"), 1)
            yield
            dve.wait_ge(*at("stats", (r + 1) * U))
            met_dve(dve)
            for u in range(U):
                nc.vector.bn_aggr(z.mv[:, u, :], z.st[:, u, :]).then_inc(z.sem("moments"), 1)
            yield
            dve.wait_ge(*at("moments", (r + 1) * U))
            nc.vector.tensor_scalar(z.ve[:, :], z.mv[:, :, 1], EPS, None, ALU.add).then_inc(z.sem("vareps"), 1)
            yield
            dve.wait_ge(*at("rstd", r + 1))
            for u in range(U):
                nc.vector.tensor_scalar(un(dst, u), un(src, u), z.mv[:, u, 0:1], z.rstd[:, u:u + 1],
                                        ALU.subtract, ALU.mult).then_inc(z.sem("xn_ready"), 1)
            yield

        def z_load_dve(dve, at, z, g):
            dve.wait_ge(*at("g_done", 0))
            met_dve(dve)
            nc.vector.tensor_copy(z.xg[:, :], x[:, bass.ts(g, GT)]).then_inc(z.sem("xg_ready"), 1)

        def z_norm_pool(pool, at, z, r):
            pool.wait_ge(*at("vareps", r + 1))
            nc.gpsimd.tensor_tensor(z.rstd[:, :], z.ve[:, :], neghalf[:, 0:U], ALU.pow).then_inc(z.sem("rstd"), 1)

        def run_streams(eng, block_name, body, with_group=False):
            with eng.Fori(0, GROUPS[block_name]) as i:
                in_turns(*[body(eng, Counts(block_name, i, suffix=z.suffix), z, *([2 * i + k] if with_group else []))
                           for k, z in enumerate(STREAMS)])

        def l0_ff_pe(pe, at, z):
            z_flip_pe(pe, at, z, z.xm, 0)
            yield
            pe.wait_ge(*at("xnT_ready", 1))
            for b in range(4):
                if b >= 2:
                    pe.wait_ge(*at("f_ready", b - 1))
                nc.tensor.matmul(z.psF[b % 2], w("L0a_w1", b * 128, b * 128 + 128), z.xmT[:, :],
                                 start=True, stop=True).then_inc(z.sem("f_psum"), 1)
                if b % 2:
                    yield
            pe.wait_ge(*at("f_ready", 4))
            bias_pe(z.psB, "L0a_b2", U)
            for u in range(U):
                for b in range(4):
                    nc.tensor.matmul(un(z.psB, u), un(z.f[:, b, :], u), w("L0a_w2", b * 128, b * 128 + 128),
                                     start=False, stop=False)
                ins = nc.tensor.matmul(un(z.psB, u), un(z.xmT, u), ident, start=False, stop=(u == U - 1))
            ins.then_inc(z.sem("y_psum"), 1)
            yield

        def l0_ff_act(act, at, z):
            act.wait_ge(*at("xnT_psum", 1))
            nc.scalar.activation(z.xmT[:, :], z.psA[:, :], ACT.Identity, bias=col("L0a_b1"),
                                 scale=col("L0a_g1")).then_inc(z.sem("xnT_ready"), 1)
            yield
            for b in range(4):
                act.wait_ge(*at("f_psum", b + 1))
                nc.scalar.activation(z.f[:, b, :], z.psF[b % 2], ACT.Relu,
                                     bias=col("L0a_fb", b)).then_inc(z.sem("f_ready"), 1)
                if b % 2:
                    yield

        def l0_ff_dve(dve, at, z, g):
            z_load_dve(dve, at, z, g)
            nc.vector.tensor_copy(z.on[:, :], hold[:, bass.ts(g, GT)]).then_inc(z.sem("hold_ready"), 1)
            yield
            dve.wait_ge(*at("hold_ready", 1))
            yield from z_norm_dve(dve, at, z, 0, z.on, z.xm)
            dve.wait_ge(*at("y_psum", 1))
            yield from z_norm_dve(dve, at, z, 1, z.psB, z.xn)
            dve.wait_ge(*at("xn_ready", 2 * U))
            v3 = z.xn[:, :].rearrange("p (u d) -> p u d", u=U)
            gain = g2b[:, 0, :].unsqueeze(1).broadcast_to([128, U, D])
            shift = g2b[:, 1, :].unsqueeze(1).broadcast_to([128, U, D])
            nc.vector.tensor_tensor(v3, v3, gain, ALU.mult).then_inc(z.sem("h_res"), 1)
            yield
            dve.wait_ge(*at("h_res", 1))
            nc.vector.tensor_tensor(v3, v3, shift, ALU.add).then_inc(z.sem("h_res"), 1)
            yield
            dve.wait_ge(*at("h_res", 2))
            nc.vector.tensor_tensor(x[:, bass.ts(g, GT)], z.xg[:, :], z.xn[:, :], ALU.add).then_inc(z.sem("g_done"), 1)
            yield

        def l0_ff_pool(pool, at, z):
            for r in range(2):
                z_norm_pool(pool, at, z, r)
                yield

        def experts_pe(pe, at, g, ne, nb, wgate, wval, wout):
            for e in range(ne):
                for b in range(nb):
                    j = e * nb + b
                    pe.wait_ge(*at("h_ready", j - 1))
                    xt = xnT_all[:, bass.ts(g, GT)]
                    nc.tensor.matmul(psS[0][:, j % 2, :], wgate(e, b), xt, start=True, stop=True)
                    nc.tensor.matmul(psS[1][:, j % 2, :], wval(e, b), xt, start=True,
                                     stop=True).then_inc(sem["gv_psum"], 1)
                if e >= 1:
                    expert_out_pe(pe, at, e - 1, nb, wout)
            expert_out_pe(pe, at, ne - 1, nb, wout)

        def expert_out_pe(pe, at, e, nb, wout):
            pe.wait_ge(*at("h_ready", (e + 1) * nb))
            pe.wait_ge(*at("acc", (e - 1) * U))
            for u in range(U):
                for b in range(nb):
                    ins = nc.tensor.matmul(un(psT[:, e % 2, :], u), un(fT[:, e % 2, b, :], u), wout(e, b),
                                           start=(b == 0), stop=(b == nb - 1))
            ins.then_inc(sem["ye_psum"], 1)

        def experts_act(act, at, ne, nb, func, bgate):
            for j in range(ne * nb):
                act.wait_ge(*at("gv_psum", j + 1))
                act.wait_ge(*at("h_ready", j - 1))
                bias = bgate(j // nb, j % nb) if bgate else 0.0
                nc.scalar.activation(sg[:, j % 2, :], psS[0][:, j % 2, :], func, bias=bias).then_inc(sem["sg_ready"], 1)

        def experts_dve(dve, at, g, ne, nb, bval):
            load_group_dve(dve, at, g)
            nc.vector.tensor_copy(gates[:, :, :], gates_all[:, bass.ts(g, U), :]).then_inc(sem["xg_ready"], 1)
            for e in range(ne):
                for b in range(nb):
                    j = e * nb + b
                    dve.wait_ge(*at("sg_ready", j + 1))
                    if b == 0:
                        dve.wait_ge(*at("ye_psum", e - 1))
                    hv = psS[1][:, j % 2, :]
                    if bval:
                        ins = nc.vector.scalar_tensor_tensor(out=fT[:, e % 2, b, :], in0=hv, scalar=bval(e, b),
                                                             in1=sg[:, j % 2, :], op0=ALU.add, op1=ALU.mult)
                    else:
                        ins = nc.vector.tensor_tensor(fT[:, e % 2, b, :], hv, sg[:, j % 2, :], ALU.mult)
                    ins.then_inc(sem["h_ready"], 1)
                if e >= 1:
                    gather_dve(dve, at, g, e - 1, ne)
            gather_dve(dve, at, g, ne - 1, ne)

        def gather_dve(dve, at, g, e, ne):
            dve.wait_ge(*at("ye_psum", e + 1))
            if e == 0:
                dve.wait_ge(*at("xg_ready", 2))
            for u in range(U):
                if e >= 1:
                    dve.wait_ge(*at("acc", (e - 1) * U + u + 1))
                base = xg if e == 0 else acc
                nc.vector.scalar_tensor_tensor(out=un(acc, u), in0=un(psT[:, e % 2, :], u),
                                               scalar=gates[:, u, e:e + 1], in1=un(base, u), op0=ALU.mult,
                                               op1=ALU.add).then_inc(sem["acc"], 1)
            if e == ne - 1:
                dve.wait_ge(*at("acc", ne * U))
                met_dve(dve)
                nc.vector.tensor_copy(x[:, bass.ts(g, GT)], acc[:, :]).then_inc(sem["x_done"], 1)

        logits = ps[:, 0, 0:NB * 8].rearrange("p (s e) -> p s e", s=NB)

        def pre_norm_dve(dve, at):
            dve.wait_ge(*at("x_done", 0))
            for s in range(NB):
                nc.vector.bn_stats(st16[:, s, :], un(x, s)).then_inc(sem["stats"], 1)
            dve.wait_ge(*at("stats", NB))
            for s in range(NB):
                nc.vector.bn_aggr(mv16[:, s, :], st16[:, s, :]).then_inc(sem["moments"], 1)
            dve.wait_ge(*at("moments", NB))
            nc.vector.tensor_scalar(ve16, mv16[:, :, 1], EPS, None, ALU.add).then_inc(sem["vareps"], 1)
            dve.wait_ge(*at("rstd", 1))
            for s in range(NB):
                nc.vector.tensor_scalar(un(xn_all, s), un(x, s), mv16[:, s, 0:1], rstd16[:, s:s + 1],
                                        ALU.subtract, ALU.mult).then_inc(sem["xn_ready"], 1)
            dve.wait_ge(*at("r_psum", 1))

        def pre_pool(pool, at, g):
            pool.wait_ge(*at("vareps", 1))
            nc.gpsimd.tensor_tensor(rstd16, ve16, neghalf[:, :], ALU.pow).then_inc(sem["rstd"], 1)

        def pre_pe(pe, at, wr, br):
            for c in range(NG):
                if c >= 2:
                    pe.wait_ge(*at("xnT_ready", c - 1))
                for u in range(U):
                    pe.wait_ge(*at("xn_ready", c * U + u + 1))
                    ins = nc.tensor.transpose(un(ps[:, 6 + c % 2, :], u), un(xn_all, c * U + u), ident)
                ins.then_inc(sem["xnT_psum"], 1)
            for s in range(NB):
                pe.wait_ge(*at("xnT_ready", s // U + 1))
                ins = nc.tensor.matmul(logits[:, s, :], un(xnT_all, s), wr, start=True, stop=br is None)
                if br is not None:
                    ins = nc.tensor.matmul(logits[:, s, :], ones_row, br, start=False, stop=True)
            ins.then_inc(sem["r_psum"], 1)

        def pre_act(act, at):
            for c in range(NG):
                act.wait_ge(*at("xnT_psum", c + 1))
                nc.scalar.copy(xnT_all[:, c * GT:(c + 1) * GT], ps[:, 6 + c % 2, :]).then_inc(sem["xnT_ready"], 1)

        def b8(t):
            return t.unsqueeze(2).broadcast_to([128, NB, 8])

        rank16 = rank.unsqueeze(1).broadcast_to([128, NB, 8])

        def first_max_dve(dve, at, k, src, m, t, dst):
            nc.vector.tensor_reduce(rm[:, m, :], src, AX.X, ALU.max).then_inc(sem["r_step"], 1)
            dve.wait_ge(*at("r_step", k + 1))
            nc.vector.tensor_tensor(rt[:, t, :, :], src, b8(rm[:, m, :]), ALU.is_equal).then_inc(sem["r_step"], 1)
            dve.wait_ge(*at("r_step", k + 2))
            nc.vector.tensor_tensor(rt[:, t, :, :], rt[:, t, :, :], rank16, ALU.mult).then_inc(sem["r_step"], 1)
            dve.wait_ge(*at("r_step", k + 3))
            nc.vector.tensor_reduce(rm[:, 5, :], rt[:, t, :, :], AX.X, ALU.max).then_inc(sem["r_step"], 1)
            dve.wait_ge(*at("r_step", k + 4))
            nc.vector.tensor_tensor(dst, rt[:, t, :, :], b8(rm[:, 5, :]), ALU.is_equal).then_inc(sem["r_step"], 1)
            dve.wait_ge(*at("r_step", k + 5))

        def l0_pre_pe(pe, at, g):
            pre_pe(pe, at, w("L0f_rw"), row("L0f_rb"))
            b2 = cols[0:E0, CAT["L0f_b2"][0]:CAT["L0f_b2"][0] + D]
            pe.wait_ge(*at("r_step", 5))
            for c in range(NG):
                for u in range(U):
                    ins = nc.tensor.matmul(ps[0:E0, 1 + c, u * 128:(u + 1) * 128], gates_all[:, c * U + u, :], ident,
                                           start=True, stop=True)
                ins.then_inc(sem["pt_psum"], 1)
            for c in range(NG):
                pe.wait_ge(*at("pt_ready", c + 1))
                for u in range(U):
                    ins = nc.tensor.matmul(un(ps[:, 1 + c, :], u), un(gT[0:E0, :], c * U + u), b2, start=True, stop=True)
                ins.then_inc(sem["y_psum"], 1)

        def l0_pre_act(act, at, g):
            pre_act(act, at)
            for c in range(NG):
                act.wait_ge(*at("pt_psum", c + 1))
                nc.scalar.copy(gT[0:E0, c * GT:(c + 1) * GT], ps[0:E0, 1 + c, :]).then_inc(sem["pt_ready"], 1)

        def l0_pre_dve(dve, at, g):
            pre_norm_dve(dve, at)
            first_max_dve(dve, at, 0, logits, 0, 0, gates_all[:, :, :])
            for c in range(NG):
                dve.wait_ge(*at("y_psum", c + 1))
                xs = x[:, c * GT:(c + 1) * GT]
                nc.vector.tensor_tensor(xs, xs, ps[:, 1 + c, :], ALU.add).then_inc(sem["x_done"], 1)

        def l0_ffn_pe(pe, at, g):
            experts_pe(pe, at, g, E0, 4,
                       lambda e, b: w("L0f_w1", e * 1024 + 512 + b * 128, e * 1024 + 512 + b * 128 + 128),
                       lambda e, b: w("L0f_w1", e * 1024 + b * 128, e * 1024 + b * 128 + 128),
                       lambda e, b: w("L0f_w2", (e * 4 + b) * 128, (e * 4 + b) * 128 + 128))

        def l0_ffn_act(act, at, g):
            experts_act(act, at, E0, 4, ACT.Sigmoid, lambda e, b: col("L0f_b1", e * 8 + 4 + b))

        def l0_ffn_dve(dve, at, g):
            experts_dve(dve, at, g, E0, 4, lambda e, b: col("L0f_b1", e * 8 + b))

        def l3_pre_pe(pe, at, g):
            pre_pe(pe, at, w("L3f_wg"), None)

        def l3_pre_act(act, at, g):
            pre_act(act, at)
            act.wait_ge(*at("r_step", 2))
            nc.scalar.activation(rt[:, 1, :, :], rt[:, 0, :, :], ACT.Exp).then_inc(sem["r_exp"], 1)

        def l3_pre_dve(dve, at, g):
            pre_norm_dve(dve, at)
            step = [0]

            def inc(ins):
                step[0] += 1
                ins.then_inc(sem["r_step"], 1)
                dve.wait_ge(*at("r_step", step[0]))

            inc(nc.vector.tensor_reduce(rm[:, 0, :], logits, AX.X, ALU.max))
            inc(nc.vector.tensor_tensor(rt[:, 0, :, :], logits, b8(rm[:, 0, :]), ALU.subtract))
            dve.wait_ge(*at("r_exp", 1))
            first_max_dve(dve, at, 2, rt[:, 1, :, :], 1, 2, rt[:, 3, :, :])
            step[0] = 7
            inc(nc.vector.tensor_scalar(rt[:, 4, :, :], rt[:, 3, :, :], -2.0, None, ALU.mult))
            inc(nc.vector.tensor_tensor(rt[:, 4, :, :], rt[:, 4, :, :], rt[:, 1, :, :], ALU.add))
            first_max_dve(dve, at, 9, rt[:, 4, :, :], 2, 2, rt[:, 5, :, :])
            step[0] = 14
            inc(nc.vector.tensor_tensor(rm[:, 3, :], rm[:, 1, :], rm[:, 2, :], ALU.add))
            nc.vector.reciprocal(rm[:, 4, :], rm[:, 3, :]).then_inc(sem["r_step"], 1)
            dve.wait_ge(*at("r_step", 16))
            nc.vector.tensor_tensor(rt[:, 3, :, :], rt[:, 3, :, :], rt[:, 5, :, :], ALU.add).then_inc(sem["g_step"], 1)
            dve.wait_ge(*at("g_step", 1))
            nc.vector.tensor_tensor(rt[:, 3, :, :], rt[:, 3, :, :], rt[:, 1, :, :], ALU.mult).then_inc(sem["g_step"], 1)
            dve.wait_ge(*at("g_step", 2))
            nc.vector.tensor_tensor(gates_all[:, :, :], rt[:, 3, :, :], b8(rm[:, 4, :]), ALU.mult).then_inc(sem["g_step"], 1)
            dve.wait_ge(*at("g_step", 3))
            dve.sem_inc(sem["x_done"], 1)

        def l3_ffn_pe(pe, at, g):
            experts_pe(pe, at, g, E3, 2,
                       lambda e, b: w("L3f_w1", (e * 2 + b) * 128, (e * 2 + b) * 128 + 128),
                       lambda e, b: w("L3f_w3", (e * 2 + b) * 128, (e * 2 + b) * 128 + 128),
                       lambda e, b: w("L3f_w2", (e * 2 + b) * 128, (e * 2 + b) * 128 + 128))

        def l3_ffn_act(act, at, g):
            experts_act(act, at, E3, 2, ACT.Silu, None)

        def l3_ffn_dve(dve, at, g):
            experts_dve(dve, at, g, E3, 2, None)

        def l1_linear_pe(pe, at, z, lhs, i, ready):
            pe.wait_ge(*at("xnT_ready", ready))
            bias_pe(z.psB, "L1f_bias", U, i * 128)
            for u in range(U):
                ins = nc.tensor.matmul(un(z.psB, u), un(lhs, u), wt[:, i * 128:(i + 1) * 128], start=False,
                                       stop=(u == U - 1))
            ins.then_inc(z.sem("y_psum"), 1)

        def l1_ffn_pe(pe, at, z):
            z_flip_pe(pe, at, z, z.xn, 0)
            yield
            for blk in range(3):
                l1_linear_pe(pe, at, z, z.xnT, 2 * blk, 2 * blk + 1)
                yield
                z_flip_pe(pe, at, z, z.xm, U * (blk + 1))
                yield
                l1_linear_pe(pe, at, z, z.xmT, 2 * blk + 1, 2 * blk + 2)
                yield
                if blk < 2:
                    pe.wait_ge(*at("h_res", blk + 1))
                    for u in range(U):
                        ins = nc.tensor.transpose(un(z.psA, u), un(z.xn, u), ident)
                    ins.then_inc(z.sem("xnT_psum"), 1)
                    yield

        def l1_ffn_act(act, at, z):
            act.wait_ge(*at("xnT_psum", 1))
            nc.scalar.copy(z.xnT[:, :], z.psA[:, :]).then_inc(z.sem("xnT_ready"), 1)
            yield
            for blk in range(3):
                act.wait_ge(*at("xnT_psum", 2 * blk + 2))
                nc.scalar.activation(z.xmT[:, :], z.psA[:, :], ACT.Gelu, bias=col("L1f_b", blk),
                                     scale=col("L1f_g", blk)).then_inc(z.sem("xnT_ready"), 1)
                yield
                if blk < 2:
                    act.wait_ge(*at("xnT_psum", 2 * blk + 3))
                    nc.scalar.copy(z.xnT[:, :], z.psA[:, :]).then_inc(z.sem("xnT_ready"), 1)
                    yield

        def l1_ffn_dve(dve, at, z, g):
            z_load_dve(dve, at, z, g)
            yield
            dve.wait_ge(*at("xg_ready", 1))
            yield from z_norm_dve(dve, at, z, 0, z.xg, z.xn)
            for blk in range(3):
                dve.wait_ge(*at("y_psum", 2 * blk + 1))
                yield from z_norm_dve(dve, at, z, blk + 1, z.psB, z.xm)
                dve.wait_ge(*at("y_psum", 2 * blk + 2))
                nc.vector.tensor_tensor(z.xn[:, :], z.xn[:, :], z.psB[:, :], ALU.add).then_inc(z.sem("h_res"), 1)
                yield
            dve.wait_ge(*at("h_res", 3))
            nc.vector.tensor_tensor(x[:, bass.ts(g, GT)], z.xg[:, :], z.xn[:, :], ALU.add).then_inc(z.sem("g_done"), 1)
            yield

        def l1_ffn_pool(pool, at, z):
            for r in range(4):
                z_norm_pool(pool, at, z, r)
                yield

        NSMP = U * 4 * NSAMP

        class Pick:

            def __init__(self, z):
                flat = z.f.rearrange("p a t -> p (a t)")
                self.ksx = flat[:, 0:NSMP].rearrange("p (u j k) -> p u j k", u=U, j=4)
                self.xsT = flat[:, NSMP:NSMP + U * NSAMP]
                self.red = flat[:, 704:704 + 3 * U * H].rearrange("p (i n) -> p i n", i=3)
                self.cand = flat[0:U * H, 896:896 + 5 * S].rearrange("p (i s) -> p i s", i=5)
                self.top8 = flat[0:U * H, 1536:1568].rearrange("p (i n) -> p i n", i=4)

        def pick_pe(pe, at, z):
            k = Pick(z)
            pe.wait_ge(*at("xn_ready", U))
            for u in range(U):
                ins = nc.tensor.matmul(z.psF[0][:, u * NSAMP:(u + 1) * NSAMP], un(z.xn, u), onehot[:, :],
                                       start=True, stop=True)
            ins.then_inc(z.sem("smp_psum"), 1)
            z_flip_pe(pe, at, z, z.xn, 0)
            yield
            pe.wait_ge(*at("smp_ready", 1))
            nc.tensor.matmul(z.psF[1][:, 0:U * NSAMP], w("L2a_wk"), k.xsT, start=True,
                             stop=True).then_inc(z.sem("smp_psum"), 1)
            pe.wait_ge(*at("xnT_ready", 1))
            nc.tensor.matmul(z.psB, w("L2a_wq"), z.xnT[:, :], start=True, stop=True).then_inc(z.sem("q_psum"), 1)
            yield
            pe.wait_ge(*at("smp_ready", 5))
            pe.wait_ge(*at("q_ready", 1))
            for u in range(U):
                if u >= 1:
                    pe.wait_ge(*at("smp_red", 4 * u))
                for gq in range(4):
                    rs = slice(32 * gq, 32 * gq + 32)
                    ins = nc.tensor.matmul(z.pairs[gq // 2][:, gq % 2, 0:4 * NSAMP], z.qT[rs, u * S:(u + 1) * S],
                                           k.ksx[rs, u, :, :], start=True, stop=True)
                ins.then_inc(z.sem("smps_psum"), 1)
                yield
            pe.wait_ge(*at("m_step", 1))
            met_pe(pe)
            nc.tensor.transpose(z.psF[0][0:U * H, 0:S], k.red[:, 2, :], ident).then_inc(z.sem("mT_psum"), 1)
            yield
            pe.wait_ge(*at("top", 9))
            met_pe(pe)
            nc.tensor.transpose(z.psF[1][:, 0:U * H], k.cand[:, 4, :],
                                ident[0:U * H, 0:U * H]).then_inc(z.sem("sel_psum"), 1)
            yield

        def pick_act(act, at, z):
            act.wait_ge(*at("smp_psum", 1))
            nc.scalar.copy(Pick(z).xsT, z.psF[0][:, 0:U * NSAMP]).then_inc(z.sem("smp_ready"), 1)
            act.wait_ge(*at("xnT_psum", 1))
            nc.scalar.copy(z.xnT[:, :], z.psA[:, :]).then_inc(z.sem("xnT_ready"), 1)
            yield
            act.wait_ge(*at("q_psum", 1))
            nc.scalar.activation(z.qT[:, :], z.psB[:, :], ACT.Identity, bias=col("L2a_bq")).then_inc(z.sem("q_ready"), 1)
            yield

        def pick_dve(dve, at, z, g):
            k = Pick(z)
            z_load_dve(dve, at, z, g)
            yield
            dve.wait_ge(*at("xg_ready", 1))
            yield from z_norm_dve(dve, at, z, 0, z.xg, z.xn)
            dve.wait_ge(*at("smp_ready", 1))
            dve.wait_ge(*at("smp_psum", 2))
            for j in range(4):
                nc.vector.tensor_scalar(k.ksx[:, :, j, :], z.psF[1][:, 0:U * NSAMP].rearrange("p (u k) -> p u k", u=U),
                                        col("L2a_bk"), heads4[:, j:j + 1], ALU.add,
                                        ALU.mult).then_inc(z.sem("smp_ready"), 1)
            yield
            for u in range(U):
                dve.wait_ge(*at("smps_psum", u + 1))
                for n, op in ((0, ALU.max), (1, ALU.add)):
                    for half in range(2):
                        c = u * H + half * 8
                        nc.vector.tensor_reduce(k.red[:, n, c:c + 8].rearrange("p (b j) -> p b j", b=2),
                                                z.pairs[half][:, :, 0:4 * NSAMP].rearrange("p b (j k) -> p b j k", j=4),
                                                AX.X, op).then_inc(z.sem("smp_red"), 1)
                yield
            dve.wait_ge(*at("smp_red", 16))
            nc.vector.scalar_tensor_tensor(out=k.red[:, 2, :], in0=k.red[:, 1, :], scalar=-1.0 / NSAMP,
                                           in1=k.red[:, 0, :], op0=ALU.mult, op1=ALU.add).then_inc(z.sem("m_step"), 1)
            yield
            dve.wait_ge(*at("mT_psum", 1))
            nc.vector.tensor_copy(k.cand[:, 0, :], z.psF[0][0:U * H, 0:S]).then_inc(z.sem("top"), 1)
            yield
            dve.wait_ge(*at("top", 1))
            for r in range(3):
                met_dve(dve)
                nc.vector.max(k.top8[:, r, :], k.cand[:, r, :]).then_inc(z.sem("top"), 1)
                yield
                dve.wait_ge(*at("top", 2 + 2 * r))
                met_dve(dve)
                nc.vector.match_replace(k.cand[:, r + 1, :], k.top8[:, r, :], k.cand[:, r, :], GONE).then_inc(z.sem("top"), 1)
                yield
                dve.wait_ge(*at("top", 3 + 2 * r))
            met_dve(dve)
            nc.vector.max(k.top8[:, 3, :], k.cand[:, 3, :]).then_inc(z.sem("m_step"), 1)
            yield
            dve.wait_ge(*at("m_step", 2))
            nc.vector.memset(k.top8[:, 3, 1:8], GONE).then_inc(z.sem("m_step"), 1)
            yield
            dve.wait_ge(*at("m_step", 3))
            met_dve(dve)
            nc.vector.match_replace(k.cand[:, 4, :], k.top8[:, 3, :], k.cand[:, 3, :], GONE).then_inc(z.sem("top"), 1)
            yield
            dve.wait_ge(*at("top", 8))
            nc.vector.tensor_scalar(k.cand[:, 4, :], k.cand[:, 4, :], GONE, None, ALU.is_equal).then_inc(z.sem("top"), 1)
            yield
            dve.wait_ge(*at("sel_psum", 1))
            nc.vector.tensor_scalar(sel_all[:, 0, bass.ts(g, U * H)], z.psF[1][:, 0:U * H], 1.0, None,
                                    ALU.mult).then_inc(z.sem("sel_ready"), 1)
            nc.vector.tensor_scalar(sel_all[:, 1, bass.ts(g, U * H)], z.psF[1][:, 0:U * H], -1.0, 1.0, ALU.mult,
                                    ALU.add).then_inc(z.sem("sel_ready"), 1)
            dve.wait_ge(*at("sel_ready", 2))
            dve.sem_inc(z.sem("g_done"), 1)
            yield

        def l2_xattn_pe(pe, at, g):
            pe.wait_ge(*at("ctx_ready", 1))
            for b in range(8):
                if b >= 2:
                    pe.wait_ge(*at("k_ready", b - 1))
                nc.tensor.matmul(psS[0][:, b % 2, 0:U * SC], w("L2x_wkv", b * 128, b * 128 + 128), ctxg[:, :],
                                 start=True, stop=True).then_inc(sem["k_psum"], 1)
            for n in range(8):
                u, c = divmod(n, 2)
                if n >= 2:
                    pe.wait_ge(*at("v_ready", n - 1))
                nc.tensor.matmul(psS[1][0:SC, c, :], ctxg[:, u * SC:(u + 1) * SC],
                                 w("L2x_wkv", 1024 + c * 512, 1024 + c * 512 + 512), start=True,
                                 stop=True).then_inc(sem["v_psum"], 1)
            flip_pe(pe, at, 0, xm, "xn_ready", U)
            pe.wait_ge(*at("xnT_ready", 1))
            for b in range(8):
                if b >= 2:
                    pe.wait_ge(*at("q_ready", b - 1))
                nc.tensor.matmul(psT[:, b % 2, :], w("L2x_wq", b * 128, b * 128 + 128), xmT[:, :],
                                 start=True, stop=True).then_inc(sem["q_psum"], 1)
            pe.wait_ge(*at("q_ready", 8))
            pe.wait_ge(*at("k_ready", 8))
            pe.wait_ge(*at("v_ready", 8))
            n = 4 * U

            def score(i):
                u, quarter = divmod(i, 4)
                if i >= 2:
                    pe.wait_ge(*at("s_sub", i - 1))
                for j in range(4):
                    h = quarter * 4 + j
                    rs = slice(64 * (h % 2), 64 * (h % 2) + 64)
                    ins = nc.tensor.matmul(psS[i % 2][:, h % 2, (j // 2) * SC:(j // 2 + 1) * SC],
                                           qT8[rs, h // 2, u * S:(u + 1) * S],
                                           kT8[rs, h // 2, u * SC:(u + 1) * SC], start=True, stop=True)
                ins.then_inc(sem["s_psum"], 1)

            def turn(i):
                pe.wait_ge(*at("s_nrm", i + 1))
                if i >= 2:
                    pe.wait_ge(*at("pt_ready", i - 1))
                for j in range(4):
                    ins = nc.tensor.transpose(psT[0:SC, i % 2, j * S:(j + 1) * S],
                                              p4[:, i % 4, j * SC:(j + 1) * SC], ident)
                ins.then_inc(sem["pt_psum"], 1)

            def value(i):
                u, quarter = divmod(i, 4)
                pe.wait_ge(*at("pt_ready", i + 1))
                if i >= 1:
                    pe.wait_ge(*at("oT_ready", i))
                for j in range(4):
                    h = quarter * 4 + 2 * (j % 2) + j // 2
                    c0 = (j % 2) * S
                    ins = nc.tensor.matmul(psB[64 * (h % 2):64 * (h % 2) + 64, c0:c0 + S],
                                           v8[0:SC, u, h * DX:(h + 1) * DX], pT4[0:SC, i % 4, j, :],
                                           start=True, stop=True)
                ins.then_inc(sem["o_psum"], 1)

            def out(u):
                pe.wait_ge(*at("oT_ready", 4 * u + 4))
                for b in range(8):
                    nc.tensor.matmul(un(psA, u), fT[:, u % 2, :, :].rearrange("p a t -> p (a t)")[:, b * S:(b + 1) * S],
                                     w("L2x_wo", b * 128, b * 128 + 128), start=(b == 0), stop=False)
                return nc.tensor.matmul(un(psA, u), ones_row, row("L2x_bo"), start=False, stop=True)

            for t in range(n + 5):
                if t < n:
                    score(t)
                if 2 <= t < n + 2:
                    turn(t - 2)
                if 3 <= t < n + 3:
                    value(t - 3)
                if t >= 8 and t % 4 == 0:
                    ins = out(t // 4 - 2)
            ins.then_inc(sem["y_psum"], 1)

        def l2_xattn_act(act, at, g):
            for b in range(8):
                act.wait_ge(*at("k_psum", b + 1))
                nc.scalar.copy(kT8[:, b, :], psS[0][:, b % 2, 0:U * SC]).then_inc(sem["k_ready"], 1)
            for n in range(8):
                u, c = divmod(n, 2)
                act.wait_ge(*at("v_psum", n + 1))
                nc.scalar.copy(v8[0:SC, u, c * 512:(c + 1) * 512], psS[1][0:SC, c, :]).then_inc(sem["v_ready"], 1)
            act.wait_ge(*at("xnT_psum", 1))
            nc.scalar.activation(xmT[:, :], psA[:, :], ACT.Identity, bias=col("L2x_b"),
                                 scale=col("L2x_g")).then_inc(sem["xnT_ready"], 1)
            for b in range(8):
                act.wait_ge(*at("q_psum", b + 1))
                nc.scalar.mul(qT8[:, b, :], psT[:, b % 2, :], float(DX) ** -0.5).then_inc(sem["q_ready"], 1)
            n = 4 * U
            for t in range(n + 4):
                if t >= 4:
                    i = t - 4
                    u, quarter = divmod(i, 4)
                    act.wait_ge(*at("o_psum", i + 1))
                    dst = fT[:, u % 2, :, :].rearrange("p a t -> p (a t)")[:, quarter * 256:(quarter + 1) * 256]
                    nc.scalar.copy(dst, psB[:, 0:256]).then_inc(sem["oT_ready"], 1)
                if 2 <= t < n + 2:
                    i = t - 2
                    act.wait_ge(*at("pt_psum", i + 1))
                    if i >= 4:
                        act.wait_ge(*at("o_psum", i - 3))
                    nc.scalar.copy(pT4[0:SC, i % 4, :, :].rearrange("p j s -> p (j s)"),
                                   psT[0:SC, i % 2, :]).then_inc(sem["pt_ready"], 1)
                if t < n:
                    act.wait_ge(*at("s_sub", t + 1))
                    pv = p4[:, t % 4, 0:4 * SC]
                    nc.scalar.activation(pv, pv, ACT.Exp).then_inc(sem["p_ready"], 1)

        def l2_xattn_dve(dve, at, g):
            norm_in_dve(dve, at, g)
            norm_dve(dve, at, 1, lambda u: un(xn, u), lambda u: un(xm, u), after=lambda u: at("xn_ready", u + 1))
            n = 4 * U

            def softmax(i):
                k = i % 2
                sv = psS[k][:, :, 0:2 * SC].rearrange("p b (j k) -> p b j k", j=2)
                mx = smx[:, k, 0:4].rearrange("p (b j) -> p b j", b=2)
                pv = p4[:, i % 4, 0:4 * SC].rearrange("p (b j k) -> p b j k", b=2, j=2)
                dve.wait_ge(*at("s_psum", i + 1))
                nc.vector.tensor_reduce(mx, sv, AX.X, ALU.max).then_inc(sem["s_max"], 1)
                dve.wait_ge(*at("s_max", i + 1))
                if i >= 4:
                    dve.wait_ge(*at("pt_psum", i - 3))
                nc.vector.tensor_tensor(pv, sv, mx.unsqueeze(3).broadcast_to([128, 2, 2, SC]),
                                        ALU.subtract).then_inc(sem["s_sub"], 1)

            def normalise(i):
                k = i % 2
                pv = p4[:, i % 4, 0:4 * SC].rearrange("p (j k) -> p j k", j=4)
                dve.wait_ge(*at("p_ready", i + 1))
                nc.vector.tensor_reduce(rec[:, k, 0:4], pv, AX.X, ALU.add).then_inc(sem["s_sum"], 1)
                dve.wait_ge(*at("s_sum", i + 1))
                nc.vector.reciprocal(rec[:, k, 4:8], rec[:, k, 0:4]).then_inc(sem["s_rec"], 1)
                dve.wait_ge(*at("s_rec", i + 1))
                nc.vector.tensor_tensor(pv, pv, rec[:, k, 4:8].unsqueeze(2).broadcast_to([128, 4, SC]),
                                        ALU.mult).then_inc(sem["s_nrm"], 1)

            for t in range(n + 1):
                if t < n:
                    softmax(t)
                if t >= 1:
                    normalise(t - 1)
            dve.wait_ge(*at("y_psum", 1))
            nc.vector.scalar_tensor_tensor(out=x[:, bass.ts(g, GT)], in0=psA[:, :], scalar=gate[:, 1:2],
                                           in1=xg[:, :], op0=ALU.mult, op1=ALU.add).then_inc(sem["x_done"], 1)

        def l2_xattn_pool(pool, at, g):
            ctx_pool(pool, at, g)
            norm_pool(pool, at, 0)
            norm_pool(pool, at, 1)

        def l2_ffn_pe(pe, at, z):
            z_flip_pe(pe, at, z, z.xn, 0)
            yield
            pe.wait_ge(*at("xnT_ready", 1))
            nc.tensor.matmul(z.psB[0:32, :], w("L2f_u1"), z.xnT[:, :], start=True, stop=True).then_inc(z.sem("q_psum"), 1)
            yield
            pe.wait_ge(*at("q_ready", 1))
            for b in range(4):
                if b >= 2:
                    pe.wait_ge(*at("f_ready", b - 1))
                nc.tensor.matmul(z.psF[b % 2], w("L2f_v1", b * 128, b * 128 + 128)[0:32, :], z.qT[0:32, :],
                                 start=True, stop=True).then_inc(z.sem("f_psum"), 1)
                if b % 2:
                    yield
            for b in range(4):
                pe.wait_ge(*at("f_ready", b + 1))
                ins = nc.tensor.matmul(z.psB[0:32, :], w("L2f_u2", b * 32, b * 32 + 32), z.f[:, b, :],
                                       start=(b == 0), stop=(b == 3))
            ins.then_inc(z.sem("o_psum"), 1)
            yield
            pe.wait_ge(*at("oT_ready", 1))
            bias_pe(z.psA, "L2f_b2", U)
            for u in range(U):
                ins = nc.tensor.matmul(un(z.psA, u), z.oT[0:32, u * S:(u + 1) * S], w("L2f_v2")[0:32, :], start=False,
                                       stop=(u == U - 1))
            ins.then_inc(z.sem("y_psum"), 1)
            yield

        def l2_ffn_act(act, at, z):
            act.wait_ge(*at("xnT_psum", 1))
            nc.scalar.copy(z.xnT[:, :], z.psA[:, :]).then_inc(z.sem("xnT_ready"), 1)
            yield
            act.wait_ge(*at("q_psum", 1))
            nc.scalar.copy(z.qT[0:32, :], z.psB[0:32, :]).then_inc(z.sem("q_ready"), 1)
            yield
            for b in range(4):
                act.wait_ge(*at("f_psum", b + 1))
                nc.scalar.activation(z.f[:, b, :], z.psF[b % 2], ACT.Gelu_apprx_tanh,
                                     bias=col("L2f_b1", b)).then_inc(z.sem("f_ready"), 1)
                if b % 2:
                    yield
            act.wait_ge(*at("o_psum", 1))
            nc.scalar.copy(z.oT[0:32, :], z.psB[0:32, :]).then_inc(z.sem("oT_ready"), 1)
            yield

        def l2_ffn_dve(dve, at, z, g):
            z_load_dve(dve, at, z, g)
            yield
            dve.wait_ge(*at("xg_ready", 1))
            yield from z_norm_dve(dve, at, z, 0, z.xg, z.xn)
            dve.wait_ge(*at("y_psum", 1))
            nc.vector.tensor_tensor(x[:, bass.ts(g, GT)], z.xg[:, :], z.psA[:, :], ALU.add).then_inc(z.sem("g_done"), 1)
            yield

        def one_norm_pool(pool, at, z):
            z_norm_pool(pool, at, z, 0)
            yield

        def pair(t, a=0, b=None):
            return t.rearrange("p (u n) -> p u n", u=2)[:, :, a:b]

        def l3_attn_pe(pe, at, z):
            def keys_values(half):
                pe.wait_ge(*at("k_ready", half + 1))
                pe.wait_ge(*at("v_ready", half + 1))
                if half:
                    pe.wait_ge(*at("kv_ready", 3))
                for i in range(2):
                    c = i * 256
                    nc.tensor.matmul(z.psA[:, c:c + D], z.f[:, half, c:c + 128], z.f[:, half, c + 128:c + 256],
                                     start=True, stop=True)
                    ins = nc.tensor.matmul(z.psA[:, c + D:c + D + 2], z.f[:, half, c:c + 128], ones[:, 0:2],
                                           start=True, stop=True)
                ins.then_inc(z.sem("s_psum"), 1)

            def outputs(half):
                pe.wait_ge(*at("kv_ready", 3 * half + 3))
                for i in range(2):
                    ins = nc.tensor.matmul(z.psF[half][:, i * 256:i * 256 + D + H], un(z.qT, 2 * half + i),
                                           z.f[:, 2, i * 256:i * 256 + D + H], start=True, stop=True)
                ins.then_inc(z.sem("o_psum"), 1)

            z_flip_pe(pe, at, z, z.xn, 0)
            yield
            pe.wait_ge(*at("xnT_ready", 1))
            nc.tensor.matmul(z.psB, w("L3a_wqkv", 0, 128), z.xnT[:, :], start=True, stop=True).then_inc(z.sem("q_psum"), 1)
            for half in range(2):
                for i in range(2):
                    ins = nc.tensor.matmul(z.psF[half][:, i * 256:i * 256 + 256], un(z.xnT, 2 * half + i),
                                           w("L3a_wqkv", 128, 384), start=True, stop=True)
                ins.then_inc(z.sem("k_psum"), 1)
            yield
            keys_values(0)
            yield
            pe.wait_ge(*at("q_ready", 1))
            outputs(0)
            keys_values(1)
            yield
            outputs(1)
            yield
            pe.wait_ge(*at("o_ready", U))
            for u in range(U):
                ins = nc.tensor.transpose(un(z.psB, u), un(z.on, u), ident)
            ins.then_inc(z.sem("oT_psum"), 1)
            yield
            pe.wait_ge(*at("oT_ready", 1))
            for u in range(U):
                ins = nc.tensor.matmul(un(z.psA, u), un(z.oT, u), w("L3a_wo"), start=True, stop=True)
            ins.then_inc(z.sem("y_psum"), 1)
            yield

        def l3_attn_act(act, at, z):
            act.wait_ge(*at("xnT_psum", 1))
            nc.scalar.copy(z.xnT[:, :], z.psA[:, :]).then_inc(z.sem("xnT_ready"), 1)
            yield
            act.wait_ge(*at("elu_min", 1))
            nc.scalar.activation(z.xm[:, :], z.xm[:, :], ACT.Exp).then_inc(z.sem("elu_exp"), 1)
            for half in range(2):
                act.wait_ge(*at("elu_min", half + 2))
                nc.scalar.copy(pair(z.f[:, half, :], 128, 256), pair(z.psF[half], 128, 256)).then_inc(z.sem("v_ready"), 1)
                k = z.xmT[:, half * 256:(half + 1) * 256]
                nc.scalar.activation(k, k, ACT.Exp).then_inc(z.sem("elu_exp"), 1)
            yield
            act.wait_ge(*at("oT_psum", 1))
            nc.scalar.copy(z.oT[:, :], z.psB[:, :]).then_inc(z.sem("oT_ready"), 1)
            yield

        def l3_attn_dve(dve, at, z, g):
            def mask_sums(half):
                dve.wait_ge(*at("s_psum", half + 1))
                if half:
                    dve.wait_ge(*at("o_psum", 1))
                nc.vector.tensor_tensor(pair(z.f[:, 2, :], 0, D), pair(z.psA, 0, D),
                                        bdiag.unsqueeze(1).broadcast_to([128, 2, D]),
                                        ALU.mult).then_inc(z.sem("kv_ready"), 1)
                for i in range(2):
                    nc.vector.tensor_scalar(z.f[:, 2, i * 256 + D:i * 256 + D + H], bdiag16,
                                            z.psA[:, i * 256 + D:i * 256 + D + 1], None,
                                            ALU.mult).then_inc(z.sem("kv_ready"), 1)

            def divide(half):
                dve.wait_ge(*at("o_psum", half + 1))
                r = z.f[:, 3, half * 2 * H:(half + 1) * 2 * H]
                nc.vector.tensor_scalar(r.rearrange("p (u h) -> p u h", u=2), pair(z.psF[half], D, D + H), 1e-6, None,
                                        ALU.max).then_inc(z.sem("o_recip"), 1)
                dve.wait_ge(*at("o_recip", 2 * half + 1))
                nc.vector.reciprocal(r, r).then_inc(z.sem("o_recip"), 1)
                dve.wait_ge(*at("o_recip", 2 * half + 2))
                for i in range(2):
                    nc.vector.tensor_tensor(un(z.on, 2 * half + i).rearrange("p (h e) -> p h e", h=H),
                                            z.psF[half][:, i * 256:i * 256 + D].rearrange("p (h e) -> p h e", h=H),
                                            r[:, i * H:(i + 1) * H].unsqueeze(2).broadcast_to([128, H, DH]),
                                            ALU.mult).then_inc(z.sem("o_ready"), 1)

            z_load_dve(dve, at, z, g)
            yield
            dve.wait_ge(*at("xg_ready", 1))
            yield from z_norm_dve(dve, at, z, 0, z.xg, z.xn)
            dve.wait_ge(*at("q_psum", 1))
            nc.vector.tensor_scalar(z.xm[:, :], z.psB[:, :], 0.0, None, ALU.min).then_inc(z.sem("elu_min"), 1)
            for half in range(2):
                dve.wait_ge(*at("k_psum", half + 1))
                nc.vector.tensor_scalar(z.xmT[:, half * 256:(half + 1) * 256].rearrange("p (u n) -> p u n", u=2),
                                        pair(z.psF[half], 0, D), 0.0, None, ALU.min).then_inc(z.sem("elu_min"), 1)
            yield
            dve.wait_ge(*at("elu_exp", 1))
            nc.vector.scalar_tensor_tensor(out=z.qT[:, :], in0=z.psB[:, :], scalar=0.0, in1=z.xm[:, :],
                                           op0=ALU.max, op1=ALU.add).then_inc(z.sem("q_ready"), 1)
            for half in range(2):
                dve.wait_ge(*at("v_ready", half + 1))
                dve.wait_ge(*at("elu_exp", half + 2))
                nc.vector.scalar_tensor_tensor(out=pair(z.f[:, half, :], 0, D), in0=pair(z.psF[half], 0, D), scalar=0.0,
                                               in1=z.xmT[:, half * 256:(half + 1) * 256].rearrange(
                                                   "p (u n) -> p u n", u=2),
                                               op0=ALU.max, op1=ALU.add).then_inc(z.sem("k_ready"), 1)
            yield
            mask_sums(0)
            yield
            mask_sums(1)
            yield
            divide(0)
            yield
            divide(1)
            yield
            dve.wait_ge(*at("y_psum", 1))
            nc.vector.tensor_tensor(x[:, bass.ts(g, GT)], z.xg[:, :], z.psA[:, :], ALU.add).then_inc(z.sem("g_done"), 1)
            yield

        def l3_xattn_pe(pe, at, z):
            ctx_rows, kT, v = z.f[:, 1, 0:U * SC], z.xmT, z.xm
            pe.wait_ge(*at("ctx_ready", 1))
            nc.tensor.matmul(z.psF[0][:, 0:U * SC], w("L3x_wk"), ctx_rows, start=True,
                             stop=True).then_inc(z.sem("k_psum"), 1)
            for u in range(U):
                ins = nc.tensor.matmul(z.psF[1][0:SC, u * 128:(u + 1) * 128], ctx_rows[:, u * SC:(u + 1) * SC],
                                       w("L3x_wv"), start=True, stop=True)
            ins.then_inc(z.sem("v_psum"), 1)
            yield
            z_flip_pe(pe, at, z, z.xn, 0)
            yield
            pe.wait_ge(*at("xnT_ready", 1))
            nc.tensor.matmul(z.psB, w("L3x_wq"), z.xnT[:, :], start=True, stop=True).then_inc(z.sem("q_psum"), 1)
            yield
            pe.wait_ge(*at("q_ready", 1))
            pe.wait_ge(*at("k_ready", 1))
            for u in range(U):
                ins = nc.tensor.matmul(z.psF[0][:, u * SC:(u + 1) * SC], un(z.qT, u), kT[:, u * SC:(u + 1) * SC],
                                       start=True, stop=True)
            ins.then_inc(z.sem("s_psum"), 1)
            yield
            pe.wait_ge(*at("s_nrm", 1))
            pe.wait_ge(*at("v_ready", 1))
            for u in range(U):
                ins = nc.tensor.transpose(z.psF[1][0:SC, u * S:(u + 1) * S], z.on[:, u * SC:(u + 1) * SC], ident)
            ins.then_inc(z.sem("pt_psum"), 1)
            yield
            pe.wait_ge(*at("pt_ready", 1))
            for u in range(U):
                ins = nc.tensor.matmul(un(z.psB, u), v[0:SC, u * 128:(u + 1) * 128], z.f[0:SC, 0, u * S:(u + 1) * S],
                                       start=True, stop=True)
            ins.then_inc(z.sem("oT_psum"), 1)
            yield
            pe.wait_ge(*at("oT_ready", 1))
            bias_pe(z.psA, "L3x_bo", U)
            for u in range(U):
                ins = nc.tensor.matmul(un(z.psA, u), un(z.oT, u), w("L3x_wo"), start=False, stop=(u == U - 1))
            ins.then_inc(z.sem("y_psum"), 1)
            yield

        def l3_xattn_act(act, at, z):
            act.wait_ge(*at("k_psum", 1))
            nc.scalar.copy(z.xmT[:, 0:U * SC], z.psF[0][:, 0:U * SC]).then_inc(z.sem("k_ready"), 1)
            act.wait_ge(*at("v_psum", 1))
            nc.scalar.copy(z.xm[0:SC, :], z.psF[1][0:SC, :]).then_inc(z.sem("v_ready"), 1)
            yield
            act.wait_ge(*at("xnT_psum", 1))
            nc.scalar.copy(z.xnT[:, :], z.psA[:, :]).then_inc(z.sem("xnT_ready"), 1)
            yield
            act.wait_ge(*at("q_psum", 1))
            nc.scalar.activation(z.qT[:, :], z.psB[:, :], ACT.Identity, bias=col("L3x_bq")).then_inc(z.sem("q_ready"), 1)
            yield
            act.wait_ge(*at("s_sub", 1))
            nc.scalar.activation(z.on[:, 0:U * SC], z.on[:, 0:U * SC], ACT.Exp,
                                 scale=float(np.float32(1.0) / np.sqrt(np.float32(D)))).then_inc(z.sem("p_ready"), 1)
            yield
            act.wait_ge(*at("pt_psum", 1))
            nc.scalar.copy(z.f[0:SC, 0, :], z.psF[1][0:SC, :]).then_inc(z.sem("pt_ready"), 1)
            yield
            act.wait_ge(*at("oT_psum", 1))
            nc.scalar.activation(z.oT[:, :], z.psB[:, :], ACT.Identity, bias=col("L3x_bv")).then_inc(z.sem("oT_ready"), 1)
            yield

        def l3_xattn_dve(dve, at, z, g):
            z_load_dve(dve, at, z, g)
            yield
            dve.wait_ge(*at("xg_ready", 1))
            yield from z_norm_dve(dve, at, z, 0, z.xg, z.xn)
            sv = z.psF[0][:, 0:U * SC].rearrange("p (u k) -> p u k", u=U)
            pv = z.on[:, 0:U * SC].rearrange("p (u k) -> p u k", u=U)
            mx, total, inverse = z.f[:, 2, 0:U], z.f[:, 2, U:2 * U], z.f[:, 2, 2 * U:3 * U]
            dve.wait_ge(*at("s_psum", 1))
            nc.vector.tensor_reduce(mx, sv, AX.X, ALU.max).then_inc(z.sem("s_max"), 1)
            yield
            dve.wait_ge(*at("s_max", 1))
            nc.vector.tensor_tensor(pv, sv, mx.unsqueeze(2).broadcast_to([128, U, SC]),
                                    ALU.subtract).then_inc(z.sem("s_sub"), 1)
            yield
            dve.wait_ge(*at("p_ready", 1))
            nc.vector.tensor_reduce(total, pv, AX.X, ALU.add).then_inc(z.sem("s_sum"), 1)
            yield
            dve.wait_ge(*at("s_sum", 1))
            nc.vector.reciprocal(inverse, total).then_inc(z.sem("s_rec"), 1)
            yield
            dve.wait_ge(*at("s_rec", 1))
            nc.vector.tensor_tensor(pv, pv, inverse.unsqueeze(2).broadcast_to([128, U, SC]),
                                    ALU.mult).then_inc(z.sem("s_nrm"), 1)
            yield
            dve.wait_ge(*at("y_psum", 1))
            nc.vector.tensor_tensor(x[:, bass.ts(g, GT)], z.xg[:, :], z.psA[:, :], ALU.add).then_inc(z.sem("g_done"), 1)
            yield

        def l3_xattn_pool(pool, at, z, g):
            pool.wait_ge(*at("g_done", 0))
            nc.gpsimd.tensor_copy(z.f[:, 1, 0:U * SC], ctxT[:, bass.ts(g, U * SC)]).then_inc(z.sem("ctx_ready"), 1)
            yield
            z_norm_pool(pool, at, z, 0)
            yield

        STREAM_PROGRAM = {
            "L0_attn_ff": (l0_ff_pe, l0_ff_act, l0_ff_dve, l0_ff_pool),
            "L1_ffn": (l1_ffn_pe, l1_ffn_act, l1_ffn_dve, l1_ffn_pool),
            "L2_attn_pick": (pick_pe, pick_act, pick_dve, one_norm_pool),
            "L2_ffn": (l2_ffn_pe, l2_ffn_act, l2_ffn_dve, one_norm_pool),
            "L3_attn": (l3_attn_pe, l3_attn_act, l3_attn_dve, one_norm_pool),
            "L3_xattn": (l3_xattn_pe, l3_xattn_act, l3_xattn_dve, l3_xattn_pool),
        }
        PROGRAM = {
            "L0_ffn_pre": (l0_pre_pe, l0_pre_act, l0_pre_dve, pre_pool),
            "L0_ffn": (l0_ffn_pe, l0_ffn_act, l0_ffn_dve, None),
            "L2_xattn": (l2_xattn_pe, l2_xattn_act, l2_xattn_dve, l2_xattn_pool),
            "L3_ffn_pre": (l3_pre_pe, l3_pre_act, l3_pre_dve, pre_pool),
            "L3_ffn": (l3_ffn_pe, l3_ffn_act, l3_ffn_dve, None),
        }

        @block.tensor
        def _(pe):
            pe.wait_ge(first_in, 32)
            pe.wait_ge(setup_v, 6)
            pe.wait_ge(setup_g, 1)
            for b in BLOCKS:
                if b == "L0_attn_ff":
                    pe.wait_ge(small_in, 16 * SMALL)
                if b == "L1_ffn":
                    pe.wait_ge(loaded[b], 16)
                    pe.wait_ge(sem["x_done"], BASE[b]["x_done"])
                    for i in range(6):
                        bank = psS[i // 4][:, 0, (i % 4) * 128:(i % 4) * 128 + 128]
                        ins = nc.tensor.matmul(bank, w("L1f_la", i * 128, i * 128 + 128)[0:32, :],
                                               w("L1f_lb", i * 128, i * 128 + 128)[0:32, :], start=True, stop=True)
                    ins.then_inc(lora_psum, 1)
                    pe.wait_ge(setup_v, 8)
                if b in loaded and b != "L0_attn":
                    pe.wait_ge(loaded[b], 16)
                if b.endswith("_pre"):
                    pe.wait_ge(loaded[b[:-4]], 16)
                if b.endswith("_ffn") and b + "_pre" in BLOCKS:
                    pe.wait_ge(sem["x_done"], BASE[b]["x_done"])
                if b == "L0_attn_ff":
                    pe.wait_ge(loaded["L0_attn"], 16)
                if b == "L2_attn_pick":
                    pe.wait_ge(loaded["L2_attn"], 16)
                if b in STREAMED:
                    run_streams(pe, b, STREAM_PROGRAM[b][0])
                    continue
                if b in HEADS_OF:
                    run_heads(pe, b, HEADS_PROGRAM[0], HEADS_OF[b])
                    continue
                if b.endswith("_pre"):
                    PROGRAM[b][0](pe, Counts(b, 0), 0)
                    continue
                with pe.Fori(0, NG) as g:
                    PROGRAM[b][0](pe, Counts(b, g), g)

        @block.scalar
        def _(act):
            act.wait_ge(first_in, 32)
            act.wait_ge(setup_g, 1)
            for b in BLOCKS:
                if b == "L0_attn_ff":
                    act.wait_ge(small_in, 16 * SMALL)
                    nc.scalar.activation(gate[:, 1:2], gate[:, 0:1], ACT.Tanh).then_inc(setup_a, 1)
                if b == "L0_xattn":
                    act.wait_ge(setup_g, SETUP_G)
                if b.endswith("_ffn") and b + "_pre" in BLOCKS:
                    act.wait_ge(sem["x_done"], BASE[b]["x_done"])
                if b in STREAMED:
                    run_streams(act, b, STREAM_PROGRAM[b][1])
                    continue
                if b in HEADS_OF:
                    run_heads(act, b, HEADS_PROGRAM[1], HEADS_OF[b])
                    continue
                if b.endswith("_pre"):
                    PROGRAM[b][1](act, Counts(b, 0), 0)
                    continue
                with act.Fori(0, NG) as g:
                    PROGRAM[b][1](act, Counts(b, g), g)

        def setup_pool(pool):
            pool.wait_ge(small_in, 16 * SMALL)
            for i, pre in enumerate(KBIAS):
                h4 = heads4s if pre == "L0x" else heads4
                nc.gpsimd.tensor_scalar(kb4[:, i, :], h4, col(pre + "_bk"), None, ALU.mult).then_inc(setup_g, 1)
            nc.gpsimd.tensor_scalar(cmask[:, :], pad_u8, -3.0e38, 4.0, ALU.mult, ALU.mult).then_inc(setup_g, 1)
            pool.wait_ge(setup_g, 5)
            nc.gpsimd.tensor_tensor(cmask[:, :].rearrange("p (b k) -> p b k", b=NB),
                                    cmask[:, :].rearrange("p (b k) -> p b k", b=NB),
                                    amask[:, :].unsqueeze(1).broadcast_to([128, NB, SC]),
                                    ALU.add).then_inc(setup_g, 1)
            nc.gpsimd.tensor_copy(idx_f[:, 0, :], idx_i[:, :]).then_inc(setup_g, 1)
            pool.wait_ge(setup_g, 7)
            nc.gpsimd.tensor_scalar(idx_f[:, 1, :], idx_f[:, 0, :], 0.0, float(S), ALU.is_lt,
                                    ALU.mult).then_inc(setup_g, 1)
            pool.wait_ge(setup_g, 8)
            nc.gpsimd.tensor_tensor(idx_f[:, 0, :], idx_f[:, 0, :], idx_f[:, 1, :], ALU.add).then_inc(setup_g, 1)
            pool.wait_ge(setup_g, 9)
            nc.gpsimd.tensor_scalar(idx_f[:, 1, :], idx_f[:, 0, :], 0.0, float(S - 1), ALU.max,
                                    ALU.min).then_inc(setup_g, 1)
            pool.wait_ge(setup_g, 10)
            nc.gpsimd.tensor_scalar(onehot[:, :], idx_f[:, 1, :], part, None, ALU.is_equal).then_inc(setup_g, 1)
            nc.gpsimd.tensor_scalar(wt[:, :], qw, 1.0 / 7.5, -1.0, ALU.mult, ALU.add).then_inc(setup_g, 1)
            pool.wait_ge(setup_g, 12)
            nc.gpsimd.tensor_tensor(wt[:, :], wt[:, :], scl, ALU.mult).then_inc(setup_g, 1)

        @block.gpsimd
        def _(pool):
            nc.gpsimd.memset(neghalf[:, :], -0.5)
            nc.gpsimd.memset(mean_w[:, :], 1.0 / S)
            nc.gpsimd.memset(vx_all[:, :, :], 1.0).then_inc(setup_g, 1)
            pool.wait_ge(setup_g, 1)
            for b in BLOCKS:
                if b == "L0_attn_ff":
                    setup_pool(pool)
                if b in STREAMED:
                    pool.wait_ge(sem["x_done"], BASE[b]["x_done"])
                    run_streams(pool, b, STREAM_PROGRAM[b][3], with_group=(b == "L3_xattn"))
                    continue
                if b in HEADS_OF:
                    run_heads(pool, b, HEADS_PROGRAM[3], HEADS_OF[b])
                    continue
                if PROGRAM[b][3] is None:
                    continue
                if b.endswith("_pre"):
                    PROGRAM[b][3](pool, Counts(b, 0), 0)
                    continue
                with pool.Fori(0, NG) as g:
                    PROGRAM[b][3](pool, Counts(b, g), g)

        @block.vector
        def _(dve):
            nc.vector.memset(ones[:, :], 1.0)
            dve.wait_ge(first_in, 32)
            nc.vector.tensor_copy(window_bf[:, :], const("window"))
            nc.vector.tensor_copy(ident_bf[:, :], ident).then_inc(setup_v, 1)
            nc.vector.memset(ones_bf[:, :], 1.0)
            rest = [rows[:, :], fT[0:3, 1, :, :].rearrange("p a t -> p (a t)")[:, 0:NROWS]]
            for k in range(2):
                nc.vector.tensor_copy(rows_bf[:, :], rest[k]).then_inc(setup_v, 1)
                dve.wait_ge(setup_v, 2 + 2 * k)
                nc.vector.scalar_tensor_tensor(out=rest[1], in0=rows_bf[:, :], scalar=const("drop")[0:3, k:k + 1],
                                               in1=rest[k], op0=ALU.mult, op1=ALU.add).then_inc(setup_v, 1)
                dve.wait_ge(setup_v, 3 + 2 * k)
            nc.vector.tensor_copy(rows_bf[:, :], rest[1]).then_inc(setup_v, 1)
            dve.wait_ge(setup_g, 1)
            dve.wait_ge(x_in, 16)
            for name, n in SETUP_COUNTS.items():
                dve.sem_inc(sem[name], n)
            for b in BLOCKS:
                if b == "L0_attn_ff":
                    dve.wait_ge(small_in, 16 * SMALL)
                    dve.wait_ge(setup_a, 1)
                if b == "L0_xattn":
                    dve.wait_ge(setup_g, SETUP_G)
                if b == "L1_ffn":
                    dve.wait_ge(lora_psum, 1)
                    nc.vector.tensor_tensor(wt[:, 0:512], wt[:, 0:512], psS[0][:, 0, :], ALU.add).then_inc(setup_v, 1)
                    nc.vector.tensor_tensor(wt[:, 512:768], wt[:, 512:768], psS[1][:, 0, 0:256],
                                            ALU.add).then_inc(setup_v, 1)
                if b in STREAMED:
                    dve.wait_ge(sem["x_done"], BASE[b]["x_done"])
                    run_streams(dve, b, STREAM_PROGRAM[b][2], with_group=True)
                    for name in ("g_done", "g_done2"):
                        dve.wait_ge(sem[name], BASE[b][name] + GROUPS[b])
                    dve.sem_inc(sem["x_done"], GROUPS[b])
                    continue
                if b in HEADS_OF:
                    run_heads(dve, b, HEADS_PROGRAM[2], HEADS_OF[b])
                    continue
                if b.endswith("_pre"):
                    PROGRAM[b][2](dve, Counts(b, 0), 0)
                    continue
                with dve.Fori(0, NG) as g:
                    PROGRAM[b][2](dve, Counts(b, g), g)


def block_cols(wm, n):
    k, c = wm.shape
    return wm.reshape(n, k // n, c).transpose(1, 0, 2).reshape(k // n, n * c)


def pad_rows(a):
    return np.concatenate([a, np.zeros((128 - a.shape[0], a.shape[1]), a.dtype)], axis=0)


ROT = np.array([c + 1 - 2 * (c % 2) for c in range(D)])


def shape_constants():
    i = np.arange(128)
    cos = np.ones((128, S), np.float32)
    sin = np.zeros((128, S), np.float32)
    tok = np.arange(S)
    for c in range(128):
        e = c % DH
        if e < 6:
            pos = [np.zeros(S), tok // 16, tok % 16][e // 2].astype(np.float32)
            cos[c], sin[c] = np.cos(pos), np.sin(pos)
            if e % 2 == 0:
                sin[c] = -sin[c]
    parts = dict(
        ident=np.eye(128), bdiag=(i[:, None] // DH == i[None, :] // DH),
        bdiag16=(i[:, None] // DH == np.arange(H)[None, :]), heads4=((i[:, None] // DH) % 4 == np.arange(4)[None, :]),
        heads4s=((i[:, None] // DH) % 4 == np.arange(4)[None, :]) * SCALE8, cos=cos, sin=sin, window=np.where(np.abs(i[:, None] - i[None, :]) <= WINDOW, 0.0, -1e9),
        quarters=(i[:, None] // 32 == np.arange(4)[None, :]), rank=np.broadcast_to(8.0 - np.arange(8), (128, 8)), part=i[:, None],
        drop=-1.0 * (i[:, None] > np.arange(2)[None, :]))
    return np.concatenate([np.asarray(parts[n], np.float32) for n, _ in CONSTS], axis=1)


def lay_out(v):
    wp = {
        "L0a_w1": v["L0_attn_W1"], "L0a_w2": block_cols(v["L0_attn_W2"], 4),
        "L0x_wq": v["L0_xattn_Wq"].T, "L0x_wk": v["L0_xattn_Wk"].T, "L0x_wv": v["L0_xattn_Wv"].T,
        "L0x_wo": v["L0_xattn_Wout"].T,
        "L0f_rw": v["L0_ffn_router_w"], "L0f_w1": v["L0_ffn_w1"].transpose(1, 0, 2).reshape(D, -1),
        "L0f_w2": block_cols(v["L0_ffn_w2"].reshape(E0 * F0, D), E0 * 4),
        "L1a_wqr": v["L1_attn_Wq"][:, ROT], "L1a_wkr": v["L1_attn_Wk"][:, ROT],
        "L1a_wq": v["L1_attn_Wq"], "L1a_wk": v["L1_attn_Wk"], "L1a_wv": v["L1_attn_Wv"], "L1a_wo": v["L1_attn_Wo"],
        "L1x_wq": v["L1_xattn_Wq"], "L1x_wk": v["L1_xattn_Wk"], "L1x_wv": v["L1_xattn_Wv"],
        "L1x_wo": v["L1_xattn_Wo"],
        "L1f_la": pad_rows(v["L1_ffn_lora_a"].transpose(1, 0, 2).reshape(32, -1)),
        "L1f_lb": pad_rows(v["L1_ffn_lora_b"].transpose(2, 0, 1).reshape(32, -1)),
        "L2a_wq": v["L2_attn_Wq"], "L2a_wk": v["L2_attn_Wk"], "L2a_wv": v["L2_attn_Wv"], "L2a_wo": v["L2_attn_Wo"],
        "L2x_wq": v["L2_xattn_w_q"], "L2x_wkv": v["L2_xattn_w_kv"], "L2x_wo": block_cols(v["L2_xattn_w_out"], 8),
        "L2f_u1": v["L2_ffn_U1"], "L2f_v1": pad_rows(v["L2_ffn_V1"]), "L2f_u2": block_cols(v["L2_ffn_U2"], 4),
        "L2f_v2": pad_rows(v["L2_ffn_V2"]),
        "L3a_wqkv": v["L3_attn_w_qkv"].T, "L3a_wo": v["L3_attn_w_out"].T,
        "L3x_wq": v["L3_xattn_Wq"].T, "L3x_wk": v["L3_xattn_Wk"].T, "L3x_wv": v["L3_xattn_Wv"].T,
        "L3x_wo": v["L3_xattn_Wo"].T,
        "L3f_wg": v["L3_ffn_wg"].T, "L3f_w1": v["L3_ffn_w1"].reshape(-1, D).T,
        "L3f_w3": v["L3_ffn_w3"].reshape(-1, D).T,
        "L3f_w2": block_cols(v["L3_ffn_w2"].transpose(0, 2, 1).reshape(E3 * F3, D), E3 * 2),
    }
    cp = {
        "L0a_g1": v["L0_attn_ln1_g"], "L0a_b1": v["L0_attn_ln1_b"], "L0a_fb": v["L0_attn_b1"],
        "L0x_bq": v["L0_xattn_bq"], "L0x_bk": v["L0_xattn_bk"], "L0x_bv": v["L0_xattn_bv"],
        "L0f_b1": v["L0_ffn_b1"], "L1a_bq": v["L1_attn_bq"], "L1a_bk": v["L1_attn_bk"], "L1a_bv": v["L1_attn_bv"],
        "L1a_bqr": v["L1_attn_bq"][ROT], "L1a_bkr": v["L1_attn_bk"][ROT],
        "L1x_bq": v["L1_xattn_bq"], "L1x_bk": v["L1_xattn_bk"], "L1x_bv": v["L1_xattn_bv"],
        "L1f_g": v["L1_ffn_ln_gamma"], "L1f_b": v["L1_ffn_ln_beta"],
        "L2a_bq": v["L2_attn_bq"], "L2a_bk": v["L2_attn_bk"], "L2a_bv": v["L2_attn_bv"],
        "L2x_g": v["L2_xattn_ln_gamma"], "L2x_b": v["L2_xattn_ln_beta"], "L2f_b1": v["L2_ffn_b1"],
        "L3x_bq": v["L3_xattn_bq"], "L3x_bv": v["L3_xattn_bv"],
    }
    rp = {
        "L0a_b2": v["L0_attn_b2"], "L0x_bo": v["L0_xattn_bout"], "L0f_rb": v["L0_ffn_router_b"],
        "L1a_bo": v["L1_attn_bo"], "L1x_bo": v["L1_xattn_bo"],
        "L1f_bias": v["L1_ffn_biases"], "L2a_bo": v["L2_attn_bo"], "L2x_bo": v["L2_xattn_b_out"],
        "L2f_b2": v["L2_ffn_b2"], "L3x_bo": v["L3_xattn_bo"],
    }
    return dict(
        x=v["x"].transpose(1, 0, 2).reshape(S, NB * D),
        ctxT=v["ctx_1024"].transpose(2, 0, 1).reshape(D, NB * SC),
        consts=shape_constants(),
        cols=np.concatenate([cp[n].reshape(-1, 128).T for n, _ in COLS[:-1]] + [pad_rows(v["L0_ffn_b2"])], axis=1),
        rows3=np.repeat(np.concatenate([rp[n].reshape(1, -1) for n, _ in ROWS], axis=1), 3, axis=0),
        w=np.concatenate([wp[n] for _, ps in WIDTHS for n, _ in ps], axis=1),
        amask=v["mask_SxS2_ff0"], pad=np.ascontiguousarray(v["mask_BxS2_bf0"]).reshape(-1).view(np.int32),
        ln2_g=v["L0_attn_ln2_g"], ln2_b=v["L0_attn_ln2_b"], gate=v["L2_xattn_gate"],
        idx=v["L2_attn_sample_idx"],
        qw=v["L1_ffn_qweights"].transpose(2, 0, 1).reshape(D, -1),
        scl=np.repeat(v["L1_ffn_scales"].transpose(2, 0, 1), 16, axis=0).reshape(D, -1),
    )


def kernel(**inputs):
    import concourse.bacc as _bacc
    from concourse.bass_utils import run_bass_kernel_spmd as _run

    arrays = {n: np.ascontiguousarray(a) for n, a in lay_out({k: np.asarray(a) for k, a in inputs.items()}).items()}
    nc = _bacc.Bacc("TRN2", target_bir_lowering=False, num_devices=1)
    io = {n: nc.dram_tensor("in_" + n, a.shape, mybir.dt.from_np(a.dtype), kind="ExternalInput").ap()
          for n, a in arrays.items()}
    io["out"] = nc.dram_tensor("out", (S, NB * D), F32, kind="ExternalOutput").ap()
    build(nc, io)
    r = _run(nc, [{"in_" + n: a for n, a in arrays.items()}], core_ids=[0])
    got = r.results[0]["out"]
    return np.ascontiguousarray(got.reshape(S, NB, D).transpose(1, 0, 2))
```
